# Optimizing a Trainium2 kernel written in Bass

```python
import numpy as np
import jax
import jax.numpy as jnp

def _softmax(x, axis=-1):
    return jax.nn.softmax(x, axis=axis)

def _gelu(x):
    return jax.nn.gelu(x, approximate=True)

def _silu(x):
    return jax.nn.silu(x)

def _sigmoid(x):
    return jax.nn.sigmoid(x)

def _layernorm(x, axis=-1, eps=1e-05):
    m = jnp.mean(x, axis=axis, keepdims=True)
    v = jnp.var(x, axis=axis, keepdims=True)
    return (x - m) / jnp.sqrt(v + eps)

def _scatter_add(tgt, idx, src, axis=0):
    return tgt.at[idx].add(src)

def _segment_sum(src, seg, n):
    return jax.ops.segment_sum(src, seg, n)
kernel_name = 'mk_pixart_seq_d4_seqx_r8_d5d2cf'

def setup_inputs(seed: int=0):
    np.random.seed(seed)
    _w = jnp.asarray

    def _rec_inputs():
        import jax
        import jax.numpy as jnp
        _rk = jax.random.key(seed)
        x = -0.0002928 + 1 * jax.random.normal(jax.random.fold_in(_rk, 1), (2, 512, 128), jnp.float32)
        _lenS = 512 - jax.random.randint(jax.random.fold_in(_rk, 7), (2,), 0, max(1, 512 // 4) + 1, jnp.int32)
        _lenS2 = 77 - jax.random.randint(jax.random.fold_in(_rk, 8), (2,), 0, max(1, 77 // 4) + 1, jnp.int32)
        cond_1024 = 0.0061147 + 1.02565 * jax.random.normal(jax.random.fold_in(_rk, 11), (2, 128), jnp.float32)
        _ctx_1024P = jax.random.normal(jax.random.fold_in(_rk, 12), (2, 16, 128), jnp.float32)
        _ctx_1024c = jax.random.dirichlet(jax.random.fold_in(_rk, 512), 0.3 * jnp.ones((16,), jnp.float32), (2, 77))
        _ctx_1024t = jnp.einsum('bsk,bkd->bsd', _ctx_1024c, _ctx_1024P)
        _ctx_1024t = _ctx_1024t * jax.lax.rsqrt(jnp.mean(jnp.square(_ctx_1024t)) + 1e-12) * 0.953939
        ctx_1024 = -0.00265004 + 0.998804 * (_ctx_1024t + 0.3 * jax.random.normal(jax.random.fold_in(_rk, 612), (2, 77, 128), jnp.float32))
        _validS = jnp.arange(512)[None, :] < _lenS[:, None]
        _validS2 = jnp.arange(77)[None, :] < _lenS2[:, None]
        _causal = jnp.tril(jnp.ones((512, 512), dtype=bool))
        mask_BxS2_bf1 = jnp.ones((2, 77), dtype=bool)
        mask_SxS_bk0 = jnp.logical_not(jnp.broadcast_to(_validS[0:1, :], (512, 512)))
        return (x, cond_1024, ctx_1024, mask_BxS2_bf1, mask_SxS_bk0)
    x, cond_1024, ctx_1024, mask_BxS2_bf1, mask_SxS_bk0 = _rec_inputs()

    def _L0_xcond_setup():
        import jax, jax.numpy as jnp
        import numpy as np
        LN_EPS = 1e-06

        def _ln(x):
            mu = jnp.mean(x, axis=-1, keepdims=True)
            var = jnp.var(x, axis=-1, keepdims=True)
            return (x - mu) * jax.lax.rsqrt(var + LN_EPS)
        key = jax.random.key(seed)
        H, NH = (128, 16)
        B, N, S = (4, 128, 77)
        MLP = int(H * 4.0)
        ks = jax.random.split(key, 20)
        s = 1.0 / np.sqrt(H)
        return {'x': jax.random.normal(ks[0], (B, N, H), jnp.float32), 'c': jax.random.normal(ks[1], (B, H), jnp.float32), 'context': jax.random.normal(ks[2], (B, S, H), jnp.float32), 'W_mod': jax.random.normal(ks[3], (H, 6 * H), jnp.float32) * s, 'b_mod': jnp.zeros((6 * H,), jnp.float32), 'W_qkv': jax.random.normal(ks[4], (H, 3 * H), jnp.float32) * s, 'b_qkv': jnp.zeros((3 * H,), jnp.float32), 'W_proj': jax.random.normal(ks[5], (H, H), jnp.float32) * s, 'b_proj': jnp.zeros((H,), jnp.float32), 'W_qc': jax.random.normal(ks[6], (H, H), jnp.float32) * s, 'b_qc': jnp.zeros((H,), jnp.float32), 'W_kvc': jax.random.normal(ks[7], (H, 2 * H), jnp.float32) * s, 'b_kvc': jnp.zeros((2 * H,), jnp.float32), 'W_cproj': jax.random.normal(ks[8], (H, H), jnp.float32) * s, 'b_cproj': jnp.zeros((H,), jnp.float32), 'W_mlp1': jax.random.normal(ks[9], (H, MLP), jnp.float32) * s, 'b_mlp1': jnp.zeros((MLP,), jnp.float32), 'W_mlp2': jax.random.normal(ks[10], (MLP, H), jnp.float32) * (1.0 / np.sqrt(MLP)), 'b_mlp2': jnp.zeros((H,), jnp.float32)}
    _L0_xcond_all = _L0_xcond_setup()
    _L0_xcond_in = {k: v for k, v in _L0_xcond_all.items() if k in ('W_mod', 'b_mod', 'W_qkv', 'b_qkv', 'W_proj', 'b_proj', 'W_qc', 'b_qc', 'W_kvc', 'b_kvc', 'W_cproj', 'b_cproj', 'W_mlp1', 'b_mlp1', 'W_mlp2', 'b_mlp2')}
    del _L0_xcond_all

    def _L1_xcond_setup():
        import jax, jax.numpy as jnp
        import numpy as np
        C = 128
        H = 16
        D = C // H
        WIN = 64
        SHIFT = 32
        TOPK = 16
        HID = 512
        EPS = 1e-06

        def _ln(x):
            x32 = x.astype(jnp.float32)
            m = x32.mean(-1, keepdims=True)
            v = jnp.mean((x32 - m) ** 2, axis=-1, keepdims=True)
            return ((x32 - m) * jax.lax.rsqrt(v + EPS)).astype(x.dtype)

        def _self_attn(h, w_qkv, b_qkv, w_so, b_so):
            B, L, _ = h.shape
            qkv = h @ w_qkv + b_qkv
            qkv = jnp.roll(qkv, -SHIFT, axis=1)
            nw = L // WIN
            qkv = qkv.reshape(B, nw, WIN, 3, H, D)
            q, k, v = (qkv[:, :, :, 0], qkv[:, :, :, 1], qkv[:, :, :, 2])
            scores = jnp.einsum('bnqhd,bnkhd->bnhqk', q, k) / jnp.sqrt(jnp.float32(D)).astype(h.dtype)
            attn = jax.nn.softmax(scores, axis=-1)
            o = jnp.einsum('bnhqk,bnkhd->bnqhd', attn, v).reshape(B, L, C)
            o = jnp.roll(o, SHIFT, axis=1)
            return o @ w_so + b_so

        def _topk_cross_attn(h, ctx, w_q, b_q, w_kv, b_kv, w_co, b_co):
            B, L, _ = h.shape
            Lc = ctx.shape[1]
            q = (h @ w_q + b_q).reshape(B, L, H, D)
            kv = (ctx @ w_kv + b_kv).reshape(B, Lc, 2, H, D)
            k, v = (kv[:, :, 0], kv[:, :, 1])
            scores = jnp.einsum('bqhd,bkhd->bhqk', q, k) / jnp.sqrt(jnp.float32(D)).astype(h.dtype)
            top_s, top_i = jax.lax.top_k(scores, TOPK)
            attn = jax.nn.softmax(top_s, axis=-1)
            v_bh = jnp.transpose(v, (0, 2, 1, 3))
            vg = jnp.take_along_axis(v_bh[:, :, None, :, :], top_i[..., None], axis=3)
            o = jnp.einsum('bhqk,bhqkd->bqhd', attn, vg).reshape(B, L, C)
            return o @ w_co + b_co

        def _swiglu(h, w_m1, b_m1, w_m2, b_m2):
            u = h @ w_m1 + b_m1
            a, b = (u[..., :HID], u[..., HID:])
            return jax.nn.silu(a) * b @ w_m2 + b_m2
        key = jax.random.key(seed)
        ks = jax.random.split(key, 24)
        s = 0.02
        inp = {'x': jax.random.normal(ks[0], (2, 512, C), jnp.float32), 'mod': jax.random.normal(ks[1], (2, C), jnp.float32), 'context': jax.random.normal(ks[2], (2, 128, C), jnp.float32), 'w_ada': jax.random.normal(ks[3], (C, 9 * C), jnp.float32) * s, 'b_ada': jnp.zeros((9 * C,), jnp.float32), 'w_qkv': jax.random.normal(ks[4], (C, 3 * C), jnp.float32) * s, 'b_qkv': jnp.zeros((3 * C,), jnp.float32), 'w_so': jax.random.normal(ks[5], (C, C), jnp.float32) * s, 'b_so': jnp.zeros((C,), jnp.float32), 'w_q': jax.random.normal(ks[6], (C, C), jnp.float32) * s, 'b_q': jnp.zeros((C,), jnp.float32), 'w_kv': jax.random.normal(ks[7], (C, 2 * C), jnp.float32) * s, 'b_kv': jnp.zeros((2 * C,), jnp.float32), 'w_co': jax.random.normal(ks[8], (C, C), jnp.float32) * s, 'b_co': jnp.zeros((C,), jnp.float32), 'w_m1': jax.random.normal(ks[9], (C, 2 * HID), jnp.float32) * s, 'b_m1': jnp.zeros((2 * HID,), jnp.float32), 'w_m2': jax.random.normal(ks[10], (HID, C), jnp.float32) * s, 'b_m2': jnp.zeros((C,), jnp.float32)}
        return inp
    _L1_xcond_all = _L1_xcond_setup()
    _L1_xcond_in = {k: v for k, v in _L1_xcond_all.items() if k in ('w_ada', 'b_ada', 'w_qkv', 'b_qkv', 'w_so', 'b_so', 'w_q', 'b_q', 'w_kv', 'b_kv', 'w_co', 'b_co', 'w_m1', 'b_m1', 'w_m2', 'b_m2')}
    del _L1_xcond_all

    def _L2_xcond_setup():
        import jax, jax.numpy as jnp
        import numpy as np
        B, N, D, H, LC = (2, 128, 128, 16, 77)
        HD = D // H
        BLOCK = 16
        ROPE_BASE = 10000.0
        EPS = 1e-05

        def _block_diff_mask(n, block_size):
            idx = np.arange(2 * n)
            q = idx[:, None]
            kv = idx[None, :]
            fq = q >= n
            fkv = kv >= n
            bq = np.where(fq, (q - n) // block_size, q // block_size)
            bkv = np.where(fkv, (kv - n) // block_size, kv // block_size)
            block_diagonal = (bq == bkv) & (fq == fkv)
            offset_block_causal = (bq > bkv) & fkv & ~fq
            block_causal = (bq >= bkv) & fq & fkv
            return jnp.asarray(block_diagonal | offset_block_causal | block_causal)

        def _rope_tables(n):
            inv_freq = 1.0 / ROPE_BASE ** (np.arange(0, HD, 2, dtype=np.float32) / HD)
            freqs = np.outer(np.arange(n, dtype=np.float32), inv_freq)
            emb = np.concatenate([freqs, freqs], axis=-1)
            cos = jnp.asarray(np.cos(emb), jnp.float32)[None, :, None, :]
            sin = jnp.asarray(np.sin(emb), jnp.float32)[None, :, None, :]
            return (cos, sin)

        def _ln(x, w):
            xf = x.astype(jnp.float32)
            mu = jnp.mean(xf, axis=-1, keepdims=True)
            var = jnp.mean(jnp.square(xf - mu), axis=-1, keepdims=True)
            y = (xf - mu) * jax.lax.rsqrt(var + EPS)
            return y * w[None, None, :]

        def _apply_rope(t, cos, sin):
            t1, t2 = jnp.split(t, 2, axis=-1)
            rot = jnp.concatenate([-t2, t1], axis=-1)
            return t * cos + rot * sin

        def _attn(q, k, v, mask):
            scale = 1.0 / np.sqrt(HD)
            s = jnp.einsum('bqhd,bkhd->bhqk', q, k) * scale
            s = jnp.where(mask, s, jnp.finfo(s.dtype).min)
            a = jax.nn.softmax(s, axis=-1)
            return jnp.einsum('bhqk,bkhd->bqhd', a, v)
        key = jax.random.key(seed)
        ks = jax.random.split(key, 16)
        w = lambda k, shp: jax.random.normal(k, shp, jnp.float32) * 0.02
        inp = {'x': jax.random.normal(ks[0], (B, 2 * N, D), jnp.float32), 'cond_global': jax.random.normal(ks[1], (B, D), jnp.float32), 'cond_tokens': jax.random.normal(ks[2], (B, LC, D), jnp.float32), 'adaLN_W': w(ks[3], (D, 9 * D)), 'adaLN_b': w(ks[4], (9 * D,)), 'norm1_w': jnp.ones((D,), jnp.float32), 'qkv_W': w(ks[5], (D, 3 * D)), 'attn_out_W': w(ks[6], (D, D)), 'normc_w': jnp.ones((D,), jnp.float32), 'cq_W': w(ks[7], (D, D)), 'ck_W': w(ks[8], (D, D)), 'cv_W': w(ks[9], (D, D)), 'co_W': w(ks[10], (D, D)), 'norm2_w': jnp.ones((D,), jnp.float32), 'mlp_W1': w(ks[11], (D, 4 * D)), 'mlp_b1': w(ks[12], (4 * D,)), 'mlp_W2': w(ks[13], (4 * D, D)), 'mlp_b2': w(ks[14], (D,)), 'cond_kv_mask': jnp.ones((B, LC), bool), 'attn_mask': _block_diff_mask(N, BLOCK)}
        return inp
    _L2_xcond_all = _L2_xcond_setup()
    _L2_xcond_in = {k: v for k, v in _L2_xcond_all.items() if k in ('adaLN_W', 'adaLN_b', 'norm1_w', 'qkv_W', 'attn_out_W', 'normc_w', 'cq_W', 'ck_W', 'cv_W', 'co_W', 'norm2_w', 'mlp_W1', 'mlp_b1', 'mlp_W2', 'mlp_b2')}
    del _L2_xcond_all

    def _L3_xcond_setup():
        import jax, jax.numpy as jnp
        import numpy as np
        EPS = 1e-05

        def _ada_ln(x, c, W_ss, b_ss):
            mu = jnp.mean(x, axis=-1, keepdims=True)
            var = jnp.mean((x - mu) ** 2, axis=-1, keepdims=True)
            h = (x - mu) / jnp.sqrt(var + EPS)
            ss = jax.nn.silu(c) @ W_ss + b_ss
            scale, bias = jnp.split(ss, 2, axis=-1)
            return (1.0 + scale)[:, None, :] * h + bias[:, None, :]
        key = jax.random.key(seed)
        ks = jax.random.split(key, 12)
        B, Lq, Lkv, H = (8, 256, 64, 128)
        s = 0.02
        return {'x_q': jax.random.normal(ks[0], (B, Lq, H), jnp.float32), 'x_kv': jax.random.normal(ks[1], (B, Lkv, H), jnp.float32), 't_vec': jax.random.normal(ks[2], (B, H), jnp.float32), 'Wq': jax.random.normal(ks[3], (H, H), jnp.float32) * s, 'bq': jnp.zeros((H,), jnp.float32), 'Wkv': jax.random.normal(ks[4], (H, 2 * H), jnp.float32) * s, 'bkv': jnp.zeros((2 * H,), jnp.float32), 'Wp': jax.random.normal(ks[5], (H, H), jnp.float32) * s, 'bp': jnp.zeros((H,), jnp.float32), 'Wss_q': jax.random.normal(ks[6], (H, 2 * H), jnp.float32) * s, 'bss_q': jnp.zeros((2 * H,), jnp.float32), 'Wss_kv': jax.random.normal(ks[7], (H, 2 * H), jnp.float32) * s, 'bss_kv': jnp.zeros((2 * H,), jnp.float32)}
    _L3_xcond_all = _L3_xcond_setup()
    _L3_xcond_in = {k: v for k, v in _L3_xcond_all.items() if k in ('Wq', 'bq', 'Wkv', 'bkv', 'Wp', 'bp', 'Wss_q', 'bss_q', 'Wss_kv', 'bss_kv')}
    del _L3_xcond_all
    return {'x': x, 'cond_1024': cond_1024, 'ctx_1024': ctx_1024, 'mask_BxS2_bf1': mask_BxS2_bf1, 'mask_SxS_bk0': mask_SxS_bk0, 'L0_xcond_W_mod': _L0_xcond_in['W_mod'], 'L0_xcond_b_mod': _L0_xcond_in['b_mod'], 'L0_xcond_W_qkv': _L0_xcond_in['W_qkv'], 'L0_xcond_b_qkv': _L0_xcond_in['b_qkv'], 'L0_xcond_W_proj': _L0_xcond_in['W_proj'], 'L0_xcond_b_proj': _L0_xcond_in['b_proj'], 'L0_xcond_W_qc': _L0_xcond_in['W_qc'], 'L0_xcond_b_qc': _L0_xcond_in['b_qc'], 'L0_xcond_W_kvc': _L0_xcond_in['W_kvc'], 'L0_xcond_b_kvc': _L0_xcond_in['b_kvc'], 'L0_xcond_W_cproj': _L0_xcond_in['W_cproj'], 'L0_xcond_b_cproj': _L0_xcond_in['b_cproj'], 'L0_xcond_W_mlp1': _L0_xcond_in['W_mlp1'], 'L0_xcond_b_mlp1': _L0_xcond_in['b_mlp1'], 'L0_xcond_W_mlp2': _L0_xcond_in['W_mlp2'], 'L0_xcond_b_mlp2': _L0_xcond_in['b_mlp2'], 'L1_xcond_w_ada': _L1_xcond_in['w_ada'], 'L1_xcond_b_ada': _L1_xcond_in['b_ada'], 'L1_xcond_w_qkv': _L1_xcond_in['w_qkv'], 'L1_xcond_b_qkv': _L1_xcond_in['b_qkv'], 'L1_xcond_w_so': _L1_xcond_in['w_so'], 'L1_xcond_b_so': _L1_xcond_in['b_so'], 'L1_xcond_w_q': _L1_xcond_in['w_q'], 'L1_xcond_b_q': _L1_xcond_in['b_q'], 'L1_xcond_w_kv': _L1_xcond_in['w_kv'], 'L1_xcond_b_kv': _L1_xcond_in['b_kv'], 'L1_xcond_w_co': _L1_xcond_in['w_co'], 'L1_xcond_b_co': _L1_xcond_in['b_co'], 'L1_xcond_w_m1': _L1_xcond_in['w_m1'], 'L1_xcond_b_m1': _L1_xcond_in['b_m1'], 'L1_xcond_w_m2': _L1_xcond_in['w_m2'], 'L1_xcond_b_m2': _L1_xcond_in['b_m2'], 'L2_xcond_adaLN_W': _L2_xcond_in['adaLN_W'], 'L2_xcond_adaLN_b': _L2_xcond_in['adaLN_b'], 'L2_xcond_norm1_w': _L2_xcond_in['norm1_w'], 'L2_xcond_qkv_W': _L2_xcond_in['qkv_W'], 'L2_xcond_attn_out_W': _L2_xcond_in['attn_out_W'], 'L2_xcond_normc_w': _L2_xcond_in['normc_w'], 'L2_xcond_cq_W': _L2_xcond_in['cq_W'], 'L2_xcond_ck_W': _L2_xcond_in['ck_W'], 'L2_xcond_cv_W': _L2_xcond_in['cv_W'], 'L2_xcond_co_W': _L2_xcond_in['co_W'], 'L2_xcond_norm2_w': _L2_xcond_in['norm2_w'], 'L2_xcond_mlp_W1': _L2_xcond_in['mlp_W1'], 'L2_xcond_mlp_b1': _L2_xcond_in['mlp_b1'], 'L2_xcond_mlp_W2': _L2_xcond_in['mlp_W2'], 'L2_xcond_mlp_b2': _L2_xcond_in['mlp_b2'], 'L3_xcond_Wq': _L3_xcond_in['Wq'], 'L3_xcond_bq': _L3_xcond_in['bq'], 'L3_xcond_Wkv': _L3_xcond_in['Wkv'], 'L3_xcond_bkv': _L3_xcond_in['bkv'], 'L3_xcond_Wp': _L3_xcond_in['Wp'], 'L3_xcond_bp': _L3_xcond_in['bp'], 'L3_xcond_Wss_q': _L3_xcond_in['Wss_q'], 'L3_xcond_bss_q': _L3_xcond_in['bss_q'], 'L3_xcond_Wss_kv': _L3_xcond_in['Wss_kv'], 'L3_xcond_bss_kv': _L3_xcond_in['bss_kv']}

def reference(x, cond_1024, ctx_1024, mask_BxS2_bf1, mask_SxS_bk0, L0_xcond_W_mod, L0_xcond_b_mod, L0_xcond_W_qkv, L0_xcond_b_qkv, L0_xcond_W_proj, L0_xcond_b_proj, L0_xcond_W_qc, L0_xcond_b_qc, L0_xcond_W_kvc, L0_xcond_b_kvc, L0_xcond_W_cproj, L0_xcond_b_cproj, L0_xcond_W_mlp1, L0_xcond_b_mlp1, L0_xcond_W_mlp2, L0_xcond_b_mlp2, L1_xcond_w_ada, L1_xcond_b_ada, L1_xcond_w_qkv, L1_xcond_b_qkv, L1_xcond_w_so, L1_xcond_b_so, L1_xcond_w_q, L1_xcond_b_q, L1_xcond_w_kv, L1_xcond_b_kv, L1_xcond_w_co, L1_xcond_b_co, L1_xcond_w_m1, L1_xcond_b_m1, L1_xcond_w_m2, L1_xcond_b_m2, L2_xcond_adaLN_W, L2_xcond_adaLN_b, L2_xcond_norm1_w, L2_xcond_qkv_W, L2_xcond_attn_out_W, L2_xcond_normc_w, L2_xcond_cq_W, L2_xcond_ck_W, L2_xcond_cv_W, L2_xcond_co_W, L2_xcond_norm2_w, L2_xcond_mlp_W1, L2_xcond_mlp_b1, L2_xcond_mlp_W2, L2_xcond_mlp_b2, L3_xcond_Wq, L3_xcond_bq, L3_xcond_Wkv, L3_xcond_bkv, L3_xcond_Wp, L3_xcond_bp, L3_xcond_Wss_q, L3_xcond_bss_q, L3_xcond_Wss_kv, L3_xcond_bss_kv):
    import jax
    import jax.numpy as jnp

    def _L0_xcond_ref(x, c, context, W_mod, b_mod, W_qkv, b_qkv, W_proj, b_proj, W_qc, b_qc, W_kvc, b_kvc, W_cproj, b_cproj, W_mlp1, b_mlp1, W_mlp2, b_mlp2):
        import jax, jax.numpy as jnp
        import numpy as np
        LN_EPS = 1e-06

        def _ln(x):
            mu = jnp.mean(x, axis=-1, keepdims=True)
            var = jnp.var(x, axis=-1, keepdims=True)
            return (x - mu) * jax.lax.rsqrt(var + LN_EPS)
        B, N, H = x.shape
        NH = 16
        hd = H // NH
        scale = hd ** (-0.5)
        c_proj = jax.nn.silu(c) @ W_mod + b_mod
        shift_a, scale_a, gate_a, shift_m, scale_m, gate_m = jnp.split(c_proj, 6, axis=-1)

        def modulate(t, shift, sc):
            return t * (1 + sc[:, None]) + shift[:, None]
        x_norm = modulate(_ln(x), shift_a, scale_a)
        qkv = x_norm @ W_qkv + b_qkv
        q, k, v = jnp.split(qkv, 3, axis=-1)
        q = q.reshape(B, N, NH, hd).transpose(0, 2, 1, 3)
        k = k.reshape(B, N, NH, hd).transpose(0, 2, 1, 3)
        v = v.reshape(B, N, NH, hd).transpose(0, 2, 1, 3)
        attn_w = jax.nn.softmax(jnp.einsum('bhqd,bhkd->bhqk', q, k) * scale, axis=-1)
        attn_out = jnp.einsum('bhqk,bhkd->bhqd', attn_w, v)
        attn_out = attn_out.transpose(0, 2, 1, 3).reshape(B, N, H)
        attn_out = attn_out @ W_proj + b_proj
        x = x + gate_a[:, None] * attn_out
        S = context.shape[1]
        q_c = _ln(x) @ W_qc + b_qc
        kv_c = _ln(context) @ W_kvc + b_kvc
        k_c, v_c = jnp.split(kv_c, 2, axis=-1)
        q_c = q_c.reshape(B, N, NH, hd).transpose(0, 2, 1, 3)
        k_c = k_c.reshape(B, S, NH, hd).transpose(0, 2, 1, 3)
        v_c = v_c.reshape(B, S, NH, hd).transpose(0, 2, 1, 3)
        c_attn_w = jax.nn.softmax(jnp.einsum('bhqd,bhsd->bhqs', q_c, k_c) * scale, axis=-1)
        c_attn_out = jnp.einsum('bhqs,bhsd->bhqd', c_attn_w, v_c)
        c_attn_out = c_attn_out.transpose(0, 2, 1, 3).reshape(B, N, H)
        c_attn_out = c_attn_out @ W_cproj + b_cproj
        x = x + c_attn_out
        x_norm2 = modulate(_ln(x), shift_m, scale_m)
        h = jax.nn.gelu(x_norm2 @ W_mlp1 + b_mlp1)
        h = h @ W_mlp2 + b_mlp2
        x = x + gate_m[:, None] * h
        return x

    def _L1_xcond_ref(x, mod, context, w_ada, b_ada, w_qkv, b_qkv, w_so, b_so, w_q, b_q, w_kv, b_kv, w_co, b_co, w_m1, b_m1, w_m2, b_m2):
        import jax, jax.numpy as jnp
        import numpy as np
        C = 128
        H = 16
        D = C // H
        WIN = 64
        SHIFT = 32
        TOPK = 16
        HID = 512
        EPS = 1e-06

        def _ln(x):
            x32 = x.astype(jnp.float32)
            m = x32.mean(-1, keepdims=True)
            v = jnp.mean((x32 - m) ** 2, axis=-1, keepdims=True)
            return ((x32 - m) * jax.lax.rsqrt(v + EPS)).astype(x.dtype)

        def _self_attn(h, w_qkv, b_qkv, w_so, b_so):
            B, L, _ = h.shape
            qkv = h @ w_qkv + b_qkv
            qkv = jnp.roll(qkv, -SHIFT, axis=1)
            nw = L // WIN
            qkv = qkv.reshape(B, nw, WIN, 3, H, D)
            q, k, v = (qkv[:, :, :, 0], qkv[:, :, :, 1], qkv[:, :, :, 2])
            scores = jnp.einsum('bnqhd,bnkhd->bnhqk', q, k) / jnp.sqrt(jnp.float32(D)).astype(h.dtype)
            attn = jax.nn.softmax(scores, axis=-1)
            o = jnp.einsum('bnhqk,bnkhd->bnqhd', attn, v).reshape(B, L, C)
            o = jnp.roll(o, SHIFT, axis=1)
            return o @ w_so + b_so

        def _topk_cross_attn(h, ctx, w_q, b_q, w_kv, b_kv, w_co, b_co):
            B, L, _ = h.shape
            Lc = ctx.shape[1]
            q = (h @ w_q + b_q).reshape(B, L, H, D)
            kv = (ctx @ w_kv + b_kv).reshape(B, Lc, 2, H, D)
            k, v = (kv[:, :, 0], kv[:, :, 1])
            scores = jnp.einsum('bqhd,bkhd->bhqk', q, k) / jnp.sqrt(jnp.float32(D)).astype(h.dtype)
            top_s, top_i = jax.lax.top_k(scores, TOPK)
            attn = jax.nn.softmax(top_s, axis=-1)
            v_bh = jnp.transpose(v, (0, 2, 1, 3))
            vg = jnp.take_along_axis(v_bh[:, :, None, :, :], top_i[..., None], axis=3)
            o = jnp.einsum('bhqk,bhqkd->bqhd', attn, vg).reshape(B, L, C)
            return o @ w_co + b_co

        def _swiglu(h, w_m1, b_m1, w_m2, b_m2):
            u = h @ w_m1 + b_m1
            a, b = (u[..., :HID], u[..., HID:])
            return jax.nn.silu(a) * b @ w_m2 + b_m2
        m = jax.nn.silu(mod) @ w_ada + b_ada
        sh_msa, sc_msa, g_msa, sh_mca, sc_mca, g_mca, sh_mlp, sc_mlp, g_mlp = [m[:, i * C:(i + 1) * C][:, None, :] for i in range(9)]
        h = _ln(x) * (1 + sc_msa) + sh_msa
        h = _self_attn(h, w_qkv, b_qkv, w_so, b_so)
        x = x + h * g_msa
        h = _ln(x) * (1 + sc_mca) + sh_mca
        h = _topk_cross_attn(h, context, w_q, b_q, w_kv, b_kv, w_co, b_co)
        x = x + h * g_mca
        h = _ln(x) * (1 + sc_mlp) + sh_mlp
        h = _swiglu(h, w_m1, b_m1, w_m2, b_m2)
        x = x + h * g_mlp
        return x

    def _L2_xcond_ref(x, cond_global, cond_tokens, adaLN_W, adaLN_b, norm1_w, qkv_W, attn_out_W, normc_w, cq_W, ck_W, cv_W, co_W, norm2_w, mlp_W1, mlp_b1, mlp_W2, mlp_b2, cond_kv_mask, attn_mask):
        import jax, jax.numpy as jnp
        import numpy as np
        B, N, D, H, LC = (2, 128, 128, 16, 77)
        HD = D // H
        BLOCK = 16
        ROPE_BASE = 10000.0
        EPS = 1e-05

        def _block_diff_mask(n, block_size):
            idx = np.arange(2 * n)
            q = idx[:, None]
            kv = idx[None, :]
            fq = q >= n
            fkv = kv >= n
            bq = np.where(fq, (q - n) // block_size, q // block_size)
            bkv = np.where(fkv, (kv - n) // block_size, kv // block_size)
            block_diagonal = (bq == bkv) & (fq == fkv)
            offset_block_causal = (bq > bkv) & fkv & ~fq
            block_causal = (bq >= bkv) & fq & fkv
            return jnp.asarray(block_diagonal | offset_block_causal | block_causal)

        def _rope_tables(n):
            inv_freq = 1.0 / ROPE_BASE ** (np.arange(0, HD, 2, dtype=np.float32) / HD)
            freqs = np.outer(np.arange(n, dtype=np.float32), inv_freq)
            emb = np.concatenate([freqs, freqs], axis=-1)
            cos = jnp.asarray(np.cos(emb), jnp.float32)[None, :, None, :]
            sin = jnp.asarray(np.sin(emb), jnp.float32)[None, :, None, :]
            return (cos, sin)

        def _ln(x, w):
            xf = x.astype(jnp.float32)
            mu = jnp.mean(xf, axis=-1, keepdims=True)
            var = jnp.mean(jnp.square(xf - mu), axis=-1, keepdims=True)
            y = (xf - mu) * jax.lax.rsqrt(var + EPS)
            return y * w[None, None, :]

        def _apply_rope(t, cos, sin):
            t1, t2 = jnp.split(t, 2, axis=-1)
            rot = jnp.concatenate([-t2, t1], axis=-1)
            return t * cos + rot * sin

        def _attn(q, k, v, mask):
            scale = 1.0 / np.sqrt(HD)
            s = jnp.einsum('bqhd,bkhd->bhqk', q, k) * scale
            s = jnp.where(mask, s, jnp.finfo(s.dtype).min)
            a = jax.nn.softmax(s, axis=-1)
            return jnp.einsum('bhqk,bkhd->bqhd', a, v)
        b, s, d = x.shape
        n = s // 2
        mod = (cond_global @ adaLN_W + adaLN_b)[:, None, :]
        sh_msa, sc_msa, g_msa, sh_x, sc_x, g_x, sh_mlp, sc_mlp, g_mlp = jnp.split(mod, 9, axis=-1)
        x_norm = _ln(x, norm1_w) * (1 + sc_msa) + sh_msa
        cos, sin = _rope_tables(n)

        def qkv(h):
            t = (h @ qkv_W).reshape(b, n, 3, H, HD)
            q, k, v = (t[:, :, 0], t[:, :, 1], t[:, :, 2])
            return (_apply_rope(q, cos, sin), _apply_rope(k, cos, sin), v)
        q1, k1, v1 = qkv(x_norm[:, :n])
        q2, k2, v2 = qkv(x_norm[:, n:])
        q = jnp.concatenate([q1, q2], axis=1)
        k = jnp.concatenate([k1, k2], axis=1)
        v = jnp.concatenate([v1, v2], axis=1)
        self_out = _attn(q, k, v, attn_mask[None, None]).reshape(b, s, d) @ attn_out_W
        x = x + g_msa * self_out
        xc = _ln(x, normc_w) * (1 + sc_x) + sh_x
        qc = (xc @ cq_W).reshape(b, s, H, HD)
        kc = (cond_tokens @ ck_W).reshape(b, LC, H, HD)
        vc = (cond_tokens @ cv_W).reshape(b, LC, H, HD)
        cross = _attn(qc, kc, vc, cond_kv_mask[:, None, None, :]).reshape(b, s, d) @ co_W
        x = x + g_x * cross
        xm = _ln(x, norm2_w) * (1 + sc_mlp) + sh_mlp
        h = jax.nn.gelu(xm @ mlp_W1 + mlp_b1, approximate=True)
        mlp_out = h @ mlp_W2 + mlp_b2
        return x + g_mlp * mlp_out

    def _L3_xcond_ref(x_q, x_kv, t_vec, Wq, bq, Wkv, bkv, Wp, bp, Wss_q, bss_q, Wss_kv, bss_kv):
        import jax, jax.numpy as jnp
        import numpy as np
        EPS = 1e-05

        def _ada_ln(x, c, W_ss, b_ss):
            mu = jnp.mean(x, axis=-1, keepdims=True)
            var = jnp.mean((x - mu) ** 2, axis=-1, keepdims=True)
            h = (x - mu) / jnp.sqrt(var + EPS)
            ss = jax.nn.silu(c) @ W_ss + b_ss
            scale, bias = jnp.split(ss, 2, axis=-1)
            return (1.0 + scale)[:, None, :] * h + bias[:, None, :]
        B, Lq, H = x_q.shape
        Lkv = x_kv.shape[1]
        nh = 16
        dh = H // nh
        xq = _ada_ln(x_q, t_vec, Wss_q, bss_q)
        xkv = _ada_ln(x_kv, t_vec, Wss_kv, bss_kv)
        q = (xq @ Wq + bq).reshape(B, Lq, nh, dh)
        kv = (xkv @ Wkv + bkv).reshape(B, Lkv, 2, nh, dh)
        k = kv[:, :, 0]
        v = kv[:, :, 1]
        scores = jnp.einsum('bqhd,bkhd->bhqk', q, k) / jnp.sqrt(jnp.float32(dh))
        attn = jax.nn.softmax(scores, axis=-1)
        out = jnp.einsum('bhqk,bkhd->bqhd', attn, v).reshape(B, Lq, H)
        return x_q + (out @ Wp + bp)
    x = _L0_xcond_ref(x, cond_1024, ctx_1024, L0_xcond_W_mod, L0_xcond_b_mod, L0_xcond_W_qkv, L0_xcond_b_qkv, L0_xcond_W_proj, L0_xcond_b_proj, L0_xcond_W_qc, L0_xcond_b_qc, L0_xcond_W_kvc, L0_xcond_b_kvc, L0_xcond_W_cproj, L0_xcond_b_cproj, L0_xcond_W_mlp1, L0_xcond_b_mlp1, L0_xcond_W_mlp2, L0_xcond_b_mlp2)
    x = _L1_xcond_ref(x, cond_1024, ctx_1024, L1_xcond_w_ada, L1_xcond_b_ada, L1_xcond_w_qkv, L1_xcond_b_qkv, L1_xcond_w_so, L1_xcond_b_so, L1_xcond_w_q, L1_xcond_b_q, L1_xcond_w_kv, L1_xcond_b_kv, L1_xcond_w_co, L1_xcond_b_co, L1_xcond_w_m1, L1_xcond_b_m1, L1_xcond_w_m2, L1_xcond_b_m2)
    x = _L2_xcond_ref(x, cond_1024, ctx_1024, L2_xcond_adaLN_W, L2_xcond_adaLN_b, L2_xcond_norm1_w, L2_xcond_qkv_W, L2_xcond_attn_out_W, L2_xcond_normc_w, L2_xcond_cq_W, L2_xcond_ck_W, L2_xcond_cv_W, L2_xcond_co_W, L2_xcond_norm2_w, L2_xcond_mlp_W1, L2_xcond_mlp_b1, L2_xcond_mlp_W2, L2_xcond_mlp_b2, mask_BxS2_bf1, mask_SxS_bk0)
    x = _L3_xcond_ref(x, ctx_1024, cond_1024, L3_xcond_Wq, L3_xcond_bq, L3_xcond_Wkv, L3_xcond_bkv, L3_xcond_Wp, L3_xcond_bp, L3_xcond_Wss_q, L3_xcond_bss_q, L3_xcond_Wss_kv, L3_xcond_bss_kv)
    return x

_drawn_inputs = setup_inputs


def setup_inputs(seed=0):
    import zlib

    import numpy as np

    out = dict(_drawn_inputs(seed))
    spreads = {'L0_xcond_b_mod': (0.0, 0.1),
     'L0_xcond_b_qkv': (0.0, 0.1),
     'L0_xcond_b_proj': (0.0, 0.1),
     'L0_xcond_b_qc': (0.0, 0.498),
     'L0_xcond_b_kvc': (0.0, 0.1),
     'L0_xcond_b_cproj': (0.0, 0.1),
     'L0_xcond_b_mlp1': (0.0, 0.1),
     'L0_xcond_b_mlp2': (0.0, 0.1),
     'L1_xcond_b_ada': (0.0, 0.715),
     'L1_xcond_b_qkv': (0.0, 0.8),
     'L1_xcond_b_so': (0.0, 0.656),
     'L1_xcond_b_q': (0.0, 0.8),
     'L1_xcond_b_kv': (0.0, 0.8),
     'L1_xcond_b_co': (0.0, 0.737),
     'L1_xcond_b_m1': (0.0, 0.8),
     'L1_xcond_b_m2': (0.0, 0.741),
     'L2_xcond_norm1_w': (1.0, 0.6),
     'L2_xcond_normc_w': (1.0, 0.6),
     'L2_xcond_norm2_w': (1.0, 0.6),
     'L3_xcond_bq': (0.0, 2.0),
     'L3_xcond_bkv': (0.0, 2.0),
     'L3_xcond_bp': (0.0, 2.0),
     'L3_xcond_bss_q': (0.0, 2.0),
     'L3_xcond_bss_kv': (0.0, 2.0)}
    factors = {'L1_xcond_w_ada': 3.22,
     'L1_xcond_w_qkv': 8.0,
     'L1_xcond_w_so': 8.0,
     'L1_xcond_w_q': 8.0,
     'L1_xcond_w_kv': 8.0,
     'L1_xcond_w_co': 8.0,
     'L1_xcond_w_m1': 8.0,
     'L1_xcond_w_m2': 8.0,
     'L2_xcond_adaLN_W': 4.369,
     'L2_xcond_adaLN_b': 8.0,
     'L2_xcond_qkv_W': 8.0,
     'L2_xcond_attn_out_W': 8.0,
     'L2_xcond_cq_W': 8.0,
     'L2_xcond_ck_W': 8.0,
     'L2_xcond_cv_W': 8.0,
     'L2_xcond_co_W': 8.0,
     'L2_xcond_mlp_W1': 5.497,
     'L2_xcond_mlp_b1': 30.161,
     'L2_xcond_mlp_W2': 5.582,
     'L2_xcond_mlp_b2': 54.55,
     'L3_xcond_Wq': 63.553,
     'L3_xcond_Wkv': 13.003,
     'L3_xcond_Wss_q': 64.0,
     'L3_xcond_Wss_kv': 48.227,
     'L3_xcond_Wp': 4.495}
    for name, (base, spread) in spreads.items():
        noise = np.random.default_rng([zlib.crc32(name.encode()), seed]).standard_normal(out[name].shape)
        drawn = base * np.exp(spread * noise) if base else spread * noise
        out[name] = jnp.asarray(drawn.astype(out[name].dtype))
    for name, factor in factors.items():
        out[name] = (out[name] * factor).astype(out[name].dtype)
    return out
```

```python
from contextlib import ExitStack

import concourse.bass as bass
import concourse.mybir as mybir
import numpy as np

ALU = mybir.AluOpType
ACT = mybir.ActivationFunctionType
AX = mybir.AxisListType.X
F32 = mybir.dt.float32
BF16 = mybir.dt.bfloat16
U8 = mybir.dt.uint8

P = 128
B, S, C = 2, 512, 128
T = S // P
H, D = 16, 8
LC = 77
HID = 512
NI = HID // P
WIN, SHIFT = 64, 32
TOPK = 16
SCALE = float(D) ** -0.5
NEG = -3.3895313892515355e38
G, HG = 4, 4
VW = D + 1

SELF0, CROSS0, WINDOW, TOPK16, SELF2, CROSS2, CROSS3 = range(7)
NSTAGE = 7
LAYER = [0, 0, 1, 1, 2, 2, 3]
OWN_KEYS = (SELF0, WINDOW, SELF2)
FULL = (SELF0, SELF2)
CTX_OF = {CROSS0: 0, TOPK16: 1, CROSS2: 2, CROSS3: 3}
MLP_AFTER = (CROSS0, TOPK16, CROSS2)
LN_EPS = [1e-6, 1e-6, 1e-5, 1e-5]

Q_PART = [0, 0, 1, 1, 0, 2]
K_PART = [0, 1, 0, 1, 2, 0]
QK_ROWS = len(Q_PART) * D
ROWS = QK_ROWS + 3

MODS = [(0, 0, 1), (0, 3, 4), (1, 0, 1), (1, 3, 4), (1, 6, 7), (2, 0, 1), (2, 3, 4), (2, 6, 7),
        (3, 1, 0), (3, 3, 2)]
MOD_OF = {(SELF0, 0): 0, (CROSS0, 1): 1, (WINDOW, 0): 2, (TOPK16, 0): 3, (TOPK16, 1): 4, (SELF2, 0): 5,
          (CROSS2, 0): 6, (CROSS2, 1): 7, (CROSS3, 0): 8}
MOD_KV3 = 9
GATED = [(0, 2, 1, "proj0"), (0, 5, NI, "down0"), (1, 2, 1, "so"), (1, 5, 1, "co"), (1, 8, NI, "down1"),
         (2, 2, 1, "ao"), (2, 5, 1, "co2"), (2, 8, NI, "down2")]
GATE_OF = {(SELF0, 0): 0, (CROSS0, 1): 1, (WINDOW, 0): 2, (TOPK16, 0): 3, (TOPK16, 1): 4, (SELF2, 0): 5,
           (CROSS2, 0): 6, (CROSS2, 1): 7}

def offsets(parts):
    at, out = 0, {}
    for name, n in parts:
        out[name] = (at, n)
        at += n
    return out, at


W_MAIN = [("q0", C), ("k0", C), ("v0", C), ("qc0", C), ("kc0", C), ("vc0", C), ("cp0", C), ("up0", HID),
          ("q1", C), ("k1", C), ("v1", C), ("qc1", C), ("kc1", C), ("vc1", C), ("up1a", HID), ("up1b", HID),
          ("q2", C), ("k2", C), ("v2", C), ("q2s", C), ("k2s", C), ("qc2", C), ("kc2", C), ("vc2", C),
          ("up2", HID), ("qc3", C), ("kc3", C), ("vc3", C), ("p3", C)]
W_AT, W_COLS = offsets(W_MAIN)
W_FIRST = W_AT["qc0"][0]
ADA_AT, ADA_COLS = offsets([(0, 6 * C), (1, 9 * C), (2, 9 * C), (3, 4 * C)])
RAW_AT, RAW_COLS = offsets([(i, n * C) for i, (_, _, n, _) in enumerate(GATED)])
COL_AT, COLS = offsets([("mod", 2 * len(MODS)), ("norm", 3), ("q0", 1), ("k0", 1), ("q1", 1), ("k1", 1),
                        ("qc0", 1), ("qc1", 1), ("qc3", 1), ("kc0", 1), ("kc1", 1), ("kc3", 1), ("up0", NI),
                        ("up1a", NI), ("up1b", NI), ("up2", NI), ("cond", B)])
VROW_AT, VROWS = offsets([("v0", C), ("v1", C), ("vc0", C), ("vc1", C), ("vc3", C)])
ROW_AT, ROWCOLS = offsets([("gate", len(GATED) * C), ("out", len(GATED) * C), ("cp0", C), ("p3", C)])

UNITS = [(s, b) for s in range(NSTAGE) for b in range(B)]


def pieces_of_prep(s, b):
    u = (s, b)
    out = [("ln", u, 0), ("hT", u, 0)]
    if s == SELF2:
        out += [("q", u), ("qs", u), ("k", u), ("ks", u), ("v", u)]
    elif s in OWN_KEYS:
        out += [("q", u), ("k", u), ("v", u)]
    else:
        out += [("q", u)]
    out.append(("stack", u))
    if s in FULL:
        out += [("mx", u, h, t) for h in range(H) for t in range(T)]
    elif s == TOPK16:
        return out + [("tk", u, h) for h in range(H)] + [("tkend", u)]
    else:
        out += [("mx", u, h, 0) for h in range(H)]
    return out + [("m", u), ("mT", u)]


def pieces_of_post(s, b):
    u = (s, b)
    out = [("oT", u, t) for t in range(T)] + [("onT", u), ("proj", u)]
    if s in MLP_AFTER:
        out += [("ln", u, 1), ("hT", u, 1)]
        if LAYER[s] == 1:
            out += [(n, u, i) for i in range(NI) for n in ("ha", "hb")]
        else:
            out += [("ha", u, i) for i in range(NI)]
        out.append(("down", u))
    if s == NSTAGE - 1:
        out.append(("out", u))
    return out


PROLOGUE = [("mod",)] + pieces_of_prep(*UNITS[0]) + [("cT",)] + [("ck", c) for c in range(4)] \
    + [("cv", c) for c in range(4)] + [("gate", i) for i in range(len(GATED))] + [("mask", t) for t in range(T)]


def pieces_beside(k):
    return (pieces_of_post(*UNITS[k - 1]) if k else []) + (pieces_of_prep(*UNITS[k + 1]) if k + 1 < len(UNITS) else [])


CHAIN = PROLOGUE + [x for k in range(len(UNITS)) for x in pieces_beside(k)] + pieces_of_post(*UNITS[-1])
NO_BANK = ("ln", "stack", "m", "tkend", "out")


def reader(x):
    if x[0] in ("q", "k"):
        return "V" if x[1][0] == SELF2 else "S"
    return "S" if x[0] in ("hT", "ck", "mask", "mT", "tk", "onT", "ha") else "V"


BANKED = [x for x in CHAIN if x[0] not in NO_BANK]
BANKS = 3
BANK_NO = {x: n for n, x in enumerate(BANKED)}


class Count:

    def __init__(self, sem, events):
        self.sem = sem
        self.after = {e: i + 1 for i, e in enumerate(events)}

    def __getitem__(self, event):
        return self.after[event]


def items_of(k):
    s, _ = UNITS[k]
    if s in FULL:
        return [(k, g, half, j) for g in range(G) for half in range(2) for j in range(HG)]
    return [(k, g, 0, j) for g in range(G) for j in range(0, HG, 2)]


def batches_of(k):
    s, _ = UNITS[k]
    return [(k, g, half) for g in range(G) for half in range(2 if s in FULL else 1)]


ITEMS = [i for k in range(len(UNITS)) for i in items_of(k)]
ITEM_NO = {x: n for n, x in enumerate(ITEMS)}
BATCHES = [x for k in range(len(UNITS)) for x in batches_of(k)]
GROUPS = [(k, g) for k in range(len(UNITS)) for g in range(G)]
RING = 6


def last_item(batch):
    k, g, half = batch
    return (k, g, half, HG - 1 if UNITS[k][0] in FULL else HG - 2)


def batch_of(item):
    return item[:3]


def chain_share(k, i):
    return (i + 1) * len(pieces_beside(k)) // len(items_of(k))


def pixart_four_layers(nc, x_in, ctx_in, cmask_in, smask_in, w_in, ada_in, raw_in, col_in, vrow_in,
                       row_in, ident_in, wmask_in, rope_in, out):
    with ExitStack() as stack:
        def sb(name, shape, dt=F32):
            return stack.enter_context(nc.sbuf_tensor(name, shape, dt))

        def sem(name):
            return stack.enter_context(nc.semaphore(name))

        X = sb("X", [P, B * T, C])
        ctx = sb("ctx", [LC, B, C])
        W = sb("W", [P, W_COLS])
        cols = sb("cols", [P, COLS])
        vrows = sb("vrows", [P, VROWS])
        rows = sb("rows", [1, ROWCOLS])
        ident = sb("ident", [P, P])
        identb = sb("identb", [P, P], BF16)
        wmask = sb("wmask", [P, S], BF16)
        rope = sb("rope", [P, 2, S])
        ones = sb("ones", [1, P])
        onesb = sb("onesb", [3, S], BF16)
        half_neg = sb("half_neg", [P, T])
        acts = sb("acts", [P, 2, B])
        M = sb("M", [P, len(MODS), 2, B])
        Wg = sb("Wg", [P, B, RAW_COLS])
        rowg = sb("rowg", [1, len(GATED), B, C])
        mask_q = sb("mask_q", [P, T, S], BF16)
        mask_k = sb("mask_k", [P, T, S], BF16)
        cmask_u8 = sb("cmask_u8", [1, B * LC], U8)
        cmask = sb("cmask", [1, B, T, LC], BF16)
        ctx_parts = sb("ctx_parts", [P, 4, 3, B * LC], BF16)
        ctx_V = sb("ctx_V", [LC, 4, B, H * VW])
        QS = sb("QS", [P, H, S], BF16)
        KS = sb("KS", [P, H, S], BF16)
        V1 = sb("V1", [P, B, T, H * VW])
        OG = sb("OG", [P, B, G, S])
        stats = sb("stats", [P, T, 6])
        mv = sb("mv", [P, T, 2])
        veps = sb("veps", [P, T])
        rstd = sb("rstd", [P, T])
        xhat = sb("xhat", [P, T, C])
        hT = sb("hT", [P, S])
        U = sb("U", [P, NI, S])
        qkf = U[:, 0:2, :]
        res = U[:, 2:4, :]
        parts = sb("parts", [P, 2, 3, S], BF16)
        mmax = sb("mmax", [P, T, H])
        mres = sb("mres", [P, T, H])
        mparts = sb("mparts", [P, T, 3, H], BF16)
        mT = sb("mT", [3 * H, S], BF16)
        junk = sb("junk", [P, S], BF16)
        top = sb("top", [P, 2, T, 16])
        nbias = sb("nbias", [P, 2, T])
        left = sb("left", [P, 2, T, LC])
        rsum = sb("rsum", [P, T, H])
        On, OT = xhat, hT
        gated = parts[:, :, :, :].rearrange("p i n s -> p (i n s)").bitcast(F32)[:, 0:2 * S]\
            .rearrange("p (i s) -> p i s", i=2)
        PQ = sb("PQ", [P, H, T * LC])
        PT = sb("PT", [P, RING, 2 * S])
        early = PT[:, :, :].rearrange("p r n -> p (r n)")
        n_ctx, n_hat, n_wide = 3 * B * LC, 2 * B * C, 2 * B * P
        ctxT = early[:, 0:n_ctx].rearrange("p (n b k) -> p n b k", n=3, b=B)
        ctx_hat = early[0:LC, n_ctx:n_ctx + n_hat].rearrange("p (n b c) -> p n b c", n=2, b=B)
        acts_wide = early[:, n_ctx + n_hat:n_ctx + n_hat + n_wide].rearrange("p (k b n) -> p k b n", k=2, b=B)
        ada = PQ[:, :, :].rearrange("p h n -> p (h n)")[:, 0:ADA_COLS]
        early_og = OG[:, :, :, :].rearrange("p b g s -> p (b g s)")
        raw = early_og[:, 0:RAW_COLS]
        mask_u8 = early_og[:, RAW_COLS:RAW_COLS + T * S // 4].bitcast(U8)
        wmask32 = early_og[:, RAW_COLS + T * S // 4:RAW_COLS + T * S // 4 + P]

        scores = [stack.enter_context(nc.psum_tensor(f"scores{i}", [P, 2 * S], F32)) for i in range(2)]
        outputs = stack.enter_context(nc.psum_tensor("outputs", [P, S], F32))
        banks = [stack.enter_context(nc.psum_tensor(f"bank{i}", [P, S], F32)) for i in range(BANKS)]

        s_small = sem("small_inputs_loaded")
        s_ada = sem("ada_loaded")
        s_x = sem("x_loaded")
        s_w0 = sem("first_weights_loaded")
        s_w = sem("weights_loaded")
        s_raw = sem("raw_weights_loaded")
        s_late = sem("late_inputs_loaded")
        s_const = sem("constants_set")
        s_vset = sem("vector_constants_set")
        s_silu = sem("silu_done")
        s_wide = sem("conditioning_widened")
        s_cmask = sem("masks_made")
        s_vchain = sem("vector_step_done")
        s_pchain = sem("pool_step_done")
        s_ones = [sem(f"ones_rows_placed{b}") for b in range(B)]
        s_qs = [sem(f"query_stack_placed{b}") for b in range(B)]
        s_ms = [sem(f"maximum_stack_placed{b}") for b in range(B)]
        s_out = sem("output_stored")

        filled = Count(sem("chain_bank_filled"), BANKED)
        emptied_by_vector = Count(sem("bank_emptied_by_vector"), [x for x in BANKED if reader(x) == "V"])
        emptied_by_scalar = Count(sem("bank_emptied_by_scalar"), [x for x in BANKED if reader(x) == "S"])
        lns = [x for x in CHAIN if x[0] == "ln"]
        lns[1:1] = [("ln", "ctx", 0), ("ln", "ctx", 1)]
        variance = Count(sem("variance_ready"), lns)
        rstd_ready = Count(sem("rstd_ready"), lns)
        normed = Count(sem("normed"), lns)
        stacks = [x for x in CHAIN if x[0] == "stack"]
        rope_q = Count(sem("roped"), [("rope", u, n) for _, u in stacks if u[0] == SELF2 for n in "qk"])
        vec_split = Count(sem("parts_made_by_vector"),
                          [("split", u) for _, u in stacks[:1]] + [("split", c) for c in range(4)]
                          + [("split", u) for _, u in stacks[1:]])
        pool_split = Count(sem("parts_made_by_pool"), [("split", u) for _, u in stacks if u[0] in OWN_KEYS])
        max_parts = Count(sem("maximum_parts_made"), [x for x in CHAIN if x[0] == "m"])
        top_found = Count(sem("top16_found"), [x for x in CHAIN if x[0] == "tk"])
        top_kept = Count(sem("top16_kept"), [x for x in CHAIN if x[0] == "tk"])
        scored = Count(sem("scores_ready"), ITEMS)
        exped = Count(sem("probabilities_ready"), ITEMS)
        summed = Count(sem("values_summed"), BATCHES)
        saved = Count(sem("outputs_saved"), GROUPS)

        def bank(x):
            return banks[BANK_NO[x] % BANKS]

        def free_bank(pe, x):
            n = BANK_NO[x]
            if n >= BANKS:
                last = BANKED[n - BANKS]
                if reader(last) == "V":
                    pe.wait_ge(emptied_by_vector.sem, emptied_by_vector[last])
                else:
                    pe.wait_ge(emptied_by_scalar.sem, emptied_by_scalar[last])
            return banks[n % BANKS]

        def w(name, i=0, n=C):
            at = W_AT[name][0] + i * n
            return W[:, at:at + n]

        def col(name, i=0, n=1):
            at = COL_AT[name][0] + i
            return cols[:, at:at + n]

        def heads(ap):
            return ap.rearrange("p (h v) -> p h v", v=VW)

        def stack_rows(b, n=ROWS):
            return slice(64 * b, 64 * b + n)

        def chain_steps(do, k):
            for x in pieces_beside(k):
                do(x)
                yield

        def beside(steps, k, i):
            before = chain_share(k, i - 1) if i else 0
            for _ in range(chain_share(k, i) - before):
                next(steps)

        block = stack.enter_context(nc.Block())

        @block.sync
        def _(sp):
            sp.dma_start(cols[:, :], col_in).then_inc(s_small, 16)
            sp.dma_start(ident[:, :], ident_in).then_inc(s_small, 16)
            sp.dma_start(X[:, :, :], x_in.rearrange("b (t p) c -> p (b t) c", p=P)).then_inc(s_x, 16)
            sp.dma_start(ada, ada_in).then_inc(s_ada, 16)
            sp.dma_start(W[:, 0:W_FIRST], w_in[:, 0:W_FIRST]).then_inc(s_w0, 16)
            sp.dma_start(vrows[:, :], vrow_in.partition_broadcast(P)).then_inc(s_small, 16)
            sp.dma_start(rows[:, :], row_in).then_inc(s_small, 16)
            sp.dma_start(ctx[:, :, :], ctx_in.rearrange("b t c -> t b c")).then_inc(s_small, 16)
            sp.dma_start(W[:, W_FIRST:], w_in[:, W_FIRST:]).then_inc(s_w, 16)
            sp.dma_start(raw, raw_in).then_inc(s_raw, 16)
            sp.dma_start(mask_u8.rearrange("p (t s) -> p t s", t=T),
                         smask_in.rearrange("(t p) s -> p t s", p=P)).then_inc(s_late, 16)
            sp.dma_start(cmask_u8[:, :], cmask_in).then_inc(s_late, 16)
            sp.dma_start(wmask32, wmask_in).then_inc(s_late, 16)
            sp.dma_start(rope[:, :, :], rope_in).then_inc(s_late, 16)
            sp.wait_ge(s_const, 1)
            for b in range(B):
                r = 64 * b + QK_ROWS
                sp.dma_start(KS[r:r + 3, :, :], onesb[:, :].unsqueeze(1).broadcast_to([3, H, S])).then_inc(s_ones[b], 16)

            def do(x):
                if x[0] == "stack":
                    s, b = u = x[1]
                    c = CTX_OF.get(s)
                    if s in OWN_KEYS:
                        sp.wait_ge(pool_split.sem, pool_split[("split", u)])
                        sp.wait_ge(vec_split.sem, vec_split[("split", u)])
                    else:
                        sp.wait_ge(vec_split.sem, vec_split[("split", u)])
                    for i, (qp, kp) in enumerate(zip(Q_PART, K_PART)):
                        r = slice(64 * b + i * D, 64 * b + (i + 1) * D)
                        sp.dma_start(QS[r, :, :], parts[:, 0, qp, :]).then_inc(s_qs[b], 16)
                        if s in OWN_KEYS:
                            sp.dma_start(KS[r, :, :], parts[:, 1, kp, :]).then_inc(s_qs[b], 16)
                        else:
                            sp.dma_start(KS[r, :, 0:LC], ctx_parts[:, c, kp, b * LC:(b + 1) * LC])\
                              .then_inc(s_qs[b], 16)
                if x[0] == "mT":
                    b = x[1][1]
                    sp.wait_ge(emptied_by_scalar.sem, emptied_by_scalar[x])
                    r = 64 * b + QK_ROWS
                    sp.dma_start(QS[r:r + 3, :, :], mT[:, :]).then_inc(s_ms[b], 16)
                if x[0] == "out":
                    b = x[1][1]
                    sp.wait_ge(emptied_by_vector.sem, emptied_by_vector[("proj", x[1])])
                    sp.dma_start(out.rearrange("b (t p) c -> p (b t) c", p=P)[:, b * T:(b + 1) * T, :],
                                 X[:, b * T:(b + 1) * T, :]).then_inc(s_out, 16)

            for x in CHAIN:
                do(x)
            sp.wait_ge(s_out, 16 * B)

        def stacks_placed(engine, u):
            s, b = u
            engine.wait_ge(s_qs[b], 16 * 2 * len(Q_PART) * (s + 1))

        def maximum_placed(engine, u):
            s, b = u
            engine.wait_ge(s_ms[b], 16 * (s + 1 - (s > TOPK16)))

        @block.gpsimd
        def _(pool):
            chain = [0]

            def link(ins):
                chain[0] += 1
                ins.then_inc(s_pchain, 1)
                pool.wait_ge(s_pchain, chain[0])

            pool.memset(onesb[:, :], 1.0).then_inc(s_const, 1)
            pool.memset(ones[:, :], 1.0).then_inc(s_const, 1)
            link(pool.memset(half_neg[:, :], -0.5))
            pool.wait_ge(s_small, 16 * 5)
            pool.tensor_copy(identb[:, :], ident[:, :]).then_inc(s_const, 1)

            def root(x, n=P, m=T):
                pool.wait_ge(variance.sem, variance[x])
                pool.tensor_tensor(rstd[0:n, 0:m], veps[0:n, 0:m], half_neg[0:n, 0:m], ALU.pow)\
                    .then_inc(rstd_ready.sem, 1)

            def do(x):
                if x[0] == "ln":
                    root(x)
                if x[0] == "stack" and x[1][0] in OWN_KEYS:
                    u = x[1]
                    if u[0] == SELF2:
                        pool.wait_ge(rope_q.sem, rope_q[("rope", u, "q")])
                    else:
                        pool.wait_ge(emptied_by_scalar.sem, emptied_by_scalar[("q", u)])
                    f, r, p = qkf[:, 0, :], res[:, 0, :], parts[:, 0]
                    link(pool.tensor_copy(p[:, 0, :], f))
                    link(pool.tensor_tensor(r, f, p[:, 0, :], ALU.subtract))
                    link(pool.tensor_copy(p[:, 1, :], r))
                    pool.tensor_tensor(p[:, 2, :], r, p[:, 1, :], ALU.subtract).then_inc(pool_split.sem, 1)
                if x[0] == "cT":
                    root(("ln", "ctx", 0), LC, B)
                    root(("ln", "ctx", 1), LC, B)
                    pool.wait_ge(s_late, 64)
                    for t in range(T):
                        pool.tensor_copy(wmask[:, t * P:(t + 1) * P], wmask32).then_inc(s_cmask, 1)
                    pool.tensor_scalar(mask_q[:, :, :], mask_u8.rearrange("p (t s) -> p t s", t=T), -1.0, -NEG,
                                       ALU.add, ALU.mult).then_inc(s_cmask, 1)
                    for t in range(T):
                        pool.tensor_scalar(cmask[:, :, t, :], cmask_u8.rearrange("p (b k) -> p b k", b=B),
                                           -1.0, -NEG, ALU.add, ALU.mult).then_inc(s_cmask, 1)

            for x in CHAIN:
                do(x)

        @block.scalar
        def _(act):
            act.wait_ge(s_small, 16 * 5)
            act.activation(acts[:, 1, :], col("cond", 0, B), ACT.Silu).then_inc(s_silu, 1)

            def do(x):
                if x[0] in NO_BANK or reader(x) != "S":
                    return
                empty = emptied_by_scalar.sem
                act.wait_ge(filled.sem, filled[x])
                src = bank(x)
                if x[0] == "hT":
                    (s, b), which = x[1:]
                    mod = MOD_OF.get((s, which))
                    runs = [(0, 0, S)]
                    if s == WINDOW:
                        runs = [(0, SHIFT, S - SHIFT), (S - SHIFT, 0, SHIFT)]
                    for to, at, n in runs:
                        if mod is None:
                            ins = act.activation(hT[:, to:to + n], src[:, at:at + n], ACT.Copy)
                        else:
                            ins = act.activation(hT[:, to:to + n], src[:, at:at + n], ACT.Identity,
                                                 bias=M[:, mod, 0, b:b + 1], scale=M[:, mod, 1, b:b + 1])
                    ins.then_inc(empty, 1)
                if x[0] in ("q", "k"):
                    s = x[1][0]
                    i = "qk".index(x[0])
                    name = f"{x[0]}{LAYER[s]}" if s in OWN_KEYS else f"qc{LAYER[s]}"
                    if s == CROSS2:
                        act.activation(qkf[:, i, :], src[:, :], ACT.Copy).then_inc(empty, 1)
                    else:
                        act.activation(qkf[:, i, :], src[:, :], ACT.Identity, bias=col(name)).then_inc(empty, 1)
                if x[0] == "ck":
                    c = x[1]
                    if c:
                        act.wait_ge(vec_split.sem, vec_split[("split", c - 1)])
                    else:
                        act.wait_ge(vec_split.sem, vec_split[("split", UNITS[0])])
                    f = qkf[:, 1, 0:B * LC]
                    if c == 2:
                        act.activation(f, src[:, 0:B * LC], ACT.Copy).then_inc(empty, 1)
                    else:
                        act.activation(f, src[:, 0:B * LC], ACT.Identity, bias=col(f"kc{c}")).then_inc(empty, 1)
                if x[0] == "mask":
                    act.copy(mask_k[:, x[1], :], src[:, :].bitcast(BF16)[:, 0:S]).then_inc(empty, 1)
                if x[0] == "mT":
                    act.copy(mT[:, :], src[0:3 * H, :].bitcast(BF16)[:, 0:S]).then_inc(empty, 1)
                if x[0] == "tk":
                    u, h = x[1:]
                    act.wait_ge(top_found.sem, top_found[x])
                    k = UNITS.index(u)
                    if u[1] > 0:
                        act.wait_ge(scored.sem, scored[(k - 1, h // HG, 0, h % HG // 2 * 2)])
                    for t in range(T):
                        ins = act.activation(PQ[:, h, t * LC:(t + 1) * LC], src[:, t * LC:(t + 1) * LC], ACT.Exp,
                                             bias=nbias[:, h % 2, t:t + 1], scale=SCALE)
                    ins.then_inc(empty, 1)
                if x[0] == "onT":
                    s = x[1][0]
                    if s == WINDOW:
                        act.copy(OT[:, SHIFT:S], src[:, 0:S - SHIFT])
                        act.copy(OT[:, 0:SHIFT], src[:, S - SHIFT:S]).then_inc(empty, 1)
                    else:
                        act.copy(OT[:, :], src[:, :]).then_inc(empty, 1)
                if x[0] == "ha":
                    (s, b), i = x[1:]
                    if LAYER[s] == 1:
                        if i >= 2:
                            act.wait_ge(emptied_by_vector.sem, emptied_by_vector[("hb", x[1], i - 2)])
                        act.activation(gated[:, i % 2, :], src[:, :], ACT.Silu, bias=col("up1a", i)).then_inc(empty, 1)
                    else:
                        act.activation(U[:, i, :], src[:, :], ACT.Gelu_apprx_tanh,
                                       bias=col(f"up{LAYER[s]}", i)).then_inc(empty, 1)

            def probabilities(item):
                k, g, half, j = item
                s, b = UNITS[k]
                n = ITEM_NO[item]
                keys = P if s in OWN_KEYS else LC
                if n >= RING:
                    act.wait_ge(summed.sem, summed[batch_of(ITEMS[n - RING])])
                act.wait_ge(scored.sem, scored[item])
                func = ACT.Copy if s == TOPK16 else ACT.Exp
                act.activation(PT[0:keys, n % RING, :], scores[n % 2][0:keys, :], func,
                               scale=1.0 if s == TOPK16 else SCALE).then_inc(exped.sem, 1)

            def save(k, g):
                b = UNITS[k][1]
                halves = 2 if UNITS[k][0] in FULL else 1
                act.wait_ge(summed.sem, summed[(k, g, halves - 1)])
                if k >= B and g == 0:
                    act.wait_ge(filled.sem, filled[("oT", UNITS[k - B], T - 1)])
                act.copy(OG[:, b, g, :], outputs[:, :]).then_inc(saved.sem, 1)

            for x in PROLOGUE:
                do(x)
            for k in range(len(UNITS)):
                items = items_of(k)
                steps = chain_steps(do, k)
                waiting = batches_of(k)
                for i, item in enumerate(items):
                    probabilities(item)
                    beside(steps, k, i)
                    while waiting and i >= items.index(last_item(waiting[0])) + 2:
                        if waiting[0][2] == (1 if UNITS[k][0] in FULL else 0):
                            save(k, waiting[0][1])
                        waiting.pop(0)
                for batch in waiting:
                    if batch[2] == (1 if UNITS[k][0] in FULL else 0):
                        save(k, batch[1])
            for x in pieces_of_post(*UNITS[-1]):
                do(x)

        @block.vector
        def _(dve):
            chain = [0]

            def link(ins):
                chain[0] += 1
                ins.then_inc(s_vchain, 1)
                dve.wait_ge(s_vchain, chain[0])

            dve.memset(V1[:, :, :, :], 1.0).then_inc(s_vset, 1)
            dve.memset(ctx_V[:, :, :, :], 1.0).then_inc(s_vset, 1)
            dve.memset(outputs[:, :], 0.0).then_inc(s_vset, 1)

            def norm(x, src, tiles, n, eps, to):
                for t in range(tiles):
                    ins = dve.bn_stats(stats[0:n, t, :], src(t))
                    if t < tiles - 1:
                        chain[0] += 1
                        ins.then_inc(s_vchain, 1)
                    else:
                        link(ins)
                for t in range(tiles):
                    ins = dve.bn_aggr(mv[0:n, t, :], stats[0:n, t, :])
                    if t < tiles - 1:
                        chain[0] += 1
                        ins.then_inc(s_vchain, 1)
                    else:
                        link(ins)
                dve.tensor_scalar(veps[0:n, 0:tiles], mv[0:n, 0:tiles, 1], eps, None, ALU.add)\
                   .then_inc(variance.sem, 1)
                dve.wait_ge(rstd_ready.sem, rstd_ready[x])
                for t in range(tiles):
                    ins = dve.tensor_scalar(to(t), src(t), mv[0:n, t, 0:1], rstd[0:n, t:t + 1],
                                            ALU.subtract, ALU.mult)
                ins.then_inc(normed.sem, 1)

            def split(f, r, p):
                link(dve.tensor_copy(p[:, 0], f))
                link(dve.tensor_tensor(r, f, p[:, 0], ALU.subtract))
                link(dve.tensor_copy(p[:, 1], r))
                dve.tensor_tensor(p[:, 2], r, p[:, 1], ALU.subtract).then_inc(vec_split.sem, 1)

            def keep_top(u, h):
                dve.wait_ge(emptied_by_scalar.sem, emptied_by_scalar[("tk", u, h)])
                dve.scalar_tensor_tensor(out=PQ[:, h, :], in0=left[:, h % 2].rearrange("p t k -> p (t k)"),
                                         scalar=NEG, in1=PQ[:, h, :], op0=ALU.is_le, op1=ALU.mult)\
                   .then_inc(top_kept.sem, 1)

            def do(x):
                name = x[0]
                empty = emptied_by_vector.sem
                if name == "ln":
                    (s, b), which = x[1:]
                    if x is CHAIN[1]:
                        dve.wait_ge(s_x, 16)
                    elif which:
                        dve.wait_ge(emptied_by_vector.sem, emptied_by_vector[("proj", x[1])])
                    elif s > 0:
                        before = (s - 1, b)
                        dve.wait_ge(emptied_by_vector.sem, emptied_by_vector[("down", before) if s - 1 in MLP_AFTER else ("proj", before)])
                    norm(x, lambda t: X[:, b * T + t, :], T, P, LN_EPS[LAYER[s]], lambda t: xhat[:, t, :])
                    return
                if name == "stack":
                    s, b = u = x[1]
                    i = 1 if s in OWN_KEYS else 0
                    if s == SELF2:
                        dve.wait_ge(rope_q.sem, rope_q[("rope", u, "k")])
                    else:
                        dve.wait_ge(emptied_by_scalar.sem, emptied_by_scalar[("k" if i else "q", u)])
                    split(qkf[:, i, :], res[:, i, :], parts[:, i])
                    return
                if name == "m":
                    s, b = x[1]
                    dve.wait_ge(emptied_by_vector.sem, emptied_by_vector[[y for y in BANKED if y[0] == "mx" and y[1] == x[1]][-1]])
                    link(dve.tensor_scalar(mparts[:, :, 0, :], mmax[:, :, :], -1.0, None, ALU.mult))
                    link(dve.scalar_tensor_tensor(out=mres[:, :, :], in0=mmax[:, :, :], scalar=-1.0,
                                                  in1=mparts[:, :, 0, :], op0=ALU.mult, op1=ALU.subtract))
                    link(dve.tensor_copy(mparts[:, :, 1, :], mres[:, :, :]))
                    dve.tensor_tensor(mparts[:, :, 2, :], mres[:, :, :], mparts[:, :, 1, :], ALU.subtract)\
                       .then_inc(max_parts.sem, 1)
                    return
                if name == "tkend":
                    keep_top(x[1], H - 1)
                    return
                if name == "cT":
                    for n, eps in enumerate((LN_EPS[0], LN_EPS[3])):
                        norm(("ln", "ctx", n), lambda t: ctx[:, t, :], B, LC, eps, lambda t: ctx_hat[:, n, t, :])
                if name in NO_BANK or (reader(x) != "V" and name != "tk"):
                    return
                dve.wait_ge(filled.sem, filled[x])
                src = bank(x)
                if name == "mod":
                    n = len(MODS)
                    bias = col("mod", 0, 2 * n)
                    m2 = M[:, :, :, :].rearrange("p m k b -> p (m k) b")
                    link(dve.tensor_tensor(m2, src[:, 0:2 * n * B].rearrange("p (m b) -> p m b", b=B),
                                           bias.unsqueeze(2).broadcast_to([P, 2 * n, B]), ALU.add))
                    link(dve.tensor_scalar(M[:, :, 1, :], M[:, :, 1, :], 1.0, None, ALU.add))
                    dve.tensor_tensor(M[:, 5:8, 1, :], M[:, 5:8, 1, :],
                                      col("norm", 0, 3).unsqueeze(2).broadcast_to([P, 3, B]),
                                      ALU.mult).then_inc(empty, 1)
                if name == "v":
                    s, b = x[1]
                    to = heads(V1[:, b].rearrange("p t n -> p (t n)"))[:, :, 0:D]
                    frm = src[:, :].rearrange("p (n d) -> p n d", d=D)
                    if s == SELF2:
                        dve.tensor_copy(to, frm).then_inc(empty, 1)
                    else:
                        at = VROW_AT[f"v{LAYER[s]}"][0]
                        bias = vrows[:, at:at + C].rearrange("p (h d) -> p h d", d=D)
                        for t in range(T):
                            ins = dve.tensor_tensor(to[:, t * H:(t + 1) * H, :], frm[:, t * H:(t + 1) * H, :],
                                                    bias, ALU.add)
                        ins.then_inc(empty, 1)
                if name in ("q", "qs", "k", "ks"):
                    u = x[1]
                    i = "qk".index(name[0])
                    if len(name) == 1:
                        dve.tensor_tensor(qkf[:, i, :], src[:, :], rope[:, 0, :], ALU.mult).then_inc(empty, 1)
                    else:
                        dve.tensor_tensor(res[:, i, :], src[:, :], rope[:, 1, :], ALU.mult).then_inc(empty, 1)
                        dve.wait_ge(emptied_by_vector.sem, emptied_by_vector[x])
                        dve.tensor_tensor(qkf[:, i, :], qkf[:, i, :], res[:, i, :], ALU.add)\
                           .then_inc(rope_q.sem, 1)
                if name == "mx":
                    (s, b), h, t = x[1:]
                    if s == SELF0:
                        dve.tensor_reduce(mmax[:, t, h:h + 1], src[:, :], AX, ALU.max).then_inc(empty, 1)
                    elif s == SELF2:
                        if h + t:
                            dve.wait_ge(emptied_by_vector.sem, emptied_by_vector[BANKED[BANK_NO[x] - 1]])
                        dve.tensor_tensor_reduce(junk[:, :], src[:, :], mask_q[:, t, :], 1.0, NEG, ALU.add, ALU.max,
                                                 mmax[:, t, h:h + 1]).then_inc(empty, 1)
                    else:
                        n = P if s == WINDOW else LC
                        dve.tensor_reduce(mmax[:, :, h:h + 1], src[:, 0:T * n].rearrange("p (t k) -> p t k", t=T),
                                          AX, ALU.max).then_inc(empty, 1)
                if name == "tk":
                    u, h = x[1:]
                    a = h % 2
                    if h >= 2:
                        dve.wait_ge(top_kept.sem, top_kept[("tk", u, h - 2)])
                    tile = [src[:, t * LC:(t + 1) * LC] for t in range(T)]
                    steps = [lambda t: dve.max(top[:, a, t, 0:8], tile[t]),
                             lambda t: dve.match_replace(left[:, a, t, :], top[:, a, t, 0:8], tile[t], NEG),
                             lambda t: dve.max(top[:, a, t, 8:16], left[:, a, t, :]),
                             lambda t: dve.match_replace(left[:, a, t, :], top[:, a, t, 8:16], left[:, a, t, :], NEG)]
                    for step in steps:
                        for t in range(T):
                            chain[0] += 1
                            step(t).then_inc(s_vchain, 1)
                        dve.wait_ge(s_vchain, chain[0])
                    dve.tensor_scalar(nbias[:, a, :], top[:, a, :, 0], -SCALE, None, ALU.mult)\
                       .then_inc(top_found.sem, 1)
                    if h:
                        keep_top(u, h - 1)
                if name == "oT":
                    t = x[2]
                    v = src[:, :].rearrange("p (h r) -> p h r", r=P // HG)
                    link(dve.reciprocal(rsum[:, t, :], v[:, :, D]))
                    dve.tensor_tensor(On[:, t, :].rearrange("p (h d) -> p h d", d=D), v[:, :, 0:D],
                                      rsum[:, t, :].unsqueeze(2).broadcast_to([P, H, D]), ALU.mult)\
                       .then_inc(empty, 1)
                if name in ("proj", "down"):
                    b = x[1][1]
                    xs = X[:, b * T:(b + 1) * T, :].rearrange("p t c -> p (t c)")
                    dve.tensor_tensor(xs, src[:, :], xs, ALU.add).then_inc(empty, 1)
                if name == "hb":
                    (s, b), i = x[1:]
                    dve.wait_ge(emptied_by_scalar.sem, emptied_by_scalar[("ha", x[1], i)])
                    dve.scalar_tensor_tensor(out=U[:, i, :], in0=src[:, :], scalar=col("up1b", i),
                                             in1=gated[:, i % 2, :], op0=ALU.add, op1=ALU.mult).then_inc(empty, 1)
                if name == "cT":
                    cs = src[:, 0:2 * B * LC].rearrange("p (n b k) -> p n b k", n=2, b=B)
                    link(dve.tensor_copy(ctxT[:, 0:2], cs))
                    for b in range(B):
                        ins = dve.tensor_scalar(ctxT[:, 2, b, :], src[:, (2 * B + b) * LC:(2 * B + b + 1) * LC],
                                                M[:, MOD_KV3, 1, b:b + 1], M[:, MOD_KV3, 0, b:b + 1],
                                                ALU.mult, ALU.add)
                    ins.then_inc(empty, 1)
                if name == "cv":
                    c = x[1]
                    to = heads(ctx_V[:, c].rearrange("p b n -> p (b n)"))[:, :, 0:D]
                    frm = src[0:LC, 0:B * C].rearrange("p (n d) -> p n d", d=D)
                    if c == 2:
                        dve.tensor_copy(to, frm).then_inc(empty, 1)
                    else:
                        at = VROW_AT[f"vc{c}"][0]
                        bias = vrows[0:LC, at:at + C].rearrange("p (h d) -> p h d", d=D)
                        for b in range(B):
                            ins = dve.tensor_tensor(to[:, b * H:(b + 1) * H, :], frm[:, b * H:(b + 1) * H, :], bias,
                                                    ALU.add)
                        ins.then_inc(empty, 1)
                if name == "gate":
                    i = x[1]
                    n = GATED[i][2]
                    at = RAW_AT[i][0]
                    for b in range(B):
                        g = src[:, b * C:(b + 1) * C].unsqueeze(1).broadcast_to([P, n, C])
                        dve.tensor_tensor(Wg[:, b, at:at + n * C].rearrange("p (n c) -> p n c", n=n), g,
                                          raw[:, at:at + n * C].rearrange("p (n c) -> p n c", n=n), ALU.mult)
                    o = ROW_AT["out"][0] + i * C
                    dve.tensor_tensor(rowg[:, i], src[0:1, 0:B * C].rearrange("p (b c) -> p b c", b=B),
                                      rows[:, o:o + C].unsqueeze(1).broadcast_to([1, B, C]), ALU.mult)\
                       .then_inc(empty, 1)

            dve.wait_ge(s_silu, 1)
            link(dve.tensor_copy(acts[:, 0, :], col("cond", 0, B)))
            dve.tensor_copy(acts_wide.rearrange("p k b n -> p (k b) n"),
                            acts[:, :, :].rearrange("p k b -> p (k b)").unsqueeze(2).broadcast_to([P, 2 * B, P]))\
               .then_inc(s_wide, 1)
            for x in PROLOGUE:
                do(x)
                if x[0] == "ck":
                    c = x[1]
                    dve.wait_ge(emptied_by_scalar.sem, emptied_by_scalar[x])
                    f, r = qkf[:, 1, 0:B * LC], res[:, 1, 0:B * LC]
                    split(f, r, ctx_parts[:, c])
            for x in CHAIN[len(PROLOGUE):]:
                do(x)

        @block.tensor
        def _(pe):
            def turn(to, frm, eye, n):
                return pe.matmul(to, frm, eye[0:n, 0:n], start=True, stop=True, is_transpose=True)

            def head_keys(s, b, h, kt=0):
                rows_ = stack_rows(b)
                return KS[rows_, h, kt * P:(kt + 1) * P] if s in OWN_KEYS else KS[rows_, h, 0:LC]

            def do(x):
                name = x[0]
                if name in NO_BANK:
                    return
                to = free_bank(pe, x)
                if name == "mod":
                    pe.wait_ge(s_ada, 16)
                    pe.wait_ge(s_wide, 1)
                    for i, (layer, *chunks) in enumerate(MODS):
                        for j, chunk in enumerate(chunks):
                            at = ADA_AT[layer][0] + chunk * C
                            n = 2 * i + j
                            ins = pe.matmul(to[:, n * B:(n + 1) * B], ada[:, at:at + C],
                                            acts[:, 0 if layer == 2 else 1, :], start=True, stop=True)
                if name == "hT":
                    pe.wait_ge(normed.sem, normed[("ln",) + x[1:]])
                    if x[1] == UNITS[0]:
                        pe.wait_ge(s_small, 16 * 5)
                    for t in range(T):
                        ins = turn(to[:, t * P:(t + 1) * P], xhat[:, t, :], ident, P)
                if name in ("q", "k", "qs", "ks"):
                    s, b = x[1]
                    if name == "q":
                        pe.wait_ge(emptied_by_scalar.sem, emptied_by_scalar[("hT", x[1], 0)])
                        if x[1] == UNITS[0]:
                            pe.wait_ge(s_w0, 16)
                    layer = LAYER[s]
                    wname = f"{name[0]}{layer}{name[1:]}" if s in OWN_KEYS else f"qc{layer}"
                    ins = pe.matmul(to[:, :], w(wname), hT[:, :], start=True, stop=True)
                if name == "v":
                    s, b = x[1]
                    for t in range(T):
                        ins = pe.matmul(to[:, t * C:(t + 1) * C], hT[:, t * P:(t + 1) * P], w(f"v{LAYER[s]}"),
                                        start=True, stop=True)
                if name == "mx":
                    (s, b), h, t = x[1:]
                    r = stack_rows(b, QK_ROWS)
                    if h + t == 0:
                        stacks_placed(pe, (s, b))
                    if s in FULL:
                        ins = pe.matmul(to[:, :], QS[r, h, t * P:(t + 1) * P], KS[r, h, :], start=True, stop=True)
                    else:
                        n = P if s == WINDOW else LC
                        masked = s in (WINDOW, CROSS2)
                        if s == WINDOW:
                            pe.matmul(to[:, :], identb[:, :], wmask[:, :], start=True, stop=False,
                                      skip_group_check=True)
                        if s == CROSS2:
                            pe.matmul(to[:, 0:T * LC], onesb[0:1, 0:P], cmask[:, b].rearrange("p t k -> p (t k)"),
                                      start=True, stop=False, skip_group_check=True)
                        for i in range(T):
                            keys = KS[r, h, i * P:(i + 1) * P] if s == WINDOW else KS[r, h, 0:LC]
                            ins = pe.matmul(to[:, i * n:(i + 1) * n], QS[r, h, i * P:(i + 1) * P], keys,
                                            start=not masked, stop=True, skip_group_check=masked)
                if name == "tk":
                    (s, b), h = x[1:]
                    r = stack_rows(b, QK_ROWS)
                    if h == 0:
                        stacks_placed(pe, (s, b))
                    for i in range(T):
                        ins = pe.matmul(to[:, i * LC:(i + 1) * LC], QS[r, h, i * P:(i + 1) * P], KS[r, h, 0:LC],
                                        start=True, stop=True)
                if name == "mT":
                    pe.wait_ge(max_parts.sem, max_parts[("m", x[1])])
                    tb = to[:, :].bitcast(BF16)
                    for t in range(T):
                        ins = turn(tb[0:3 * H, t * P:(t + 1) * P], mparts[:, t].rearrange("p a h -> p (a h)"),
                                   identb, P)
                if name == "oT":
                    u, t = x[1:]
                    if t == 0:
                        pe.wait_ge(saved.sem, saved[(UNITS.index(u), G - 1)])
                    for g in range(G):
                        ins = turn(to[:, g * P:(g + 1) * P], OG[:, u[1], g, t * P:(t + 1) * P], ident, P)
                if name == "onT":
                    pe.wait_ge(emptied_by_vector.sem, emptied_by_vector[("oT", x[1], T - 1)])
                    for t in range(T):
                        ins = turn(to[:, t * P:(t + 1) * P], On[:, t, :], ident, P)
                if name == "proj":
                    s, b = x[1]
                    pe.wait_ge(emptied_by_scalar.sem, emptied_by_scalar[("onT", x[1])])
                    i = GATE_OF.get((s, 0))
                    if i is None:
                        matrix = w("cp0" if s == CROSS0 else "p3")
                        at = ROW_AT["cp0" if s == CROSS0 else "p3"][0]
                        bias = rows[:, at:at + C]
                    else:
                        at = RAW_AT[i][0]
                        matrix, bias = Wg[:, b, at:at + C], rowg[:, i, b, :]
                    for t in range(T):
                        pe.matmul(to[:, t * C:(t + 1) * C], OT[:, t * P:(t + 1) * P], matrix, start=True, stop=False)
                        ins = pe.matmul(to[:, t * C:(t + 1) * C], ones[:, :], bias, start=False, stop=True)
                if name in ("ha", "hb"):
                    (s, b), i = x[1:]
                    if name == "ha" and i == 0:
                        pe.wait_ge(emptied_by_scalar.sem, emptied_by_scalar[("hT", x[1], 1)])
                    layer = LAYER[s]
                    wname = f"up{layer}" + (name[1] if layer == 1 else "")
                    ins = pe.matmul(to[:, :], w(wname, i), hT[:, :], start=True, stop=True)
                if name == "down":
                    s, b = x[1]
                    if LAYER[s] == 1:
                        pe.wait_ge(emptied_by_vector.sem, emptied_by_vector[("hb", x[1], NI - 1)])
                    else:
                        pe.wait_ge(emptied_by_scalar.sem, emptied_by_scalar[("ha", x[1], NI - 1)])
                    i = GATE_OF[(s, 1)]
                    at = RAW_AT[i][0]
                    for t in range(T):
                        for n in range(NI):
                            pe.matmul(to[:, t * C:(t + 1) * C], U[:, n, t * P:(t + 1) * P],
                                      Wg[:, b, at + n * C:at + (n + 1) * C], start=n == 0, stop=False)
                        ins = pe.matmul(to[:, t * C:(t + 1) * C], ones[:, :], rowg[:, i, b, :], start=False, stop=True)
                if name == "cT":
                    pe.wait_ge(normed.sem, normed[("ln", "ctx", 1)])
                    for n in range(3):
                        for b in range(B):
                            frm = ctx[:, b, :] if n == 0 else ctx_hat[:, n - 1, b, :]
                            ins = turn(to[:, (n * B + b) * LC:(n * B + b + 1) * LC], frm, ident, LC)
                if name == "ck":
                    c = x[1]
                    if c == 0:
                        pe.wait_ge(emptied_by_vector.sem, emptied_by_vector[("cT",)])
                        pe.wait_ge(s_w, 16)
                    src = ctxT[:, (1, 0, 0, 2)[c]].rearrange("p b k -> p (b k)")
                    ins = pe.matmul(to[:, 0:B * LC], w(f"kc{c}"), src, start=True, stop=True)
                if name == "cv":
                    c = x[1]
                    for b in range(B):
                        ins = pe.matmul(to[0:LC, b * C:(b + 1) * C], ctxT[:, (1, 0, 0, 2)[c], b, :], w(f"vc{c}"),
                                        start=True, stop=True)
                if name == "gate":
                    i = x[1]
                    layer, chunk = GATED[i][:2]
                    if i == 0:
                        pe.wait_ge(s_raw, 16)
                    at = ADA_AT[layer][0] + chunk * C
                    o = ROW_AT["gate"][0] + i * C
                    for b in range(B):
                        pe.matmul(to[:, b * C:(b + 1) * C], acts_wide[:, 0 if layer == 2 else 1, b, :],
                                  ada[:, at:at + C], start=True, stop=False)
                        ins = pe.matmul(to[:, b * C:(b + 1) * C], ones[:, :], rows[:, o:o + C], start=False, stop=True)
                if name == "mask":
                    kt = x[1]
                    pe.wait_ge(s_cmask, 1 + 2 * T)
                    tb = to[:, :].bitcast(BF16)
                    for t in range(T):
                        ins = turn(tb[:, t * P:(t + 1) * P], mask_q[:, t, kt * P:(kt + 1) * P], identb, P)
                ins.then_inc(filled.sem, 1)

            def score(item):
                k, g, half, j = item
                s, b = UNITS[k]
                n = ITEM_NO[item]
                if n >= 2:
                    pe.wait_ge(exped.sem, exped[ITEMS[n - 2]])
                to = scores[n % 2]
                if s != TOPK16 and (g, half, j) == (0, 0, 0):
                    maximum_placed(pe, (s, b))
                    if s == SELF0:
                        pe.wait_ge(s_ones[b], 16)
                r = stack_rows(b)
                for a in range(2):
                    h = g * HG + (j if s in FULL else j + a)
                    out_ = to[:, a * S:(a + 1) * S]
                    if s == SELF0:
                        ins = pe.matmul(out_, head_keys(s, b, h, 2 * half + a), QS[r, h, :], start=True, stop=True)
                    if s == SELF2:
                        pe.matmul(out_, identb[:, :], mask_k[:, 2 * half + a, :], start=True, stop=False)
                        ins = pe.matmul(out_, head_keys(s, b, h, 2 * half + a), QS[r, h, :], start=False, stop=True)
                    if s == WINDOW:
                        pe.matmul(out_, identb[:, :], wmask[:, :], start=True, stop=False, skip_group_check=True)
                        for t in range(T):
                            c = slice(t * P, (t + 1) * P)
                            ins = pe.matmul(out_[:, c], KS[r, h, c], QS[r, h, c], start=False, stop=True,
                                            skip_group_check=True)
                    if s == CROSS2:
                        pe.matmul(out_[0:LC, :], cmask[:, b, 0, :], onesb[0:1, :], start=True, stop=False)
                        ins = pe.matmul(out_[0:LC, :], head_keys(s, b, h), QS[r, h, :], start=False, stop=True)
                    if s in (CROSS0, CROSS3):
                        ins = pe.matmul(out_[0:LC, :], head_keys(s, b, h), QS[r, h, :], start=True, stop=True)
                    if s == TOPK16:
                        pe.wait_ge(top_kept.sem, top_kept[("tk", (s, b), h)])
                        for t in range(T):
                            ins = turn(out_[0:LC, t * P:(t + 1) * P], PQ[:, h, t * LC:(t + 1) * LC], ident, P)
                ins.then_inc(scored.sem, 1)

            def sum_values(batch):
                k, g, half = batch
                s, b = UNITS[k]
                pe.wait_ge(exped.sem, exped[last_item(batch)])
                if half == 0 and (k, g) != (0, 0):
                    at = GROUPS.index((k, g))
                    pe.wait_ge(saved.sem, saved[GROUPS[at - 1]])
                if (k, g, half) == (0, 0, 0):
                    pe.wait_ge(s_vset, 3)
                if s in FULL:
                    for a in range(2):
                        for j in range(HG):
                            h = g * HG + j
                            slot = ITEM_NO[(k, g, half, j)] % RING
                            kt = 2 * half + a
                            ins = pe.matmul(outputs[32 * j:32 * j + VW, :], V1[:, b, kt, h * VW:(h + 1) * VW],
                                            PT[:, slot, a * S:(a + 1) * S], start=kt == 0, stop=kt == T - 1)
                else:
                    for t in (range(T) if s == WINDOW else [0]):
                        for j in range(HG):
                            h = g * HG + j
                            slot = ITEM_NO[(k, g, 0, j // 2 * 2)] % RING
                            a = j % 2
                            if s == WINDOW:
                                c = slice(t * P, (t + 1) * P)
                                ins = pe.matmul(outputs[32 * j:32 * j + VW, c], V1[:, b, t, h * VW:(h + 1) * VW],
                                                PT[:, slot, a * S + t * P:a * S + (t + 1) * P], start=True, stop=True)
                            else:
                                ins = pe.matmul(outputs[32 * j:32 * j + VW, :],
                                                ctx_V[:, CTX_OF[s], b, h * VW:(h + 1) * VW],
                                                PT[0:LC, slot, a * S:(a + 1) * S], start=True, stop=True)
                ins.then_inc(summed.sem, 1)

            pe.wait_ge(s_const, 3)
            for x in PROLOGUE:
                do(x)
            for k in range(len(UNITS)):
                items = items_of(k)
                steps = chain_steps(do, k)
                waiting = batches_of(k)
                for i, item in enumerate(items):
                    score(item)
                    while waiting and i >= items.index(last_item(waiting[0])) + 2:
                        sum_values(waiting.pop(0))
                    beside(steps, k, i)
                for batch in waiting:
                    sum_values(batch)
            for x in pieces_of_post(*UNITS[-1]):
                do(x)


def _layout(i):
    f = lambda a: np.asarray(a)
    L0, L1, L2, L3 = ({k[9:]: f(v) for k, v in i.items() if k.startswith(f"L{n}_xcond_")} for n in range(4))

    def dh(a):
        return a.reshape(a.shape[:-1] + (H, D)).swapaxes(-1, -2).reshape(a.shape)

    def swap(a):
        a = a.reshape(a.shape[:-1] + (H, 2, D // 2))
        return a[..., ::-1, :].reshape(a.shape[:-3] + (C,))

    def cut(a, *n):
        return [a[..., j * C:(j + 1) * C] for j in n]

    def tall(a):
        return a.reshape(NI, P, C).transpose(1, 0, 2).reshape(P, NI * C)

    q0, k0, v0 = cut(L0["W_qkv"], 0, 1, 2)
    kc0, vc0 = cut(L0["W_kvc"], 0, 1)
    q1, k1, v1 = cut(L1["w_qkv"], 0, 1, 2)
    kc1, vc1 = cut(L1["w_kv"], 0, 1)
    q2, k2, v2 = cut(L2["qkv_W"], 0, 1, 2)
    kc3, vc3 = cut(L3["Wkv"], 0, 1)
    weights = {"q0": dh(q0), "k0": dh(k0), "v0": v0, "qc0": dh(L0["W_qc"]), "kc0": dh(kc0), "vc0": vc0,
               "cp0": L0["W_cproj"], "up0": L0["W_mlp1"], "q1": dh(q1), "k1": dh(k1), "v1": v1,
               "qc1": dh(L1["w_q"]), "kc1": dh(kc1), "vc1": vc1, "up1a": L1["w_m1"][:, :HID],
               "up1b": L1["w_m1"][:, HID:], "q2": dh(q2), "k2": dh(k2), "v2": v2, "q2s": dh(swap(q2)),
               "k2s": dh(swap(k2)), "qc2": dh(L2["cq_W"]), "kc2": dh(L2["ck_W"]), "vc2": L2["cv_W"],
               "up2": L2["mlp_W1"], "qc3": dh(L3["Wq"]), "kc3": dh(kc3), "vc3": vc3, "p3": L3["Wp"]}
    w_pack = np.concatenate([weights[n] for n, _ in W_MAIN], 1)
    ada = np.concatenate([L0["W_mod"], L1["w_ada"], L2["adaLN_W"], L3["Wss_q"], L3["Wss_kv"]], 1)
    raw = np.concatenate([L0["W_proj"], tall(L0["W_mlp2"]), L1["w_so"], L1["w_co"], tall(L1["w_m2"]),
                          L2["attn_out_W"], L2["co_W"], tall(L2["mlp_W2"])], 1)
    b_ada = [L0["b_mod"], L1["b_ada"], L2["adaLN_b"], np.concatenate([L3["bss_q"], L3["bss_kv"]])]
    mod_cols = [b_ada[layer][c * C:(c + 1) * C] for layer, *cs in MODS for c in cs]
    bq0, bk0, bv0 = cut(L0["b_qkv"], 0, 1, 2)
    bq1, bk1, bv1 = cut(L1["b_qkv"], 0, 1, 2)
    bkc0, bvc0 = cut(L0["b_kvc"], 0, 1)
    bkc1, bvc1 = cut(L1["b_kv"], 0, 1)
    bkc3, bvc3 = cut(L3["bkv"], 0, 1)
    blocks = lambda a: [a[j * P:(j + 1) * P] for j in range(NI)]
    columns = mod_cols + [L2["norm1_w"], L2["normc_w"], L2["norm2_w"], dh(bq0), dh(bk0), dh(bq1), dh(bk1),
                          dh(L0["b_qc"]), dh(L1["b_q"]), dh(L3["bq"]), dh(bkc0), dh(bkc1), dh(bkc3)] \
        + blocks(L0["b_mlp1"]) + blocks(L1["b_m1"][:HID]) + blocks(L1["b_m1"][HID:]) + blocks(L2["mlp_b1"]) \
        + [f(i["cond_1024"])[j] for j in range(B)]
    vrow = np.concatenate([bv0, bv1, bvc0, bvc1, bvc3])
    zero = np.zeros(C, np.float32)
    row = np.concatenate([b_ada[layer][c * C:(c + 1) * C] for layer, c, _, _ in GATED]
                         + [L0["b_proj"], L0["b_mlp2"], L1["b_so"], L1["b_co"], L1["b_m2"], zero, zero, L2["mlp_b2"]]
                         + [L0["b_cproj"], L3["bp"]])

    eye = np.eye(P, dtype=np.float32)
    a = np.arange(P)
    window = np.where(a[:, None] // WIN == a[None, :] // WIN, 0.0, NEG).astype(np.float32)
    freq = 1.0 / 10000.0 ** (np.arange(0, D, 2, dtype=np.float32) / D)
    angle = np.outer(np.arange(S // 2, dtype=np.float32), freq)
    emb = np.concatenate([angle, angle], -1)
    table = np.stack([np.cos(emb), np.sin(emb) * np.where(np.arange(D) < D // 2, -1.0, 1.0)]).astype(np.float32)
    table = np.tile(table.transpose(2, 0, 1)[:, None], (1, H, 1, 2)).reshape(P, 2, S)
    return {
        "x": f(i["x"]), "ctx": f(i["ctx_1024"]),
        "cmask": f(i["mask_BxS2_bf1"]).reshape(1, B * LC),
        "smask": f(i["mask_SxS_bk0"]),
        "w": w_pack, "ada": ada, "raw": raw, "col": np.stack(columns, 1), "vrow": vrow, "row": row[None],
        "ident": eye, "wmask": window,
        "rope": table,
    }


def kernel(**inputs):
    import concourse.bacc as bacc
    from concourse.bass_utils import run_bass_kernel_spmd

    nc = bacc.Bacc("TRN2", target_bir_lowering=False, num_devices=1)
    arrays, args = {}, []
    for name, a in _layout(inputs).items():
        a = np.ascontiguousarray(a)
        arrays[f"in_{name}"] = a
        args.append(nc.dram_tensor(f"in_{name}", a.shape, mybir.dt.from_np(a.dtype), kind="ExternalInput").ap())
    args.append(nc.dram_tensor("out_0", (B, S, C), F32, kind="ExternalOutput").ap())
    pixart_four_layers(nc, *args)
    r = run_bass_kernel_spmd(nc, [arrays], core_ids=[0])
    return r.results[0]["out_0"]
```

```python
from contextlib import ExitStack

import concourse.bass as bass
import concourse.mybir as mybir
import numpy as np

ALU = mybir.AluOpType
ACT = mybir.ActivationFunctionType
AX = mybir.AxisListType.X
F32 = mybir.dt.float32
BF16 = mybir.dt.bfloat16
U8 = mybir.dt.uint8

P = 128
B, S, C = 2, 512, 128
T = S // P
H, D = 16, 8
LC = 77
HID = 512
NI = HID // P
WIN, SHIFT = 64, 32
TOPK = 16
SCALE = float(D) ** -0.5
NEG = -3.3895313892515355e38
G, HG = 4, 4
VW = D + 1

SELF0, CROSS0, WINDOW, TOPK16, SELF2, CROSS2, CROSS3 = range(7)
NSTAGE = 7
LAYER = [0, 0, 1, 1, 2, 2, 3]
OWN_KEYS = (SELF0, WINDOW, SELF2)
FULL = (SELF0, SELF2)
CTX_OF = {CROSS0: 0, TOPK16: 1, CROSS2: 2, CROSS3: 3}
MLP_AFTER = (CROSS0, TOPK16, CROSS2)
LN_EPS = [1e-6, 1e-6, 1e-5, 1e-5]

Q_PART = [0, 0, 1, 1, 0, 2]
K_PART = [0, 1, 0, 1, 2, 0]
H2 = H // 2
QK_ROWS = 2 * len(Q_PART) * D
ROWS = QK_ROWS + 2 * 3
LCP = 96

MODS = [(0, 0, 1), (0, 3, 4), (1, 0, 1), (1, 3, 4), (1, 6, 7), (2, 0, 1), (2, 3, 4), (2, 6, 7),
        (3, 1, 0), (3, 3, 2)]
MOD_OF = {(SELF0, 0): 0, (CROSS0, 1): 1, (WINDOW, 0): 2, (TOPK16, 0): 3, (TOPK16, 1): 4, (SELF2, 0): 5,
          (CROSS2, 0): 6, (CROSS2, 1): 7, (CROSS3, 0): 8}
MOD_KV3 = 9
GATED = [(0, 2, 1, "proj0"), (0, 5, NI, "down0"), (1, 2, 1, "so"), (1, 5, 1, "co"), (1, 8, NI, "down1"),
         (2, 2, 1, "ao"), (2, 5, 1, "co2"), (2, 8, NI, "down2")]
GATE_OF = {(SELF0, 0): 0, (CROSS0, 1): 1, (WINDOW, 0): 2, (TOPK16, 0): 3, (TOPK16, 1): 4, (SELF2, 0): 5,
           (CROSS2, 0): 6, (CROSS2, 1): 7}

def offsets(parts):
    at, out = 0, {}
    for name, n in parts:
        out[name] = (at, n)
        at += n
    return out, at


W_MAIN = [("q0", C), ("k0", C), ("v0", C), ("qc0", C), ("cp0", C), ("up0", HID),
          ("q1", C), ("k1", C), ("v1", C), ("qc1", C), ("up1a", HID), ("up1b", HID),
          ("q2", C), ("k2", C), ("v2", C), ("q2s", C), ("k2s", C), ("qc2", C),
          ("up2", HID), ("qc3", C), ("p3", C)]
W_AT, W_COLS = offsets(W_MAIN)
W_FIRST = W_AT["qc0"][0]
W_CTX = [(f"{n}{c}", C) for c in range(4) for n in ("kc", "vc")]
CTX_AT, CTX_COLS = offsets(W_CTX)
ADA_AT, ADA_COLS = offsets([(0, 6 * C), (1, 9 * C), (2, 9 * C), (3, 4 * C)])
RAW_AT, RAW_COLS = offsets([(i, n * C) for i, (_, _, n, _) in enumerate(GATED)])
COL_AT, COLS = offsets([("mod", 2 * len(MODS)), ("norm", 3), ("q0", 1), ("k0", 1), ("q1", 1), ("k1", 1),
                        ("qc0", 1), ("qc1", 1), ("qc3", 1), ("kc0", 1), ("kc1", 1), ("kc3", 1), ("up0", NI),
                        ("up1a", NI), ("up1b", NI), ("up2", NI), ("cond", B)])
VROW_AT, VROWS = offsets([("v0", C), ("v1", C), ("cp0", C), ("p3", C), ("vc0", C), ("vc1", C), ("vc3", C)])
BIASED = [0, 1, 2, 3, 4, 7]
ROW_AT, ROWCOLS = offsets([("gate", len(GATED) * C), ("out", len(BIASED) * C)])

UNITS = [(s, b) for s in range(NSTAGE) for b in range(B)]


def prep(s, b):
    u = (s, b)
    out = [(("kc", u), 0.1)] if s in CTX_OF else []
    out += [(("ln", u, 0), 3.5), (("hT", u, 0), 1.5)]
    names = {SELF2: ("k", "ks", "q", "qs", "v"), SELF0: ("k", "q", "v"), WINDOW: ("k", "q", "v")}.get(s, ("q",))
    out += [((n, u), 1.0) for n in names] + [(("stack", u), 12.0)]
    if s in FULL:
        out += [(("mx", u, h, t), 0.6) for h in range(H) for t in range(T)]
    elif s != TOPK16:
        out += [(("mx", u, h, 0), 0.6) for h in range(H)]
    if s != TOPK16:
        out += [(("m", u), 2.0), (("mT", u), 3.5)]
    return out


def probabilities_of(s, b):
    u = (s, b)
    items = [("ex", u, g, kt, j) for g in range(G) for kt in range(T if s in FULL else 1) for j in range(HG)]
    out = []
    for n, x in enumerate(items):
        if s == TOPK16:
            out.append((("tk", u, n), 2.9))
            if n >= TK_LAG:
                out.append((items[n - TK_LAG], 0.1))
        else:
            out.append((x, 0.6))
        done = n - PV_LAG - (TK_LAG if s == TOPK16 else 0)
        if done >= 0 and items[done][4] == HG - 1:
            out += sums(items[done])
    if s == TOPK16:
        out.append((("tkend", u), 0.5))
        out += [(x, 0.6) for x in items[-TK_LAG:]]
    return out + sums(items[-1])


def sums(item):
    _, u, g, kt, _ = item
    out = [(("pv", u, g, kt), 0.1)]
    return out + [(("save", u, g), 0.1)] if kt == (T - 1 if u[0] in FULL else 0) else out


def post(s, b):
    u = (s, b)
    out = [(("oT", u, t), 1.2) for t in range(T)] + [(("onT", u), 1.5), (("proj", u), 2.0)]
    if s in MLP_AFTER:
        out += [(("ln", u, 1), 3.5), (("hT", u, 1), 1.5)]
        out += [((n, u, i), 0.8) for i in range(NI) for n in (("ha", "hb") if LAYER[s] == 1 else ("ha",))]
        out.append((("down", u), 3.5))
    if s == NSTAGE - 1:
        out.append((("out", u), 0))
    return out


PV_LAG = 2
TK_LAG = 2
B_LAG = 45.0

PROLOGUE = [("mod",)]
EARLY = [("cT",)] + [("ck", c) for c in range(4)] + [("cv", c) for c in range(4)] \
    + [("gate", i) for i in range(len(GATED))] + [("mask", t) for t in range(T)]


def program():
    timed = []
    for b in range(B):
        at = b * B_LAG
        for s in range(NSTAGE):
            for x, cost in prep(s, b) + probabilities_of(s, b) + post(s, b):
                timed.append((at, b, len(timed), x))
                at += cost
    merged = [x for _, _, _, x in sorted(timed)]
    first = merged.index(("stack", UNITS[0])) + 1
    last = merged.index(("m", UNITS[0]))
    gap = (last - first) // (len(EARLY) + 1)
    for n, x in enumerate(EARLY):
        merged.insert(first + n * (gap + 1), x)
    return PROLOGUE + merged


CHAIN = program()
NO_BANK = ("ln", "stack", "kc", "m", "tkend", "out", "ex", "pv", "save")


def reader(x):
    if x[0] in ("q", "k"):
        return "V" if x[1][0] == SELF2 else "S"
    return "S" if x[0] in ("hT", "ck", "mask", "mT", "tk", "onT", "ha") else "V"


BANKED = [x for x in CHAIN if x[0] not in NO_BANK]
BANKS = 3
BANK_NO = {x: n for n, x in enumerate(BANKED)}
ITEMS = [x for x in CHAIN if x[0] == "ex"]
ITEM_NO = {x: n for n, x in enumerate(ITEMS)}
OWN_ITEMS = [[x for x in ITEMS if x[1][1] == b] for b in range(B)]
OWN_NO = {x: n for own in OWN_ITEMS for n, x in enumerate(own)}
SAVES = [[x for x in CHAIN if x[0] == "save" and x[1][1] == b] for b in range(B)]
SCORES = 3
RING = 6


KEEPS = [("tk", x[1], x[2] - 1 if x[0] == "tk" else H - 1) for x in CHAIN
         if x[0] == "tkend" or (x[0] == "tk" and x[2])]


def bias_row(u, which):
    s = u[0]
    i = GATE_OF.get((s, which))
    if i is None:
        return "cp0" if s == CROSS0 else "p3"
    return i if i in BIASED else None


class Count:

    def __init__(self, sem, events):
        self.sem = sem
        self.after = {e: i + 1 for i, e in enumerate(events)}

    def __getitem__(self, event):
        return self.after[event]


def pixart_four_layers(nc, x_in, ctx_in, cmask_in, smask_in, w_in, wc_in, ada_in, raw_in, col_in, vrow_in,
                       row_in, ident_in, wmask_in, rope_in, out):
    with ExitStack() as stack:
        def sb(name, shape, dt=F32):
            return stack.enter_context(nc.sbuf_tensor(name, shape, dt))

        def sem(name):
            return stack.enter_context(nc.semaphore(name))

        X = sb("X", [P, B * T, C])
        ctx = sb("ctx", [LC, B, C])
        W = sb("W", [P, W_COLS])
        cols = sb("cols", [P, COLS])
        vrows = sb("vrows", [P, VROWS])
        ident = sb("ident", [P, P])
        identb = sb("identb", [P, P], BF16)
        wmask = sb("wmask", [P, P], BF16)
        rope = sb("rope", [P, 2, S // 2])
        first_row = sb("first_row", [P, S], BF16)
        onesb = sb("onesb", [3, S], BF16)
        half_neg = sb("half_neg", [P, T])
        acts = sb("acts", [P, 2, B])
        M = sb("M", [P, len(MODS), 2, B])
        Wg = sb("Wg", [P, B, RAW_COLS])
        rowg = sb("rowg", [P, len(BIASED), B, C])
        mask_q = sb("mask_q", [P, T, S], BF16)
        mask_k = sb("mask_k", [P, T, S], BF16)
        cmask_u8 = sb("cmask_u8", [1, B * LC], U8)
        cmask = sb("cmask", [P, B, LCP], BF16)
        ctx_parts = sb("ctx_parts", [P, 4, 3, B * LC], BF16)
        ctx_V = sb("ctx_V", [LCP, 4, B, H * VW])
        QS = sb("QS", [P, B, H2, S], BF16)
        KS = sb("KS", [P, B, H, S], BF16)
        KC = sb("KC", [P, B, H, LCP], BF16)
        V1 = sb("V1", [P, B, T, H * VW])
        PT = sb("PT", [P, B, RING, S])
        PQ = sb("PQ", [P, B, 4, T * LC])
        stats = sb("stats", [P, B, T, 6])
        mv = sb("mv", [P, B, T, 2])
        veps = sb("veps", [P, B, T])
        rstd = sb("rstd", [P, B, T])
        xhat = sb("xhat", [P, B, T, C])
        hT = sb("hT", [P, B, S])
        mmax = sb("mmax", [P, B, T, H])
        mres = sb("mres", [P, B, T, H])
        mparts = sb("mparts", [P, B, T, 2, 3, H2], BF16)
        mT = sb("mT", [3 * H, B, S], BF16)
        junk = sb("junk", [P, S], BF16)
        top = sb("top", [P, B, 2, T, 16])
        nbias = sb("nbias", [P, B, 2, T])
        left = sb("left", [P, B, 2, T, LC])
        rsum = sb("rsum", [P, B, T, H])
        ctx_mv = sb("ctx_mv", [LC, B, 2])
        ctx_stats = sb("ctx_stats", [LC, B, 6])
        ctx_veps = sb("ctx_veps", [LC, 2, B])
        ctx_rstd = sb("ctx_rstd", [LC, 2, B])
        work = sb("work", [P, B, 5, S])
        U = work[:, :, 0:NI, :]
        OG = work[:, :, 0:G, :]
        qkf = work[:, :, 0:2, :]
        parts = work[:, :, 2:5, :].rearrange("p b i s -> p b (i s)").bitcast(BF16)\
            .rearrange("p b (i n s) -> p b i n s", i=2, n=3)
        flat = xhat[:, :, :, :].rearrange("p b t c -> p b (t c)")
        res = flat
        gated = (work[:, :, NI, :], flat)
        On, OT = xhat, hT

        early, at = PT[:, :, :, :].rearrange("p b r n -> p (b r n)"), 0

        def cut(n):
            nonlocal at
            at += n
            return early[:, at - n:at]

        ada = cut(ADA_COLS)
        Wc = cut(CTX_COLS)
        ctxT = cut(3 * B * LC).rearrange("p (n b k) -> p n b k", n=3, b=B)
        ctx_hat = cut(2 * B * C)[0:LC].rearrange("p (n b c) -> p n b c", n=2, b=B)
        acts_wide = cut(2 * B * P).rearrange("p (k b n) -> p k b n", k=2, b=B)
        early, at = PQ[:, :, :, :].rearrange("p b a n -> p (b a n)"), 0
        rows = cut(ROWCOLS)
        wmask32 = cut(P)
        gate_row = cut(2 * B * C).rearrange("p (i b c) -> p i b c", i=2, b=B)
        raw = Wg[:, 0, :]
        mask_u8 = mask_k[:, :, :].rearrange("p t s -> p (t s)").bitcast(U8)[:, 0:T * S]
        ctx_k = junk[:, :].bitcast(F32)[:, 0:B * LC]

        scores = [stack.enter_context(nc.psum_tensor(f"scores{i}", [P, S], F32)) for i in range(SCORES)]
        outputs = [stack.enter_context(nc.psum_tensor(f"outputs{b}", [P, S], F32)) for b in range(B)]
        banks = [stack.enter_context(nc.psum_tensor(f"bank{i}", [P, S], F32)) for i in range(BANKS)]

        s_small = sem("small_inputs_loaded")
        s_ada = sem("ada_loaded")
        s_x = sem("x_loaded")
        s_w0 = sem("first_weights_loaded")
        s_ctx = sem("context_loaded")
        s_vrows = sem("value_biases_loaded")
        s_wc = sem("context_weights_loaded")
        s_w = sem("weights_loaded")
        s_raw = sem("raw_weights_loaded")
        s_late = sem("late_inputs_loaded")
        s_const = sem("constants_set")
        s_vset = sem("vector_constants_set")
        s_silu = sem("silu_done")
        s_wide = sem("conditioning_widened")
        s_cmask = sem("masks_made")
        s_vchain = sem("vector_step_done")
        s_pchain = sem("pool_step_done")
        s_zero = sem("key_stack_zeroed")
        s_czero = sem("context_stacks_zeroed")
        s_ones = [sem(f"ones_rows_placed{b}") for b in range(B)]
        s_qs = [sem(f"query_stack_placed{b}") for b in range(B)]
        s_ks = [sem(f"key_stack_placed{b}") for b in range(B)]
        s_ms = [sem(f"maximum_stack_placed{b}") for b in range(B)]
        s_out = sem("output_stored")

        filled = Count(sem("chain_bank_filled"), BANKED)
        emptied_by_vector = Count(sem("bank_emptied_by_vector"), [x for x in BANKED if reader(x) == "V"])
        emptied_by_scalar = Count(sem("bank_emptied_by_scalar"), [x for x in BANKED if reader(x) == "S"])
        lns = [x for x in CHAIN if x[0] == "ln"]
        ctx_at = len([x for x in CHAIN[:CHAIN.index(("cT",))] if x[0] == "ln"])
        lns[ctx_at:ctx_at] = [("ln", "ctx", 0), ("ln", "ctx", 1)]
        variance = Count(sem("variance_ready"), lns)
        rstd_ready = Count(sem("rstd_ready"), lns)
        normed = Count(sem("normed"), lns)
        firsts = [x for x in CHAIN if x[0] in ("q", "k", "ck") and reader(x) == "S"]
        first_part = Count(sem("first_part_made"), firsts)
        stacks = [x for x in CHAIN if x[0] == "stack"]
        rope_q = Count(sem("roped"), [x for x in CHAIN if x[0] in ("qs", "ks")])
        split_q = Count(sem("query_parts_made"), stacks)
        split_k = Count(sem("key_parts_made"), [x for x in stacks if x[1][0] in OWN_KEYS])
        split_c = Count(sem("context_key_parts_made"), [x for x in CHAIN if x[0] == "ck"])
        biased = Count(sem("output_bias_added"), [(x[1], w) for x in CHAIN for w in range(2)
                                                  if x[0] == "onT" and not w or x[0] == "ha" and w and not x[2]
                                                  if bias_row(x[1], w) is not None])
        max_parts = Count(sem("maximum_parts_made"), [x for x in CHAIN if x[0] == "m"])
        top_found = Count(sem("top16_found"), [x for x in CHAIN if x[0] == "tk"])
        top_kept = Count(sem("top16_kept"), KEEPS)
        scored = Count(sem("scores_ready"), ITEMS)
        exped = Count(sem("probabilities_ready"), ITEMS)
        summed = Count(sem("values_summed"), [x for x in CHAIN if x[0] == "pv"])
        saved = Count(sem("outputs_saved"), [x for x in CHAIN if x[0] == "save"])

        def bank(x):
            return banks[BANK_NO[x] % BANKS]

        def free_bank(pe, x):
            n = BANK_NO[x]
            if n >= BANKS:
                last = BANKED[n - BANKS]
                if reader(last) == "V":
                    pe.wait_ge(emptied_by_vector.sem, emptied_by_vector[last])
                else:
                    pe.wait_ge(emptied_by_scalar.sem, emptied_by_scalar[last])
            return banks[n % BANKS]

        def w(name, i=0, n=C):
            at = W_AT[name][0] + i * n
            return W[:, at:at + n]

        def wc(name):
            return Wc[:, CTX_AT[name][0]:CTX_AT[name][0] + C]

        def col(name, i=0, n=1):
            at = COL_AT[name][0] + i
            return cols[:, at:at + n]

        def heads(ap):
            return ap.rearrange("p (h v) -> p h v", v=VW)

        block = stack.enter_context(nc.Block())

        @block.sync
        def _(sp):
            sp.dma_start(cols[:, :], col_in).then_inc(s_small, 16)
            sp.dma_start(ident[:, :], ident_in).then_inc(s_small, 16)
            sp.dma_start(X[:, :, :], x_in.rearrange("b (t p) c -> p (b t) c", p=P)).then_inc(s_x, 16)
            sp.dma_start(ada, ada_in).then_inc(s_ada, 16)
            sp.dma_start(W[:, 0:W_FIRST], w_in[:, 0:W_FIRST]).then_inc(s_w0, 16)
            sp.dma_start(ctx[:, :, :], ctx_in.rearrange("b t c -> t b c")).then_inc(s_ctx, 16)
            sp.dma_start(vrows[:, :], vrow_in.partition_broadcast(P)).then_inc(s_vrows, 16)
            sp.wait_ge(s_const, 1)
            sp.wait_ge(s_czero, 1)
            for b in range(B):
                sp.wait_ge(s_zero, b + 1)
                for half in range(2):
                    r = QK_ROWS + 3 * half
                    sp.dma_start(KS[r:r + 3, b, half * H2:(half + 1) * H2, :],
                                 onesb[:, :].unsqueeze(1).broadcast_to([3, H2, S])).then_inc(s_ones[b], 16)
                    sp.dma_start(KC[r:r + 3, b, half * H2:(half + 1) * H2, 0:LC],
                                 onesb[:, 0:LC].unsqueeze(1).broadcast_to([3, H2, LC])).then_inc(s_ones[b], 16)
            sp.dma_start(Wc, wc_in).then_inc(s_wc, 16)
            sp.dma_start(raw, raw_in).then_inc(s_raw, 16)
            sp.dma_start(rows, row_in.partition_broadcast(P)).then_inc(s_raw, 16)
            sp.dma_start(mask_u8.rearrange("p (t s) -> p t s", t=T),
                         smask_in.rearrange("(t p) s -> p t s", p=P)).then_inc(s_late, 16)
            sp.dma_start(cmask_u8[:, :], cmask_in).then_inc(s_late, 16)
            sp.dma_start(wmask32, wmask_in).then_inc(s_late, 16)
            sp.dma_start(rope[:, :, :], rope_in).then_inc(s_late, 16)
            sp.dma_start(W[:, W_FIRST:], w_in[:, W_FIRST:]).then_inc(s_w, 16)

            def do(x):
                if x[0] == "kc":
                    s, b = x[1]
                    c = CTX_OF[s]
                    sp.wait_ge(split_c.sem, split_c[("ck", c)])
                    before = [u for u in UNITS[:UNITS.index((s, b))] if u[1] == b and u[0] in CTX_OF]
                    if before:
                        last = [y for y in ITEMS if y[1] == before[-1]][-1]
                        sp.wait_ge(scored.sem, scored[last])
                    for i, kp in enumerate(K_PART):
                        for half in range(2):
                            r = 2 * D * i + D * half
                            sp.dma_start(KC[r:r + D, b, half * H2:(half + 1) * H2, 0:LC],
                                         ctx_parts[64 * half:64 * half + 64, c, kp, b * LC:(b + 1) * LC])\
                              .then_inc(s_ks[b], 16)
                if x[0] == "stack":
                    s, b = x[1]
                    if s in OWN_KEYS:
                        sp.wait_ge(split_k.sem, split_k[x])
                        for i, kp in enumerate(K_PART):
                            for half in range(2):
                                r = 2 * D * i + D * half
                                sp.dma_start(KS[r:r + D, b, half * H2:(half + 1) * H2, :],
                                             parts[64 * half:64 * half + 64, b, 1, kp, :]).then_inc(s_ks[b], 16)
                    sp.wait_ge(split_q.sem, split_q[x])
                    for i, qp in enumerate(Q_PART):
                        sp.dma_start(QS[2 * D * i:2 * D * (i + 1), b, :, :], parts[:, b, 0, qp, :])\
                          .then_inc(s_qs[b], 16)
                if x[0] == "mT":
                    b = x[1][1]
                    sp.wait_ge(emptied_by_scalar.sem, emptied_by_scalar[x])
                    sp.dma_start(QS[QK_ROWS:ROWS, b, :, :], mT[:, b, :]).then_inc(s_ms[b], 16)
                if x[0] == "out":
                    b = x[1][1]
                    sp.wait_ge(emptied_by_vector.sem, emptied_by_vector[("proj", x[1])])
                    sp.dma_start(out.rearrange("b (t p) c -> p (b t) c", p=P)[:, b * T:(b + 1) * T, :],
                                 X[:, b * T:(b + 1) * T, :]).then_inc(s_out, 16)

            for x in CHAIN:
                do(x)
            sp.wait_ge(s_out, 16 * B)

        def key_moves(u):
            return 16 * 12 * (u[0] + 1)

        def query_moves(u):
            return 16 * 6 * (u[0] + 1)

        def max_moves(u):
            return 16 * (u[0] + 1 - (u[0] > TOPK16))

        @block.gpsimd
        def _(pool):
            chain = [0]

            def link(ins):
                chain[0] += 1
                ins.then_inc(s_pchain, 1)
                pool.wait_ge(s_pchain, chain[0])

            pool.memset(onesb[:, :], 1.0).then_inc(s_const, 1)
            pool.memset(KC[:, :, :, :], 0.0).then_inc(s_czero, 1)
            link(pool.memset(half_neg[:, :], -0.5))
            link(pool.memset(first_row[:, :], 0.0))
            pool.memset(first_row[0:1, :], 1.0).then_inc(s_const, 1)
            link(pool.memset(cmask[:, :, :], 0.0))
            pool.wait_ge(s_small, 32)
            pool.tensor_copy(identb[:, :], ident[:, :]).then_inc(s_const, 1)

            def do(x):
                if x[0] == "ln":
                    (s, b), which = x[1:]
                    pool.wait_ge(variance.sem, variance[x])
                    pool.tensor_tensor(rstd[:, b, :], veps[:, b, :], half_neg[:, :], ALU.pow)\
                        .then_inc(rstd_ready.sem, 1)
                if x[0] == "onT" or (x[0] == "ha" and x[2] == 0):
                    (s, b), which = x[1], int(x[0] == "ha")
                    row = bias_row(x[1], which)
                    if row is not None:
                        if x == ("onT", (CROSS0, 0)):
                            pool.wait_ge(s_vrows, 16)
                        if row in ("cp0", "p3"):
                            at = VROW_AT[row][0]
                            row = vrows[:, at:at + C]
                        else:
                            row = rowg[:, BIASED.index(row), b, :]
                        pool.wait_ge(normed.sem, normed[("ln", (s, b), which)])
                        xs = X[:, b * T:(b + 1) * T, :]
                        pool.tensor_tensor(xs, xs, row.unsqueeze(1).broadcast_to([P, T, C]), ALU.add)\
                            .then_inc(biased.sem, 1)
                if x[0] == "stack" and x[1][0] in OWN_KEYS:
                    s, b = x[1]
                    f, p = qkf[:, b, 1, :], parts[:, b, 1]
                    if s == SELF2:
                        pool.wait_ge(rope_q.sem, rope_q[("ks", x[1])])
                        link(pool.tensor_copy(p[:, 0, :], f))
                    else:
                        pool.wait_ge(emptied_by_scalar.sem, emptied_by_scalar[("k", x[1])])
                    link(pool.tensor_tensor(f, f, p[:, 0, :], ALU.subtract))
                    link(pool.tensor_copy(p[:, 1, :], f))
                    pool.tensor_tensor(p[:, 2, :], f, p[:, 1, :], ALU.subtract).then_inc(split_k.sem, 1)
                if x[0] == "cT":
                    for n in range(2):
                        pool.wait_ge(variance.sem, variance[("ln", "ctx", n)])
                        pool.tensor_tensor(ctx_rstd[:, n, :], ctx_veps[:, n, :], half_neg[0:LC, 0:B], ALU.pow)\
                            .then_inc(rstd_ready.sem, 1)
                    pool.wait_ge(s_late, 64)
                    pool.tensor_copy(wmask[:, :], wmask32).then_inc(s_cmask, 1)
                    pool.tensor_scalar(mask_q[:, :, :], mask_u8.rearrange("p (t s) -> p t s", t=T), -1.0, -NEG,
                                       ALU.add, ALU.mult).then_inc(s_cmask, 1)
                    pool.tensor_scalar(cmask[0:1, :, 0:LC], cmask_u8.rearrange("p (b k) -> p b k", b=B),
                                       -1.0, -NEG, ALU.add, ALU.mult).then_inc(s_cmask, 1)

            for x in CHAIN:
                do(x)

        @block.scalar
        def _(act):
            act.wait_ge(s_small, 32)
            act.activation(acts[:, 1, :], col("cond", 0, B), ACT.Silu).then_inc(s_silu, 1)

            def two_parts(src, f, part, bias):
                for to, done in ((part, first_part), (f, emptied_by_scalar)):
                    if bias is None:
                        act.activation(to, src, ACT.Copy).then_inc(done.sem, 1)
                    else:
                        act.activation(to, src, ACT.Identity, bias=bias).then_inc(done.sem, 1)

            def exponentials(x):
                n, (s, b) = ITEM_NO[x], x[1]
                own = OWN_NO[x]
                keys = P if s in OWN_KEYS else LC if s == TOPK16 else LCP
                if own >= RING:
                    last = OWN_ITEMS[b][own - RING]
                    act.wait_ge(summed.sem, summed[("pv",) + last[1:4]])
                elif own == 0:
                    act.wait_ge(emptied_by_vector.sem, emptied_by_vector[("gate", len(GATED) - 1)])
                act.wait_ge(scored.sem, scored[x])
                to = PT[0:keys, b, own % RING, :]
                if s == TOPK16:
                    act.activation(to, scores[n % SCORES][0:keys, :], ACT.Copy).then_inc(exped.sem, 1)
                else:
                    act.activation(to, scores[n % SCORES][0:keys, :], ACT.Exp, scale=SCALE).then_inc(exped.sem, 1)

            def do(x):
                if x[0] == "ex":
                    exponentials(x)
                if x[0] == "save":
                    (s, b), g = x[1:]
                    act.wait_ge(summed.sem, summed[("pv", x[1], g, T - 1 if s in FULL else 0)])
                    if s and g == 0:
                        act.wait_ge(filled.sem, filled[("oT", (s - 1, b), T - 1)])
                    act.copy(OG[:, b, g, :], outputs[b][:, :]).then_inc(saved.sem, 1)
                if x[0] in NO_BANK or reader(x) != "S":
                    return
                empty = emptied_by_scalar.sem
                act.wait_ge(filled.sem, filled[x])
                src = bank(x)
                if x[0] == "hT":
                    (s, b), which = x[1:]
                    mod = MOD_OF.get((s, which))
                    runs = [(0, 0, S)]
                    if s == WINDOW:
                        runs = [(0, SHIFT, S - SHIFT), (S - SHIFT, 0, SHIFT)]
                    for to, at, n in runs:
                        if mod is None:
                            ins = act.activation(hT[:, b, to:to + n], src[:, at:at + n], ACT.Copy)
                        else:
                            ins = act.activation(hT[:, b, to:to + n], src[:, at:at + n], ACT.Identity,
                                                 bias=M[:, mod, 0, b:b + 1], scale=M[:, mod, 1, b:b + 1])
                    ins.then_inc(empty, 1)
                if x[0] in ("q", "k"):
                    s, b = x[1]
                    i = "qk".index(x[0])
                    name = f"{x[0]}{LAYER[s]}" if s in OWN_KEYS else f"qc{LAYER[s]}"
                    two_parts(src[:, :], qkf[:, b, i, :], parts[:, b, i, 0, :], None if s == CROSS2 else col(name))
                if x[0] == "ck":
                    c = x[1]
                    if c:
                        act.wait_ge(split_c.sem, split_c[("ck", c - 1)])
                    two_parts(src[:, 0:B * LC], ctx_k, ctx_parts[:, c, 0, :],
                              None if c == 2 else col(f"kc{c}"))
                if x[0] == "mask":
                    act.copy(mask_k[:, x[1], :], src[:, :].bitcast(BF16)[:, 0:S]).then_inc(empty, 1)
                if x[0] == "mT":
                    act.copy(mT[:, x[1][1], :], src[0:3 * H, :].bitcast(BF16)[:, 0:S]).then_inc(empty, 1)
                if x[0] == "tk":
                    (s, b), h = x[1:]
                    act.wait_ge(top_found.sem, top_found[x])
                    if h >= 4:
                        last = ("ex", x[1], (h - 4) // HG, 0, h % HG)
                        act.wait_ge(scored.sem, scored[last])
                    for t in range(T):
                        ins = act.activation(PQ[:, b, h % 4, t * LC:(t + 1) * LC], src[:, t * LC:(t + 1) * LC],
                                             ACT.Exp, bias=nbias[:, b, h % 2, t:t + 1], scale=SCALE)
                    ins.then_inc(empty, 1)
                if x[0] == "onT":
                    s, b = x[1]
                    if s == WINDOW:
                        act.copy(OT[:, b, SHIFT:S], src[:, 0:S - SHIFT])
                        act.copy(OT[:, b, 0:SHIFT], src[:, S - SHIFT:S]).then_inc(empty, 1)
                    else:
                        act.copy(OT[:, b, :], src[:, :]).then_inc(empty, 1)
                if x[0] == "ha":
                    (s, b), i = x[1:]
                    if LAYER[s] == 1:
                        if i >= 2:
                            act.wait_ge(emptied_by_vector.sem, emptied_by_vector[("hb", x[1], i - 2)])
                        act.activation(gated[i % 2][:, b, :], src[:, :], ACT.Silu, bias=col("up1a", i))\
                           .then_inc(empty, 1)
                    else:
                        act.activation(U[:, b, i, :], src[:, :], ACT.Gelu_apprx_tanh,
                                       bias=col(f"up{LAYER[s]}", i)).then_inc(empty, 1)

            for x in CHAIN:
                do(x)

        @block.vector
        def _(dve):
            chain = [0]

            def link(ins):
                chain[0] += 1
                ins.then_inc(s_vchain, 1)
                dve.wait_ge(s_vchain, chain[0])

            for b in range(B):
                dve.memset(KS[:, b, :, :], 0.0).then_inc(s_zero, 1)
            dve.wait_ge(s_silu, 1)
            link(dve.tensor_copy(acts[:, 0, :], col("cond", 0, B)))
            dve.tensor_copy(acts_wide.rearrange("p k b n -> p (k b) n"),
                            acts[:, :, :].rearrange("p k b -> p (k b)").unsqueeze(2).broadcast_to([P, 2 * B, P]))\
               .then_inc(s_wide, 1)

            def norm(src, tiles, n, eps, stat, mean, v, r, to, x):
                for t in range(tiles):
                    chain[0] += 1
                    dve.bn_stats(stat[0:n, t, :], src(t)).then_inc(s_vchain, 1)
                dve.wait_ge(s_vchain, chain[0])
                for t in range(tiles):
                    chain[0] += 1
                    dve.bn_aggr(mean[0:n, t, :], stat[0:n, t, :]).then_inc(s_vchain, 1)
                dve.wait_ge(s_vchain, chain[0])
                dve.tensor_scalar(v, mean[0:n, 0:tiles, 1], eps, None, ALU.add).then_inc(variance.sem, 1)
                dve.wait_ge(rstd_ready.sem, rstd_ready[x])
                for t in range(tiles):
                    ins = dve.tensor_scalar(to(t), src(t), mean[0:n, t, 0:1], r[:, t:t + 1], ALU.subtract, ALU.mult)
                ins.then_inc(normed.sem, 1)

            def split(f, p, done):
                link(dve.tensor_tensor(f, f, p[:, 0], ALU.subtract))
                link(dve.tensor_copy(p[:, 1], f))
                dve.tensor_tensor(p[:, 2], f, p[:, 1], ALU.subtract).then_inc(done.sem, 1)

            def keep_top(u, h):
                b = u[1]
                dve.wait_ge(emptied_by_scalar.sem, emptied_by_scalar[("tk", u, h)])
                dve.scalar_tensor_tensor(out=PQ[:, b, h % 4, :], in0=left[:, b, h % 2].rearrange("p t k -> p (t k)"),
                                         scalar=NEG, in1=PQ[:, b, h % 4, :], op0=ALU.is_le, op1=ALU.mult)\
                   .then_inc(top_kept.sem, 1)

            def do(x):
                name = x[0]
                empty = emptied_by_vector.sem
                if name == "ln":
                    (s, b), which = x[1:]
                    if which:
                        dve.wait_ge(emptied_by_vector.sem, emptied_by_vector[("proj", x[1])])
                    elif s > 0:
                        before = ("down" if s - 1 in MLP_AFTER else "proj", (s - 1, b))
                        dve.wait_ge(emptied_by_vector.sem, emptied_by_vector[before])
                    else:
                        dve.wait_ge(s_x, 16)
                    norm(lambda t: X[:, b * T + t, :], T, P, LN_EPS[LAYER[s]], stats[:, b], mv[:, b],
                         veps[:, b, :], rstd[:, b, :], lambda t: xhat[:, b, t, :], x)
                if name == "stack":
                    s, b = x[1]
                    if s == SELF2:
                        dve.wait_ge(rope_q.sem, rope_q[("qs", x[1])])
                        link(dve.tensor_copy(parts[:, b, 0, 0, :], qkf[:, b, 0, :]))
                    else:
                        dve.wait_ge(emptied_by_scalar.sem, emptied_by_scalar[("q", x[1])])
                    split(qkf[:, b, 0, :], parts[:, b, 0], split_q)
                if name == "m":
                    s, b = x[1]
                    last = ("mx", x[1], H - 1, T - 1 if s in FULL else 0)
                    dve.wait_ge(emptied_by_vector.sem, emptied_by_vector[last])

                    def halves(ap):
                        return ap.rearrange("p t (a h) -> p t a h", a=2)

                    top_, rest = halves(mmax[:, b]), halves(mres[:, b])
                    for t in range(T):
                        chain[0] += 1
                        dve.tensor_scalar(mparts[:, b, t, :, 0, :], top_[:, t], -1.0, None, ALU.mult)\
                           .then_inc(s_vchain, 1)
                    dve.wait_ge(s_vchain, chain[0])
                    for t in range(T):
                        chain[0] += 1
                        dve.scalar_tensor_tensor(out=rest[:, t], in0=top_[:, t], scalar=-1.0,
                                                 in1=mparts[:, b, t, :, 0, :], op0=ALU.mult, op1=ALU.subtract)\
                           .then_inc(s_vchain, 1)
                    dve.wait_ge(s_vchain, chain[0])
                    link(dve.tensor_copy(mparts[:, b, :, :, 1, :], rest))
                    dve.tensor_tensor(mparts[:, b, :, :, 2, :], rest, mparts[:, b, :, :, 1, :], ALU.subtract)\
                       .then_inc(max_parts.sem, 1)
                if name == "tkend":
                    keep_top(x[1], H - 1)
                if name == "cT":
                    dve.wait_ge(s_ctx, 16)
                    for n, eps in enumerate((LN_EPS[0], LN_EPS[3])):
                        norm(lambda t: ctx[:, t, :], B, LC, eps, ctx_stats, ctx_mv, ctx_veps[:, n, :],
                             ctx_rstd[:, n, :], lambda t: ctx_hat[:, n, t, :], ("ln", "ctx", n))
                if name == "ck":
                    dve.wait_ge(emptied_by_scalar.sem, emptied_by_scalar[x])
                    split(ctx_k, ctx_parts[:, x[1]], split_c)
                if name in NO_BANK or (reader(x) != "V" and name != "tk"):
                    return
                dve.wait_ge(filled.sem, filled[x])
                src = bank(x)
                if name == "mod":
                    n = len(MODS)
                    bias = col("mod", 0, 2 * n)
                    m2 = M[:, :, :, :].rearrange("p m k b -> p (m k) b")
                    link(dve.tensor_tensor(m2, src[:, 0:2 * n * B].rearrange("p (m b) -> p m b", b=B),
                                           bias.unsqueeze(2).broadcast_to([P, 2 * n, B]), ALU.add))
                    link(dve.tensor_scalar(M[:, :, 1, :], M[:, :, 1, :], 1.0, None, ALU.add))
                    dve.tensor_tensor(M[:, 5:8, 1, :], M[:, 5:8, 1, :],
                                      col("norm", 0, 3).unsqueeze(2).broadcast_to([P, 3, B]),
                                      ALU.mult).then_inc(empty, 1)
                    dve.memset(V1[:, :, :, :], 1.0).then_inc(s_vset, 1)
                    dve.memset(outputs[0][:, :], 0.0).then_inc(s_vset, 1)
                    dve.memset(outputs[1][:, :], 0.0).then_inc(s_vset, 1)
                    link(dve.memset(ctx_V[:, :, :, :], 0.0))
                    link(dve.memset(ctx_V[0:LC, :, :, :], 1.0))
                if name == "v":
                    s, b = x[1]
                    to = heads(V1[:, b].rearrange("p t n -> p (t n)"))[:, :, 0:D]
                    frm = src[:, :].rearrange("p (n d) -> p n d", d=D)
                    if s == SELF2:
                        dve.tensor_copy(to, frm).then_inc(empty, 1)
                    else:
                        if x[1] == UNITS[0]:
                            dve.wait_ge(s_vrows, 16)
                        at = VROW_AT[f"v{LAYER[s]}"][0]
                        bias = vrows[:, at:at + C].rearrange("p (h d) -> p h d", d=D)
                        for t in range(T):
                            ins = dve.tensor_tensor(to[:, t * H:(t + 1) * H, :], frm[:, t * H:(t + 1) * H, :],
                                                    bias, ALU.add)
                        ins.then_inc(empty, 1)
                if name in ("q", "qs", "k", "ks"):
                    b = x[1][1]
                    i = "qk".index(name[0])
                    if x == ("k", (SELF2, 0)):
                        dve.wait_ge(s_late, 64)
                    table = rope[:, len(name) - 1, :].unsqueeze(1).broadcast_to([P, 2, S // 2])
                    to = qkf[:, b, i, :] if len(name) == 1 else res[:, b, :]
                    dve.tensor_tensor(to.rearrange("p (n s) -> p n s", n=2),
                                      src[:, :].rearrange("p (n s) -> p n s", n=2), table, ALU.mult)\
                       .then_inc(empty, 1)
                    if len(name) == 2:
                        dve.wait_ge(emptied_by_vector.sem, emptied_by_vector[x])
                        dve.tensor_tensor(qkf[:, b, i, :], qkf[:, b, i, :], res[:, b, :], ALU.add)\
                           .then_inc(rope_q.sem, 1)
                if name == "mx":
                    (s, b), h, t = x[1:]
                    if s == SELF0:
                        dve.tensor_reduce(mmax[:, b, t, h:h + 1], src[:, :], AX, ALU.max).then_inc(empty, 1)
                    elif s == SELF2:
                        last = [y for y in BANKED[:BANK_NO[x]] if y[0] == "mx" and y[1][0] == SELF2][-1:]
                        if last:
                            dve.wait_ge(emptied_by_vector.sem, emptied_by_vector[last[0]])
                        dve.tensor_tensor_reduce(junk[:, :], src[:, :], mask_q[:, t, :], 1.0, NEG, ALU.add, ALU.max,
                                                 mmax[:, b, t, h:h + 1]).then_inc(empty, 1)
                    else:
                        n = P if s == WINDOW else LC
                        dve.tensor_reduce(mmax[:, b, :, h:h + 1], src[:, 0:T * n].rearrange("p (t k) -> p t k", t=T),
                                          AX, ALU.max).then_inc(empty, 1)
                if name == "tk":
                    u, h = x[1:]
                    b, a = u[1], h % 2
                    if h >= 2:
                        dve.wait_ge(top_kept.sem, top_kept[("tk", u, h - 2)])
                    tile = [src[:, t * LC:(t + 1) * LC] for t in range(T)]
                    best, rest = top[:, b, a], left[:, b, a]
                    for t in range(T):
                        chain[0] += 1
                        dve.max(best[:, t, 0:8], tile[t]).then_inc(s_vchain, 1)
                    dve.wait_ge(s_vchain, chain[0])
                    for t in range(T):
                        chain[0] += 1
                        dve.match_replace(rest[:, t, :], best[:, t, 0:8], tile[t], NEG).then_inc(s_vchain, 1)
                    dve.wait_ge(s_vchain, chain[0])
                    dve.tensor_scalar(nbias[:, b, a, :], best[:, :, 0], -SCALE, None, ALU.mult)\
                       .then_inc(top_found.sem, 1)
                    for t in range(T):
                        chain[0] += 1
                        dve.max(best[:, t, 8:16], rest[:, t, :]).then_inc(s_vchain, 1)
                    dve.wait_ge(s_vchain, chain[0])
                    for t in range(T):
                        chain[0] += 1
                        dve.match_replace(rest[:, t, :], best[:, t, 8:16], rest[:, t, :], NEG).then_inc(s_vchain, 1)
                    dve.wait_ge(s_vchain, chain[0])
                    if h:
                        keep_top(u, h - 1)
                if name == "oT":
                    b, t = x[1][1], x[2]
                    v = src[:, :].rearrange("p (h r) -> p h r", r=P // HG)
                    link(dve.reciprocal(rsum[:, b, t, :], v[:, :, D]))
                    dve.tensor_tensor(On[:, b, t, :].rearrange("p (h d) -> p h d", d=D), v[:, :, 0:D],
                                      rsum[:, b, t, :].unsqueeze(2).broadcast_to([P, H, D]), ALU.mult)\
                       .then_inc(empty, 1)
                if name in ("proj", "down"):
                    b, which = x[1][1], int(name == "down")
                    if bias_row(x[1], which) is not None:
                        dve.wait_ge(biased.sem, biased[(x[1], which)])
                    xs = X[:, b * T:(b + 1) * T, :].rearrange("p t c -> p (t c)")
                    dve.tensor_tensor(xs, src[:, :], xs, ALU.add).then_inc(empty, 1)
                if name == "hb":
                    (s, b), i = x[1:]
                    dve.wait_ge(emptied_by_scalar.sem, emptied_by_scalar[("ha", x[1], i)])
                    dve.scalar_tensor_tensor(out=U[:, b, i, :], in0=src[:, :], scalar=col("up1b", i),
                                             in1=gated[i % 2][:, b, :], op0=ALU.add, op1=ALU.mult).then_inc(empty, 1)
                if name == "cT":
                    cs = src[:, 0:2 * B * LC].rearrange("p (n b k) -> p n b k", n=2, b=B)
                    link(dve.tensor_copy(ctxT[:, 0:2], cs))
                    for b in range(B):
                        ins = dve.tensor_scalar(ctxT[:, 2, b, :], src[:, (2 * B + b) * LC:(2 * B + b + 1) * LC],
                                                M[:, MOD_KV3, 1, b:b + 1], M[:, MOD_KV3, 0, b:b + 1],
                                                ALU.mult, ALU.add)
                    ins.then_inc(empty, 1)
                if name == "cv":
                    c = x[1]
                    to = heads(ctx_V[0:LC, c].rearrange("p b n -> p (b n)"))[:, :, 0:D]
                    frm = src[0:LC, 0:B * C].rearrange("p (n d) -> p n d", d=D)
                    if c == 2:
                        dve.tensor_copy(to, frm).then_inc(empty, 1)
                    else:
                        at = VROW_AT[f"vc{c}"][0]
                        bias = vrows[0:LC, at:at + C].rearrange("p (h d) -> p h d", d=D)
                        for b in range(B):
                            ins = dve.tensor_tensor(to[:, b * H:(b + 1) * H, :], frm[:, b * H:(b + 1) * H, :], bias,
                                                    ALU.add)
                        ins.then_inc(empty, 1)
                if name == "gate":
                    i = x[1]
                    n = GATED[i][2]
                    at, o = RAW_AT[i][0], ROW_AT["gate"][0] + i * C
                    if i == 0:
                        dve.wait_ge(s_raw, 32)
                    if i >= 2:
                        dve.wait_ge(emptied_by_vector.sem, emptied_by_vector[("gate", i - 2)])
                    g = gate_row[:, i % 2]
                    link(dve.tensor_tensor(g, src[:, 0:B * C].rearrange("p (b c) -> p b c", b=B),
                                           rows[:, o:o + C].unsqueeze(1).broadcast_to([P, B, C]), ALU.add))
                    if i in BIASED:
                        o = ROW_AT["out"][0] + BIASED.index(i) * C
                        chain[0] += 1
                        dve.tensor_tensor(rowg[:, BIASED.index(i)], g,
                                          rows[:, o:o + C].unsqueeze(1).broadcast_to([P, B, C]), ALU.mult)\
                           .then_inc(s_vchain, 1)
                    for b in (1, 0):
                        ins = dve.tensor_tensor(Wg[:, b, at:at + n * C].rearrange("p (n c) -> p n c", n=n),
                                                g[:, b, :].unsqueeze(1).broadcast_to([P, n, C]),
                                                raw[:, at:at + n * C].rearrange("p (n c) -> p n c", n=n), ALU.mult)
                    ins.then_inc(empty, 1)

            for x in CHAIN:
                do(x)

        @block.tensor
        def _(pe):
            def turn(to, frm, eye, n):
                return pe.matmul(to, frm, eye[0:n, 0:n], start=True, stop=True, is_transpose=True)

            def queries(b, h, rows_, at=0, n=S):
                return QS[0:rows_, b, h % H2, at:at + n]

            def stacks_placed(u):
                pe.wait_ge(s_qs[u[1]], query_moves(u))
                pe.wait_ge(s_ks[u[1]], key_moves(u))

            def piece(x):
                name = x[0]
                to = free_bank(pe, x)
                if name == "mod":
                    pe.wait_ge(s_ada, 16)
                    pe.wait_ge(s_wide, 1)
                    for i, (layer, *chunks) in enumerate(MODS):
                        for j, chunk in enumerate(chunks):
                            at = ADA_AT[layer][0] + chunk * C
                            n = 2 * i + j
                            ins = pe.matmul(to[:, n * B:(n + 1) * B], ada[:, at:at + C],
                                            acts[:, 0 if layer == 2 else 1, :], start=True, stop=True)
                if name == "hT":
                    b = x[1][1]
                    pe.wait_ge(normed.sem, normed[("ln",) + x[1:]])
                    if x[1] == UNITS[0]:
                        pe.wait_ge(s_small, 32)
                    for t in range(T):
                        ins = turn(to[:, t * P:(t + 1) * P], xhat[:, b, t, :], ident, P)
                if name in ("q", "k", "qs", "ks"):
                    s, b = x[1]
                    pe.wait_ge(emptied_by_scalar.sem, emptied_by_scalar[("hT", x[1], 0)])
                    if x[1] == UNITS[0]:
                        pe.wait_ge(s_w0, 16)
                    if x[1] == (CROSS0, 0):
                        pe.wait_ge(s_w, 16)
                    wname = f"{name[0]}{LAYER[s]}{name[1:]}" if s in OWN_KEYS else f"qc{LAYER[s]}"
                    ins = pe.matmul(to[:, :], w(wname), hT[:, b, :], start=True, stop=True)
                if name == "v":
                    s, b = x[1]
                    for t in range(T):
                        ins = pe.matmul(to[:, t * C:(t + 1) * C], hT[:, b, t * P:(t + 1) * P], w(f"v{LAYER[s]}"),
                                        start=True, stop=True)
                if name == "mx":
                    (s, b), h, t = x[1:]
                    if h + t == 0:
                        stacks_placed(x[1])
                        pe.wait_ge(s_const, 3)
                    if s in FULL:
                        ins = pe.matmul(to[:, :], queries(b, h, QK_ROWS, t * P, P), KS[0:QK_ROWS, b, h, :],
                                        start=True, stop=True)
                    else:
                        n = P if s == WINDOW else LC
                        masked = s in (WINDOW, CROSS2)
                        tiles = to[:, 0:T * n].rearrange("p (t k) -> p t k", t=T)
                        if s == WINDOW:
                            pe.matmul(tiles, identb[:, :], wmask[:, :].unsqueeze(1).broadcast_to([P, T, P]),
                                      start=True, stop=False, skip_group_check=True)
                        if s == CROSS2:
                            pe.matmul(tiles, first_row[:, 0:P], cmask[:, b, 0:LC].unsqueeze(1).broadcast_to([P, T, LC]),
                                      start=True, stop=False, skip_group_check=True)
                        for i in range(T):
                            keys = KS[0:QK_ROWS, b, h, i * P:(i + 1) * P] if s == WINDOW else KC[0:QK_ROWS, b, h, 0:LC]
                            ins = pe.matmul(to[:, i * n:(i + 1) * n], queries(b, h, QK_ROWS, i * P, P), keys,
                                            start=not masked, stop=True, skip_group_check=masked)
                if name == "tk":
                    u, h = x[1:]
                    if h == 0:
                        stacks_placed(u)
                    for i in range(T):
                        ins = pe.matmul(to[:, i * LC:(i + 1) * LC], queries(u[1], h, QK_ROWS, i * P, P),
                                        KC[0:QK_ROWS, u[1], h, 0:LC], start=True, stop=True)
                if name == "mT":
                    b = x[1][1]
                    pe.wait_ge(max_parts.sem, max_parts[("m", x[1])])
                    tb = to[:, :].bitcast(BF16)
                    for t in range(T):
                        ins = turn(tb[0:3 * H, t * P:(t + 1) * P], mparts[:, b, t].rearrange("p a n h -> p (a n h)"),
                                   identb, P)
                if name == "oT":
                    u, t = x[1:]
                    pe.wait_ge(saved.sem, saved[("save", u, G - 1)])
                    for g in range(G):
                        ins = turn(to[:, g * P:(g + 1) * P], OG[:, u[1], g, t * P:(t + 1) * P], ident, P)
                if name == "onT":
                    pe.wait_ge(emptied_by_vector.sem, emptied_by_vector[("oT", x[1], T - 1)])
                    for t in range(T):
                        ins = turn(to[:, t * P:(t + 1) * P], On[:, x[1][1], t, :], ident, P)
                if name == "proj":
                    s, b = x[1]
                    pe.wait_ge(emptied_by_scalar.sem, emptied_by_scalar[("onT", x[1])])
                    i = GATE_OF.get((s, 0))
                    if i is None:
                        matrix = w("cp0" if s == CROSS0 else "p3")
                    else:
                        matrix = Wg[:, b, RAW_AT[i][0]:RAW_AT[i][0] + C]
                    for t in range(T):
                        ins = pe.matmul(to[:, t * C:(t + 1) * C], OT[:, b, t * P:(t + 1) * P], matrix,
                                        start=True, stop=True)
                if name in ("ha", "hb"):
                    (s, b), i = x[1:]
                    pe.wait_ge(emptied_by_scalar.sem, emptied_by_scalar[("hT", x[1], 1)])
                    wname = f"up{LAYER[s]}" + (name[1] if LAYER[s] == 1 else "")
                    ins = pe.matmul(to[:, :], w(wname, i), hT[:, b, :], start=True, stop=True)
                if name == "down":
                    s, b = x[1]
                    if LAYER[s] == 1:
                        pe.wait_ge(emptied_by_vector.sem, emptied_by_vector[("hb", x[1], NI - 1)])
                    else:
                        pe.wait_ge(emptied_by_scalar.sem, emptied_by_scalar[("ha", x[1], NI - 1)])
                    at = RAW_AT[GATE_OF[(s, 1)]][0]
                    for t in range(T):
                        for n in range(NI):
                            ins = pe.matmul(to[:, t * C:(t + 1) * C], U[:, b, n, t * P:(t + 1) * P],
                                            Wg[:, b, at + n * C:at + (n + 1) * C], start=n == 0, stop=n == NI - 1)
                if name == "cT":
                    pe.wait_ge(normed.sem, normed[("ln", "ctx", 1)])
                    for n in range(3):
                        for b in range(B):
                            frm = ctx[:, b, :] if n == 0 else ctx_hat[:, n - 1, b, :]
                            ins = turn(to[:, (n * B + b) * LC:(n * B + b + 1) * LC], frm, ident, LC)
                if name == "ck":
                    pe.wait_ge(emptied_by_vector.sem, emptied_by_vector[("cT",)])
                    pe.wait_ge(s_wc, 16)
                    src = ctxT[:, (1, 0, 0, 2)[x[1]]].rearrange("p b k -> p (b k)")
                    ins = pe.matmul(to[:, 0:B * LC], wc(f"kc{x[1]}"), src, start=True, stop=True)
                if name == "cv":
                    c = x[1]
                    for b in range(B):
                        ins = pe.matmul(to[0:LC, b * C:(b + 1) * C], ctxT[:, (1, 0, 0, 2)[c], b, :], wc(f"vc{c}"),
                                        start=True, stop=True)
                if name == "gate":
                    layer, chunk = GATED[x[1]][:2]
                    at = ADA_AT[layer][0] + chunk * C
                    for b in range(B):
                        ins = pe.matmul(to[:, b * C:(b + 1) * C], acts_wide[:, 0 if layer == 2 else 1, b, :],
                                        ada[:, at:at + C], start=True, stop=True)
                if name == "mask":
                    kt = x[1]
                    pe.wait_ge(s_cmask, 3)
                    tb = to[:, :].bitcast(BF16)
                    for t in range(T):
                        ins = turn(tb[:, t * P:(t + 1) * P], mask_q[:, t, kt * P:(kt + 1) * P], identb, P)
                ins.then_inc(filled.sem, 1)

            def score(x):
                u, g, kt, j = x[1:]
                (s, b), h, n = u, g * HG + j, ITEM_NO[x]
                if n >= SCORES:
                    pe.wait_ge(exped.sem, exped[ITEMS[n - SCORES]])
                to = scores[n % SCORES]
                if s != TOPK16 and g + kt + j == 0:
                    pe.wait_ge(s_ms[b], max_moves(u))
                    if s == SELF0:
                        pe.wait_ge(s_ones[b], 16 * 4)
                q = queries(b, h, ROWS)
                if s in FULL:
                    if s == SELF2:
                        pe.matmul(to[:, :], identb[:, :], mask_k[:, kt, :], start=True, stop=False)
                    ins = pe.matmul(to[:, :], KS[0:ROWS, b, h, kt * P:(kt + 1) * P], q, start=s == SELF0, stop=True)
                if s == WINDOW:
                    pe.matmul(to[:, :].rearrange("p (t k) -> p t k", t=T), identb[:, :],
                              wmask[:, :].unsqueeze(1).broadcast_to([P, T, P]), start=True, stop=False,
                              skip_group_check=True)
                    for t in range(T):
                        c = slice(t * P, (t + 1) * P)
                        ins = pe.matmul(to[:, c], KS[0:ROWS, b, h, c], q[:, c], start=False, stop=True,
                                        skip_group_check=True)
                if s in (CROSS0, CROSS2, CROSS3):
                    if s == CROSS2:
                        pe.matmul(to[0:LCP, :], cmask[:, b, :], first_row[:, :], start=True, stop=False)
                    ins = pe.matmul(to[0:LCP, :], KC[0:ROWS, b, h, :], q, start=s != CROSS2, stop=True)
                if s == TOPK16:
                    pe.wait_ge(top_kept.sem, top_kept[("tk", u, h)])
                    for t in range(T):
                        ins = turn(to[0:LC, t * P:(t + 1) * P], PQ[:, b, h % 4, t * LC:(t + 1) * LC], ident, P)
                ins.then_inc(scored.sem, 1)

            def sum_values(x):
                u, g, kt = x[1:]
                s, b = u
                to = outputs[b]
                pe.wait_ge(exped.sem, exped[("ex", u, g, kt, HG - 1)])
                if kt == 0:
                    at = SAVES[b].index(("save", u, g))
                    if at:
                        pe.wait_ge(saved.sem, saved[SAVES[b][at - 1]])
                    else:
                        pe.wait_ge(s_vset, 3)
                    if s in OWN_KEYS:
                        pe.wait_ge(emptied_by_vector.sem, emptied_by_vector[("v", u)])
                if s == WINDOW:
                    for t in range(T):
                        c = slice(t * P, (t + 1) * P)
                        for j in range(HG):
                            h, slot = g * HG + j, OWN_NO[("ex", u, g, kt, j)] % RING
                            ins = pe.matmul(to[32 * j:32 * j + VW, c], V1[:, b, t, h * VW:(h + 1) * VW],
                                            PT[:, b, slot, c], start=True, stop=True)
                else:
                    for j in range(HG):
                        h, slot = g * HG + j, OWN_NO[("ex", u, g, kt, j)] % RING
                        v = slice(h * VW, (h + 1) * VW)
                        if s in FULL:
                            ins = pe.matmul(to[32 * j:32 * j + VW, :], V1[:, b, kt, v], PT[:, b, slot, :],
                                            start=kt == 0, stop=kt == T - 1)
                        else:
                            ins = pe.matmul(to[32 * j:32 * j + VW, :], ctx_V[:, CTX_OF[s], b, v],
                                            PT[0:LCP, b, slot, :], start=True, stop=True)
                ins.then_inc(summed.sem, 1)

            for x in CHAIN:
                if x[0] == "ex":
                    score(x)
                elif x[0] == "pv":
                    sum_values(x)
                elif x[0] not in NO_BANK:
                    piece(x)


def _layout(i):
    f = lambda a: np.asarray(a)
    L0, L1, L2, L3 = ({k[9:]: f(v) for k, v in i.items() if k.startswith(f"L{n}_xcond_")} for n in range(4))

    def dh(a):
        return a.reshape(a.shape[:-1] + (2, H2, D)).swapaxes(-1, -2).reshape(a.shape)

    def swap(a):
        a = a.reshape(a.shape[:-1] + (H, 2, D // 2))
        return a[..., ::-1, :].reshape(a.shape[:-3] + (C,))

    def cut(a, *n):
        return [a[..., j * C:(j + 1) * C] for j in n]

    def tall(a):
        return a.reshape(NI, P, C).transpose(1, 0, 2).reshape(P, NI * C)

    q0, k0, v0 = cut(L0["W_qkv"], 0, 1, 2)
    kc0, vc0 = cut(L0["W_kvc"], 0, 1)
    q1, k1, v1 = cut(L1["w_qkv"], 0, 1, 2)
    kc1, vc1 = cut(L1["w_kv"], 0, 1)
    q2, k2, v2 = cut(L2["qkv_W"], 0, 1, 2)
    kc3, vc3 = cut(L3["Wkv"], 0, 1)
    weights = {"q0": dh(q0), "k0": dh(k0), "v0": v0, "qc0": dh(L0["W_qc"]), "kc0": dh(kc0), "vc0": vc0,
               "cp0": L0["W_cproj"], "up0": L0["W_mlp1"], "q1": dh(q1), "k1": dh(k1), "v1": v1,
               "qc1": dh(L1["w_q"]), "kc1": dh(kc1), "vc1": vc1, "up1a": L1["w_m1"][:, :HID],
               "up1b": L1["w_m1"][:, HID:], "q2": dh(q2), "k2": dh(k2), "v2": v2, "q2s": dh(swap(q2)),
               "k2s": dh(swap(k2)), "qc2": dh(L2["cq_W"]), "kc2": dh(L2["ck_W"]), "vc2": L2["cv_W"],
               "up2": L2["mlp_W1"], "qc3": dh(L3["Wq"]), "kc3": dh(kc3), "vc3": vc3, "p3": L3["Wp"]}
    w_pack = np.concatenate([weights[n] for n, _ in W_MAIN], 1)
    wc_pack = np.concatenate([weights[n] for n, _ in W_CTX], 1)
    ada = np.concatenate([L0["W_mod"], L1["w_ada"], L2["adaLN_W"], L3["Wss_q"], L3["Wss_kv"]], 1)
    raw = np.concatenate([L0["W_proj"], tall(L0["W_mlp2"]), L1["w_so"], L1["w_co"], tall(L1["w_m2"]),
                          L2["attn_out_W"], L2["co_W"], tall(L2["mlp_W2"])], 1)
    b_ada = [L0["b_mod"], L1["b_ada"], L2["adaLN_b"], np.concatenate([L3["bss_q"], L3["bss_kv"]])]
    mod_cols = [b_ada[layer][c * C:(c + 1) * C] for layer, *cs in MODS for c in cs]
    bq0, bk0, bv0 = cut(L0["b_qkv"], 0, 1, 2)
    bq1, bk1, bv1 = cut(L1["b_qkv"], 0, 1, 2)
    bkc0, bvc0 = cut(L0["b_kvc"], 0, 1)
    bkc1, bvc1 = cut(L1["b_kv"], 0, 1)
    bkc3, bvc3 = cut(L3["bkv"], 0, 1)
    blocks = lambda a: [a[j * P:(j + 1) * P] for j in range(NI)]
    columns = mod_cols + [L2["norm1_w"], L2["normc_w"], L2["norm2_w"], dh(bq0), dh(bk0), dh(bq1), dh(bk1),
                          dh(L0["b_qc"]), dh(L1["b_q"]), dh(L3["bq"]), dh(bkc0), dh(bkc1), dh(bkc3)] \
        + blocks(L0["b_mlp1"]) + blocks(L1["b_m1"][:HID]) + blocks(L1["b_m1"][HID:]) + blocks(L2["mlp_b1"]) \
        + [f(i["cond_1024"])[j] for j in range(B)]
    vrow = np.concatenate([bv0, bv1, L0["b_cproj"], L3["bp"], bvc0, bvc1, bvc3])
    row = np.concatenate([b_ada[layer][c * C:(c + 1) * C] for layer, c, _, _ in GATED]
                         + [L0["b_proj"], L0["b_mlp2"], L1["b_so"], L1["b_co"], L1["b_m2"], L2["mlp_b2"]])

    eye = np.eye(P, dtype=np.float32)
    a = np.arange(P)
    window = np.where(a[:, None] // WIN == a[None, :] // WIN, 0.0, NEG).astype(np.float32)
    freq = 1.0 / 10000.0 ** (np.arange(0, D, 2, dtype=np.float32) / D)
    angle = np.outer(np.arange(S // 2, dtype=np.float32), freq)
    emb = np.concatenate([angle, angle], -1)
    table = np.stack([np.cos(emb), np.sin(emb) * np.where(np.arange(D) < D // 2, -1.0, 1.0)]).astype(np.float32)
    table = np.broadcast_to(table.transpose(2, 0, 1)[:, None], (2, D, H2, 2, S // 2)).reshape(P, 2, S // 2)
    return {
        "x": f(i["x"]), "ctx": f(i["ctx_1024"]),
        "cmask": f(i["mask_BxS2_bf1"]).reshape(1, B * LC),
        "smask": f(i["mask_SxS_bk0"]),
        "w": w_pack, "wc": wc_pack, "ada": ada, "raw": raw, "col": np.stack(columns, 1), "vrow": vrow, "row": row,
        "ident": eye, "wmask": window,
        "rope": table,
    }


def kernel(**inputs):
    import concourse.bacc as bacc
    from concourse.bass_utils import run_bass_kernel_spmd

    nc = bacc.Bacc("TRN2", target_bir_lowering=False, num_devices=1)
    arrays, args = {}, []
    for name, a in _layout(inputs).items():
        a = np.ascontiguousarray(a)
        arrays[f"in_{name}"] = a
        args.append(nc.dram_tensor(f"in_{name}", a.shape, mybir.dt.from_np(a.dtype), kind="ExternalInput").ap())
    args.append(nc.dram_tensor("out_0", (B, S, C), F32, kind="ExternalOutput").ap())
    pixart_four_layers(nc, *args)
    r = run_bass_kernel_spmd(nc, [arrays], core_ids=[0])
    return r.results[0]["out_0"]
```

```python
from contextlib import ExitStack

import concourse.bass as bass
import concourse.mybir as mybir
import numpy as np

ALU = mybir.AluOpType
ACT = mybir.ActivationFunctionType
AX = mybir.AxisListType.X
F32 = mybir.dt.float32
BF16 = mybir.dt.bfloat16
U8 = mybir.dt.uint8

P = 128
B, S, C = 2, 512, 128
T = S // P
H, D = 16, 8
LC = 77
HID = 512
NI = HID // P
WIN, SHIFT = 64, 32
TOPK = 16
SCALE = float(D) ** -0.5
NEG = -3.3895313892515355e38
G, HG = 4, 4
VW = D + 1

SELF0, CROSS0, WINDOW, TOPK16, SELF2, CROSS2, CROSS3 = range(7)
NSTAGE = 7
LAYER = [0, 0, 1, 1, 2, 2, 3]
OWN_KEYS = (SELF0, WINDOW, SELF2)
FULL = (SELF0, SELF2)
CTX_OF = {CROSS0: 0, TOPK16: 1, CROSS2: 2, CROSS3: 3}
MLP_AFTER = (CROSS0, TOPK16, CROSS2)
LN_EPS = [1e-6, 1e-6, 1e-5, 1e-5]

Q_PART = [0, 0, 1, 1, 0, 2]
K_PART = [0, 1, 0, 1, 2, 0]
H2 = H // 2
QK_ROWS = 2 * len(Q_PART) * D
ROWS = QK_ROWS + 2 * 3
LCP = 96

MODS = [(0, 0, 1), (0, 3, 4), (1, 0, 1), (1, 3, 4), (1, 6, 7), (2, 0, 1), (2, 3, 4), (2, 6, 7),
        (3, 1, 0), (3, 3, 2)]
MOD_OF = {(SELF0, 0): 0, (CROSS0, 1): 1, (WINDOW, 0): 2, (TOPK16, 0): 3, (TOPK16, 1): 4, (SELF2, 0): 5,
          (CROSS2, 0): 6, (CROSS2, 1): 7, (CROSS3, 0): 8}
MOD_KV3 = 9
FIRST_MODS = 2
GATED = [(0, 2, 1, "proj0"), (0, 5, NI, "down0"), (1, 2, 1, "so"), (1, 5, 1, "co"), (1, 8, NI, "down1"),
         (2, 2, 1, "ao"), (2, 5, 1, "co2"), (2, 8, NI, "down2")]
GATE_OF = {(SELF0, 0): 0, (CROSS0, 1): 1, (WINDOW, 0): 2, (TOPK16, 0): 3, (TOPK16, 1): 4, (SELF2, 0): 5,
           (CROSS2, 0): 6, (CROSS2, 1): 7}

def offsets(parts):
    at, out = 0, {}
    for name, n in parts:
        out[name] = (at, n)
        at += n
    return out, at


W_MAIN = [("q0", C), ("k0", C), ("v0", C), ("qc0", C), ("cp0", C), ("up0", HID),
          ("q1", C), ("k1", C), ("v1", C), ("qc1", C), ("up1a", HID), ("up1b", HID),
          ("q2", C), ("k2", C), ("v2", C), ("q2s", C), ("k2s", C), ("qc2", C),
          ("up2", HID), ("qc3", C), ("p3", C)]
W_AT, W_COLS = offsets(W_MAIN)
W_FIRST = W_AT["qc0"][0]
W_CTX = [(f"{n}{c}", C) for c in range(4) for n in ("kc", "vc")]
CTX_AT, CTX_COLS = offsets(W_CTX)
ADA_AT, ADA_COLS = offsets([(0, 6 * C), (1, 9 * C), (2, 9 * C), (3, 4 * C)])
ADA_FIRST = ADA_AT[1][0]
RAW_AT, RAW_COLS = offsets([(i, n * C) for i, (_, _, n, _) in enumerate(GATED)])
COL_AT, COLS = offsets([("mod", 2 * len(MODS)), ("norm", 3), ("q0", 1), ("k0", 1), ("q1", 1), ("k1", 1),
                        ("qc0", 1), ("qc1", 1), ("qc3", 1), ("kc0", 1), ("kc1", 1), ("kc3", 1), ("up0", NI),
                        ("up1a", NI), ("up1b", NI), ("up2", NI), ("cond", B)])
VROW_AT, VROWS = offsets([("v0", C), ("v1", C), ("cp0", C), ("p3", C), ("vc0", C), ("vc1", C), ("vc3", C)])
GATE_ROWS = 4
BIASED = [0, 1, 2, 3, 4, 7]
ROW_AT, ROWCOLS = offsets([("gate", len(GATED) * C), ("out", len(BIASED) * C)])

UNITS = [(s, b) for s in range(NSTAGE) for b in range(B)]


def prep(s, b):
    u = (s, b)
    names = {SELF2: ("k", "ks", "q", "qs", "v"), SELF0: ("k", "q", "v"), WINDOW: ("k", "q", "v")}.get(s, ("q",))
    return [("ln", u, 0), ("hT", u, 0)] + [(n, u) for n in names] + [("stack", u)]


def with_sums(items, s, lead):
    out = []
    for n, x in enumerate(items):
        out += lead(n) + [x]
        if n >= PV_LAG and items[n - PV_LAG][4] == HG - 1:
            out += sums(items[n - PV_LAG], s)
    return out + sums(items[-1], s)


def sums(item, s):
    _, u, g, kt, _ = item
    return [("pv", u, g, kt)] + ([("save", u, g)] if kt == (T - 1 if s in FULL else 0) else [])


def probabilities_of(s, b):
    u = (s, b)
    items = [("ex", u, g, kt, j) for g in range(G) for kt in range(T if s in FULL else 1) for j in range(HG)]
    if s == TOPK16:
        finds = [("tk", u, h) for h in range(H)] + [("tkend", u)]
        return finds[:TK_LAG] + with_sums(items, s, lambda n: finds[n + TK_LAG:n + TK_LAG + 1])
    maxima = [("mx", u, h, t) for h in range(H) for t in range(T if s in FULL else 1)]
    ends = [[("m", u, half), ("mT", u, half)] for half in range(2)]
    half = len(maxima) // 2
    lead = maxima[:half] + ends[0] + maxima[half:half + MX_AHEAD]
    rest = maxima[half + MX_AHEAD:]
    last = len(rest) - 1
    kc = [("kc", (s + 1, b))] if s in OWN_KEYS else []
    return lead + with_sums(items, s, lambda n: rest[n:n + 1] + (ends[1] + kc if n == last else []))


def post(s, b):
    u = (s, b)
    out = [("kc", (CROSS3, b))] if s == CROSS2 else []
    out += [("oT", u, t) for t in range(T)] + [("onT", u), ("proj", u)]
    if s in MLP_AFTER:
        out += [("ln", u, 1), ("hT", u, 1)]
        out += [(n, u, i) for i in range(NI) for n in (("ha", "hb") if LAYER[s] == 1 else ("ha",))]
        out.append(("down", u))
    if s == NSTAGE - 1:
        out.append(("out", u))
    return out


PV_LAG = 2
TK_LAG = 2
MX_AHEAD = 3
PROLOGUE = [("mod", 0)]
EARLY = [("mod", 1), ("cT",)] + [("ck", c) for c in range(4)] + [("cv", c) for c in range(4)] \
    + [("gate", i) for i in range(len(GATED))]
MASKS = [("mask", t) for t in range(T)]
NEEDS = {"ln": ("proj", "down"), "hT": ("ln",), "k": ("hT",), "ks": ("hT",), "q": ("hT",), "qs": ("hT",),
         "v": ("hT",), "stack": ("k", "ks", "q", "qs"), "mx": ("stack",), "tk": ("stack",), "m": ("mx",),
         "mT": ("m",), "ex": ("mT",), "oT": ("save",), "onT": ("oT",), "proj": ("onT",), "ha": ("hT",),
         "hb": ("hT",), "down": ("ha", "hb")}


def price(x):
    name, s = x[0], x[1][0] if len(x) > 1 and isinstance(x[1], tuple) else None
    return {"ln": (0, "V", 3.5, 1.5), "hT": (0.5, "S", 0.7, 0), "k": (0.9, "S", 1.2, 0), "q": (0.9, "S", 1.2, 0),
            "ks": (0.9, "V", 1.2, 0), "qs": (0.9, "V", 1.2, 0), "v": (0.5, "V", 0.7, 0),
            "stack": (0, "V", 1.2, 15.0 if s in OWN_KEYS else 10.0),
            "mx": (0.22 if s in FULL else 0.65 if s == WINDOW else 0.4, "V", 0.6, 0),
            "m": (0, "V", 0.7, 0.3), "mT": (0.4, "S", 0.5, 3.5),
            "ex": (0.22 + 0.22 * (s in (SELF2, CROSS2)) + 0.43 * (s == WINDOW), "S", 0.7, 0),
            "pv": (1.0, "", 0, 0), "save": (0, "S", 0.45, 0), "tk": (0.35, "V", 3.4, 0), "tkend": (0, "V", 0.4, 0),
            "oT": (0.45, "V", 0.5, 0), "onT": (0.45, "S", 0.6, 0), "proj": (0.45, "V", 0.7, 0),
            "ha": (0.9, "S", 0.6, 0), "hb": (0.9, "V", 0.7, 0), "down": (1.8, "V", 0.7, 0),
            "ck": (0.3, "V", 0.9, 0), "cv": (0.3, "V", 0.4, 0), "gate": (0.45, "V", 0.4, 0),
            "mask": (0.3, "S", 0.5, 0), "mod": (0.5, "V", 4.0, 0), "cT": (0.6, "V", 5.0, 0)}.get(name, (0, "", 0, 0))


def timed(b):
    free = {"T": 0.0, "V": 0.0, "S": 0.0, "": 0.0}
    ring = {True: [0.0] * SCORES, False: [0.0] * BANKS}
    at, ended, out = 0.0, {}, []
    for x in [x for s in range(NSTAGE) for x in prep(s, b) + probabilities_of(s, b) + post(s, b)]:
        tensor, other, cost, latency = price(x)
        banks = ring[x[0] == "ex"]
        at = max([at] + [ended.get(name, 0.0) for name in NEEDS.get(x[0], ())])
        if tensor:
            at = max(at, free["T"], banks[0] if x[0] != "pv" else 0.0)
            free["T"] = at + tensor
        end = max(at + tensor, free[other]) + cost
        if other:
            free[other] = end
        if tensor and x[0] != "pv":
            banks[:] = banks[1:] + [end]
        ended[x[0]] = end + latency
        out.append((at, x))
    return out


def program():
    streams = [timed(0), [(at + LAG[x[1][0]], x) for at, x in timed(1)],
               [(EARLY_AT + n * EARLY_STEP, x) for n, x in enumerate(EARLY)],
               [(MASKS_AT, x) for x in MASKS]]
    order = []
    while any(streams):
        left = [i for i in range(4) if streams[i]]
        if streams[2]:
            left = [i for i in left if streams[i][0][1][0] != "ex"]
        order.append(streams[min(left, key=lambda i: streams[i][0][0])].pop(0)[1])
    return PROLOGUE + order


LAG = (20,) * NSTAGE
EARLY_AT, EARLY_STEP = 15, 1
MASKS_AT = 100
BANKS = 3
SCORES = 3
RING = 6
CHAIN = program()
NO_BANK = ("ln", "stack", "kc", "m", "tkend", "out", "ex", "pv", "save")


def reader(x):
    if x[0] in ("q", "k"):
        return "V" if x[1][0] == SELF2 else "S"
    return "S" if x[0] in ("hT", "ck", "mask", "mT", "tk", "onT", "ha") else "V"


BANKED = [x for x in CHAIN if x[0] not in NO_BANK]
MASKED_MAXIMA = [x for x in CHAIN if x[0] == "mx" and x[1][0] == SELF2]
BANK_NO = {x: n for n, x in enumerate(BANKED)}
ITEMS = [x for x in CHAIN if x[0] == "ex"]
ITEM_NO = {x: n for n, x in enumerate(ITEMS)}
OWN_ITEMS = [[x for x in ITEMS if x[1][1] == b] for b in range(B)]
OWN_NO = {x: n for own in OWN_ITEMS for n, x in enumerate(own)}
SAVES = [[x for x in CHAIN if x[0] == "save" and x[1][1] == b] for b in range(B)]


KEEPS = [("tk", x[1], x[2] - 1 if x[0] == "tk" else H - 1) for x in CHAIN
         if x[0] == "tkend" or (x[0] == "tk" and x[2])]


def bias_row(u, which):
    s = u[0]
    i = GATE_OF.get((s, which))
    if i is None:
        return "cp0" if s == CROSS0 else "p3"
    return i if i in BIASED else None


class Count:

    def __init__(self, sem, events):
        self.sem = sem
        self.after = {e: i + 1 for i, e in enumerate(events)}

    def __getitem__(self, event):
        return self.after[event]


def pixart_four_layers(nc, x_in, ctx_in, cmask_in, smask_in, w_in, wc_in, ada_in, raw_in, col_in, vrow_in,
                       row_in, ident_in, wmask_in, rope_in, out):
    with ExitStack() as stack:
        def sb(name, shape, dt=F32):
            return stack.enter_context(nc.sbuf_tensor(name, shape, dt))

        def sem(name):
            return stack.enter_context(nc.semaphore(name))

        X = sb("X", [P, B * T, C])
        ctx = sb("ctx", [LC, B, C])
        W = sb("W", [P, W_COLS])
        cols = sb("cols", [P, COLS])
        vrows = sb("vrows", [P, VROWS])
        ident = sb("ident", [P, P])
        identb = sb("identb", [P, P], BF16)
        wmask = sb("wmask", [P, P], BF16)
        rope = sb("rope", [P, 2, S // 2])
        first_row = sb("first_row", [P, S], BF16)
        onesb = sb("onesb", [3, S], BF16)
        half_neg = sb("half_neg", [P, T])
        acts = sb("acts", [P, 2, B])
        M = sb("M", [P, len(MODS), 2, B])
        Wg = sb("Wg", [P, B, RAW_COLS])
        rowg = sb("rowg", [P, len(BIASED), B, C])
        mask_q = sb("mask_q", [P, T, S], BF16)
        mask_k = sb("mask_k", [P, T, S], BF16)
        cmask_u8 = sb("cmask_u8", [1, B * LC], U8)
        cmask = sb("cmask", [P, B, LCP], BF16)
        ctx_parts = sb("ctx_parts", [P, 4, 3, B * LC], BF16)
        ctx_V = sb("ctx_V", [LCP, 4, B, H * VW])
        QS = sb("QS", [P, B, H2, S], BF16)
        KS = sb("KS", [P, B, H, S], BF16)
        KC = sb("KC", [P, B, H, LCP], BF16)
        V1 = sb("V1", [P, B, T, H * VW])
        PT = sb("PT", [P, B, RING, S])
        PQ = sb("PQ", [P, B, 4, T * LC])
        stats = sb("stats", [P, B, T, 6])
        mv = sb("mv", [P, B, T, 2])
        veps = sb("veps", [P, B, T])
        rstd = sb("rstd", [P, B, T])
        xhat = sb("xhat", [P, B, T, C])
        hT = sb("hT", [P, B, S])
        mmax = sb("mmax", [P, B, T, H])
        mres = sb("mres", [P, B, T, H])
        mparts = sb("mparts", [P, B, T, 2, 3, H2], BF16)
        mT = sb("mT", [3 * H2, B, 2, S], BF16)
        junk = sb("junk", [P, 2, S], BF16)
        top = sb("top", [P, B, 2, T, 16])
        nbias = sb("nbias", [P, B, 2, T])
        left = sb("left", [P, B, 2, T, LC])
        rsum = sb("rsum", [P, B, T, H])
        ctx_mv = sb("ctx_mv", [LC, B, 2])
        ctx_stats = sb("ctx_stats", [LC, B, 6])
        ctx_veps = sb("ctx_veps", [LC, 2, B])
        ctx_rstd = sb("ctx_rstd", [LC, 2, B])
        work = sb("work", [P, B, 5, S])
        U = work[:, :, 0:NI, :]
        OG = work[:, :, 0:G, :]
        qkf = work[:, :, 0:2, :]
        parts = work[:, :, 2:5, :].rearrange("p b i s -> p b (i s)").bitcast(BF16)\
            .rearrange("p b (i n s) -> p b i n s", i=2, n=3)
        flat = xhat[:, :, :, :].rearrange("p b t c -> p b (t c)")
        res = flat
        gated = (work[:, :, NI, :], flat)
        On, OT = xhat, hT

        early, at = PT[:, :, :, :].rearrange("p b r n -> p (b r n)"), 0

        def cut(n):
            nonlocal at
            at += n
            return early[:, at - n:at]

        ada = cut(ADA_COLS)
        Wc = cut(CTX_COLS)
        ctxT = cut(3 * B * LC).rearrange("p (n b k) -> p n b k", n=3, b=B)
        ctx_hat = cut(2 * B * C)[0:LC].rearrange("p (n b c) -> p n b c", n=2, b=B)
        acts_wide = cut(2 * B * P).rearrange("p (k b n) -> p k b n", k=2, b=B)
        early, at = PQ[:, :, :, :].rearrange("p b a n -> p (b a n)"), 0
        rows = cut(ROWCOLS)
        wmask32 = cut(P)
        gate_row = mask_q[:, :, :].rearrange("p t s -> p (t s)").bitcast(F32)\
            .rearrange("p (i b c) -> p i b c", i=GATE_ROWS, b=B)
        raw = Wg[:, 0, :]
        mask_u8 = mask_k[:, :, :].rearrange("p t s -> p (t s)").bitcast(U8)[:, 0:T * S]
        ctx_k = junk[:, 0, :].bitcast(F32)[:, 0:B * LC]

        scores = [stack.enter_context(nc.psum_tensor(f"scores{i}", [P, S], F32)) for i in range(SCORES)]
        outputs = [stack.enter_context(nc.psum_tensor(f"outputs{b}", [P, S], F32)) for b in range(B)]
        banks = [stack.enter_context(nc.psum_tensor(f"bank{i}", [P, S], F32)) for i in range(BANKS)]

        s_small = sem("small_inputs_loaded")
        s_ada0 = sem("first_ada_loaded")
        s_ada = sem("ada_loaded")
        s_x = sem("x_loaded")
        s_w0 = sem("first_weights_loaded")
        s_ctx = sem("context_loaded")
        s_vrows = sem("value_biases_loaded")
        s_wc = sem("context_weights_loaded")
        s_w = sem("weights_loaded")
        s_raw = sem("raw_weights_loaded")
        s_late = sem("late_inputs_loaded")
        s_const = sem("constants_set")
        s_vset = sem("vector_constants_set")
        s_silu = sem("silu_done")
        s_wide = sem("conditioning_widened")
        s_cmask = sem("masks_made")
        s_vchain = sem("vector_step_done")
        s_pchain = sem("pool_step_done")
        s_zero = sem("key_stack_zeroed")
        s_czero = sem("context_stacks_zeroed")
        s_ones = [sem(f"ones_rows_placed{b}") for b in range(B)]
        s_qs = [sem(f"query_stack_placed{b}") for b in range(B)]
        s_ks = [sem(f"key_stack_placed{b}") for b in range(B)]
        s_kc = [sem(f"context_key_stack_placed{b}") for b in range(B)]
        s_ms = [sem(f"maximum_stack_placed{b}") for b in range(B)]
        s_out = sem("output_stored")

        filled = Count(sem("chain_bank_filled"), BANKED)
        emptied_by_vector = Count(sem("bank_emptied_by_vector"), [x for x in BANKED if reader(x) == "V"])
        emptied_by_scalar = Count(sem("bank_emptied_by_scalar"), [x for x in BANKED if reader(x) == "S"])
        lns = [x for x in CHAIN if x[0] == "ln"]
        ctx_at = len([x for x in CHAIN[:CHAIN.index(("cT",))] if x[0] == "ln"])
        lns[ctx_at:ctx_at] = [("ln", "ctx", 0), ("ln", "ctx", 1)]
        variance = Count(sem("variance_ready"), lns)
        rstd_ready = Count(sem("rstd_ready"), lns)
        normed = Count(sem("normed"), lns)
        firsts = [x for x in CHAIN if x[0] in ("q", "k", "ck") and reader(x) == "S"]
        first_part = Count(sem("first_part_made"), firsts)
        stacks = [x for x in CHAIN if x[0] == "stack"]
        rope_q = Count(sem("roped"), [x for x in CHAIN if x[0] in ("qs", "ks")])
        split_q = Count(sem("query_parts_made"), stacks)
        split_k = Count(sem("key_parts_made"), [x for x in stacks if x[1][0] in OWN_KEYS])
        split_c = Count(sem("context_key_parts_made"), [x for x in CHAIN if x[0] == "ck"])
        biased = Count(sem("output_bias_added"), [(x[1], w) for x in CHAIN for w in range(2)
                                                  if x[0] == "onT" and not w or x[0] == "ha" and w and not x[2]
                                                  if bias_row(x[1], w) is not None])
        weighted = Count(sem("matrix_gated"), [x for x in CHAIN if x[0] == "gate"])
        max_parts = Count(sem("maximum_parts_made"), [x for x in CHAIN if x[0] == "m"])
        top_found = Count(sem("top16_found"), [x for x in CHAIN if x[0] == "tk"])
        top_kept = Count(sem("top16_kept"), KEEPS)
        scored = Count(sem("scores_ready"), ITEMS)
        exped = Count(sem("probabilities_ready"), ITEMS)
        summed = Count(sem("values_summed"), [x for x in CHAIN if x[0] == "pv"])
        saved = Count(sem("outputs_saved"), [x for x in CHAIN if x[0] == "save"])

        def bank(x):
            return banks[BANK_NO[x] % BANKS]

        def free_bank(pe, x):
            n = BANK_NO[x]
            if n >= BANKS:
                last = BANKED[n - BANKS]
                if reader(last) == "V":
                    pe.wait_ge(emptied_by_vector.sem, emptied_by_vector[last])
                else:
                    pe.wait_ge(emptied_by_scalar.sem, emptied_by_scalar[last])
            return banks[n % BANKS]

        def w(name, i=0, n=C):
            at = W_AT[name][0] + i * n
            return W[:, at:at + n]

        def wc(name):
            return Wc[:, CTX_AT[name][0]:CTX_AT[name][0] + C]

        def col(name, i=0, n=1):
            at = COL_AT[name][0] + i
            return cols[:, at:at + n]

        def mods_of(x):
            return range(FIRST_MODS) if x == ("mod", 0) else range(FIRST_MODS, len(MODS))

        def heads(ap):
            return ap.rearrange("p (h v) -> p h v", v=VW)

        block = stack.enter_context(nc.Block())

        @block.sync
        def _(sp):
            sp.dma_start(cols[:, :], col_in).then_inc(s_small, 16)
            sp.dma_start(ident[:, :], ident_in).then_inc(s_small, 16)
            sp.dma_start(X[:, :, :], x_in.rearrange("b (t p) c -> p (b t) c", p=P)).then_inc(s_x, 16)
            sp.dma_start(ada[:, 0:ADA_FIRST], ada_in[:, 0:ADA_FIRST]).then_inc(s_ada0, 16)
            sp.dma_start(W[:, 0:W_FIRST], w_in[:, 0:W_FIRST]).then_inc(s_w0, 16)
            sp.dma_start(ctx[:, :, :], ctx_in.rearrange("b t c -> t b c")).then_inc(s_ctx, 16)
            sp.dma_start(vrows[:, :], vrow_in.partition_broadcast(P)).then_inc(s_vrows, 16)
            sp.dma_start(ada[:, ADA_FIRST:], ada_in[:, ADA_FIRST:]).then_inc(s_ada, 16)
            sp.dma_start(Wc, wc_in).then_inc(s_wc, 16)
            sp.dma_start(raw, raw_in).then_inc(s_raw, 16)
            sp.dma_start(rows, row_in.partition_broadcast(P)).then_inc(s_raw, 16)
            sp.wait_ge(s_const, 1)
            sp.wait_ge(s_czero, 1)
            for b in range(B):
                sp.wait_ge(s_zero, b + 1)
                for half in range(2):
                    r = QK_ROWS + 3 * half
                    sp.dma_start(KS[r:r + 3, b, half * H2:(half + 1) * H2, :],
                                 onesb[:, :].unsqueeze(1).broadcast_to([3, H2, S])).then_inc(s_ones[b], 16)
                    sp.dma_start(KC[r:r + 3, b, half * H2:(half + 1) * H2, 0:LC],
                                 onesb[:, 0:LC].unsqueeze(1).broadcast_to([3, H2, LC])).then_inc(s_ones[b], 16)
            sp.dma_start(mask_u8.rearrange("p (t s) -> p t s", t=T),
                         smask_in.rearrange("(t p) s -> p t s", p=P)).then_inc(s_late, 16)
            sp.dma_start(cmask_u8[:, :], cmask_in).then_inc(s_late, 16)
            sp.dma_start(wmask32, wmask_in).then_inc(s_late, 16)
            sp.dma_start(rope[:, :, :], rope_in).then_inc(s_late, 16)
            sp.dma_start(W[:, W_FIRST:], w_in[:, W_FIRST:]).then_inc(s_w, 16)

            def do(x):
                if x[0] == "kc":
                    s, b = x[1]
                    c = CTX_OF[s]
                    sp.wait_ge(split_c.sem, split_c[("ck", c)])
                    before = [u for u in UNITS[:UNITS.index((s, b))] if u[1] == b and u[0] in CTX_OF]
                    if before:
                        last = [y for y in ITEMS if y[1] == before[-1]][-1]
                        sp.wait_ge(scored.sem, scored[last])
                    for i, kp in enumerate(K_PART):
                        for half in range(2):
                            r = 2 * D * i + D * half
                            sp.dma_start(KC[r:r + D, b, half * H2:(half + 1) * H2, 0:LC],
                                         ctx_parts[64 * half:64 * half + 64, c, kp, b * LC:(b + 1) * LC])\
                              .then_inc(s_kc[b], 16)
                if x[0] == "stack":
                    s, b = x[1]

                    def move_keys(part):
                        for i in [i for i in range(len(K_PART)) if K_PART[i] == part]:
                            for half in range(2):
                                r = 2 * D * i + D * half
                                sp.dma_start(KS[r:r + D, b, half * H2:(half + 1) * H2, :],
                                             parts[64 * half:64 * half + 64, b, 1, part, :]).then_inc(s_ks[b], 16)

                    def move_queries(part):
                        for i in [i for i in range(len(Q_PART)) if Q_PART[i] == part]:
                            sp.dma_start(QS[2 * D * i:2 * D * (i + 1), b, :, :], parts[:, b, 0, part, :])\
                              .then_inc(s_qs[b], 16)

                    if s in OWN_KEYS:
                        if s == SELF2:
                            sp.wait_ge(split_k.sem, split_k[x])
                        else:
                            sp.wait_ge(first_part.sem, first_part[("k", x[1])])
                        move_keys(0)
                    if s == SELF2:
                        sp.wait_ge(split_q.sem, split_q[x])
                    else:
                        sp.wait_ge(first_part.sem, first_part[("q", x[1])])
                    move_queries(0)
                    sp.wait_ge(split_q.sem, split_q[x])
                    move_queries(1)
                    move_queries(2)
                    if s in OWN_KEYS:
                        sp.wait_ge(split_k.sem, split_k[x])
                        move_keys(1)
                        move_keys(2)
                if x[0] == "mT":
                    b, half = x[1][1], x[2]
                    r = QK_ROWS + 3 * half
                    sp.wait_ge(emptied_by_scalar.sem, emptied_by_scalar[x])
                    sp.dma_start(QS[r:r + 3, b, :, :], mT[:, b, half, :]).then_inc(s_ms[b], 16)
                if x[0] == "out":
                    b = x[1][1]
                    sp.wait_ge(emptied_by_vector.sem, emptied_by_vector[("proj", x[1])])
                    sp.dma_start(out.rearrange("b (t p) c -> p (b t) c", p=P)[:, b * T:(b + 1) * T, :],
                                 X[:, b * T:(b + 1) * T, :]).then_inc(s_out, 16)

            for x in CHAIN:
                do(x)
            sp.wait_ge(s_out, 16 * B)

        def key_moves(u):
            stages = OWN_KEYS if u[0] in OWN_KEYS else tuple(CTX_OF)
            return 16 * 12 * (stages.index(u[0]) + 1)

        def query_moves(u):
            return 16 * 6 * (u[0] + 1)

        def max_moves(u, half):
            return 16 * (2 * (u[0] - (u[0] > TOPK16)) + half + 1)

        @block.gpsimd
        def _(pool):
            chain = [0]

            def link(ins):
                chain[0] += 1
                ins.then_inc(s_pchain, 1)
                pool.wait_ge(s_pchain, chain[0])

            pool.memset(onesb[:, :], 1.0).then_inc(s_const, 1)
            pool.memset(KC[:, :, :, :], 0.0).then_inc(s_czero, 1)
            link(pool.memset(half_neg[:, :], -0.5))
            link(pool.memset(first_row[:, :], 0.0))
            pool.memset(first_row[0:1, :], 1.0).then_inc(s_const, 1)
            link(pool.memset(cmask[:, :, :], 0.0))
            pool.wait_ge(s_small, 32)
            pool.tensor_copy(identb[:, :], ident[:, :]).then_inc(s_const, 1)

            def do(x):
                if x[0] == "ln":
                    (s, b), which = x[1:]
                    pool.wait_ge(variance.sem, variance[x])
                    pool.tensor_tensor(rstd[:, b, :], veps[:, b, :], half_neg[:, :], ALU.pow)\
                        .then_inc(rstd_ready.sem, 1)
                if x[0] == "onT" or (x[0] == "ha" and x[2] == 0):
                    (s, b), which = x[1], int(x[0] == "ha")
                    row = bias_row(x[1], which)
                    if row is not None:
                        if x == ("onT", (CROSS0, 0)):
                            pool.wait_ge(s_vrows, 16)
                        if row in ("cp0", "p3"):
                            at = VROW_AT[row][0]
                            row = vrows[:, at:at + C]
                        else:
                            pool.wait_ge(weighted.sem, weighted[("gate", row)])
                            row = rowg[:, BIASED.index(row), b, :]
                        pool.wait_ge(normed.sem, normed[("ln", (s, b), which)])
                        xs = X[:, b * T:(b + 1) * T, :]
                        pool.tensor_tensor(xs, xs, row.unsqueeze(1).broadcast_to([P, T, C]), ALU.add)\
                            .then_inc(biased.sem, 1)
                if x[0] == "stack" and x[1][0] in OWN_KEYS:
                    s, b = x[1]
                    f, p = qkf[:, b, 1, :], parts[:, b, 1]
                    if s == SELF2:
                        pool.wait_ge(rope_q.sem, rope_q[("ks", x[1])])
                        link(pool.tensor_copy(p[:, 0, :], f))
                    else:
                        pool.wait_ge(emptied_by_scalar.sem, emptied_by_scalar[("k", x[1])])
                    link(pool.tensor_tensor(f, f, p[:, 0, :], ALU.subtract))
                    link(pool.tensor_copy(p[:, 1, :], f))
                    pool.tensor_tensor(p[:, 2, :], f, p[:, 1, :], ALU.subtract).then_inc(split_k.sem, 1)
                if x[0] == "gate":
                    i = x[1]
                    n, at, g = GATED[i][2], RAW_AT[i][0], gate_row[:, i % GATE_ROWS]
                    pool.wait_ge(emptied_by_vector.sem, emptied_by_vector[x])
                    if i in BIASED:
                        o = ROW_AT["out"][0] + BIASED.index(i) * C
                        pool.tensor_tensor(rowg[:, BIASED.index(i)], g,
                                           rows[:, o:o + C].unsqueeze(1).broadcast_to([P, B, C]), ALU.mult)
                    for b in (1, 0):
                        ins = pool.tensor_tensor(Wg[:, b, at:at + n * C].rearrange("p (n c) -> p n c", n=n),
                                                 g[:, b, :].unsqueeze(1).broadcast_to([P, n, C]),
                                                 raw[:, at:at + n * C].rearrange("p (n c) -> p n c", n=n), ALU.mult)
                    ins.then_inc(weighted.sem, 1)
                if x[0] == "cT":
                    for n in range(2):
                        pool.wait_ge(variance.sem, variance[("ln", "ctx", n)])
                        pool.tensor_tensor(ctx_rstd[:, n, :], ctx_veps[:, n, :], half_neg[0:LC, 0:B], ALU.pow)\
                            .then_inc(rstd_ready.sem, 1)
                if x == ("mask", 0):
                    pool.wait_ge(s_late, 64)
                    pool.wait_ge(weighted.sem, weighted[("gate", len(GATED) - 1)])
                    pool.tensor_copy(wmask[:, :], wmask32).then_inc(s_cmask, 1)
                    pool.tensor_scalar(mask_q[:, :, :], mask_u8.rearrange("p (t s) -> p t s", t=T), -1.0, -NEG,
                                       ALU.add, ALU.mult).then_inc(s_cmask, 1)
                    pool.tensor_scalar(cmask[0:1, :, 0:LC], cmask_u8.rearrange("p (b k) -> p b k", b=B),
                                       -1.0, -NEG, ALU.add, ALU.mult).then_inc(s_cmask, 1)

            for x in CHAIN:
                do(x)

        @block.scalar
        def _(act):
            act.wait_ge(s_small, 32)
            act.activation(acts[:, 1, :], col("cond", 0, B), ACT.Silu).then_inc(s_silu, 1)

            def two_parts(src, f, part, bias):
                for to, done in ((part, first_part), (f, emptied_by_scalar)):
                    if bias is None:
                        act.activation(to, src, ACT.Copy).then_inc(done.sem, 1)
                    else:
                        act.activation(to, src, ACT.Identity, bias=bias).then_inc(done.sem, 1)

            def exponentials(x):
                n, (s, b) = ITEM_NO[x], x[1]
                own = OWN_NO[x]
                keys = P if s in OWN_KEYS else LC if s == TOPK16 else LCP
                if own >= RING:
                    last = OWN_ITEMS[b][own - RING]
                    act.wait_ge(summed.sem, summed[("pv",) + last[1:4]])
                elif own == 0:
                    act.wait_ge(emptied_by_vector.sem, emptied_by_vector[("gate", len(GATED) - 1)])
                act.wait_ge(scored.sem, scored[x])
                to = PT[0:keys, b, own % RING, :]
                if s == TOPK16:
                    act.activation(to, scores[n % SCORES][0:keys, :], ACT.Copy).then_inc(exped.sem, 1)
                else:
                    act.activation(to, scores[n % SCORES][0:keys, :], ACT.Exp, scale=SCALE).then_inc(exped.sem, 1)

            def do(x):
                if x[0] == "ex":
                    exponentials(x)
                if x[0] == "save":
                    (s, b), g = x[1:]
                    act.wait_ge(summed.sem, summed[("pv", x[1], g, T - 1 if s in FULL else 0)])
                    if s and g == 0:
                        act.wait_ge(filled.sem, filled[("oT", (s - 1, b), T - 1)])
                    act.copy(OG[:, b, g, :], outputs[b][:, :]).then_inc(saved.sem, 1)
                if x[0] in NO_BANK or reader(x) != "S":
                    return
                empty = emptied_by_scalar.sem
                act.wait_ge(filled.sem, filled[x])
                src = bank(x)
                if x[0] == "hT":
                    (s, b), which = x[1:]
                    mod = MOD_OF.get((s, which))
                    if mod is not None:
                        made = ("mod", 0 if mod < FIRST_MODS else 1)
                        act.wait_ge(emptied_by_vector.sem, emptied_by_vector[made])
                    runs = [(0, 0, S)]
                    if s == WINDOW:
                        runs = [(0, SHIFT, S - SHIFT), (S - SHIFT, 0, SHIFT)]
                    for to, at, n in runs:
                        if mod is None:
                            ins = act.activation(hT[:, b, to:to + n], src[:, at:at + n], ACT.Copy)
                        else:
                            ins = act.activation(hT[:, b, to:to + n], src[:, at:at + n], ACT.Identity,
                                                 bias=M[:, mod, 0, b:b + 1], scale=M[:, mod, 1, b:b + 1])
                    ins.then_inc(empty, 1)
                if x[0] in ("q", "k"):
                    s, b = x[1]
                    i = "qk".index(x[0])
                    name = f"{x[0]}{LAYER[s]}" if s in OWN_KEYS else f"qc{LAYER[s]}"
                    two_parts(src[:, :], qkf[:, b, i, :], parts[:, b, i, 0, :], None if s == CROSS2 else col(name))
                if x[0] == "ck":
                    c = x[1]
                    if c:
                        act.wait_ge(split_c.sem, split_c[("ck", c - 1)])
                    two_parts(src[:, 0:B * LC], ctx_k, ctx_parts[:, c, 0, :],
                              None if c == 2 else col(f"kc{c}"))
                if x[0] == "mask":
                    act.copy(mask_k[:, x[1], :], src[:, :].bitcast(BF16)[:, 0:S]).then_inc(empty, 1)
                if x[0] == "mT":
                    act.copy(mT[:, x[1][1], x[2], :], src[0:3 * H2, :].bitcast(BF16)[:, 0:S]).then_inc(empty, 1)
                if x[0] == "tk":
                    (s, b), h = x[1:]
                    act.wait_ge(top_found.sem, top_found[x])
                    if h == 0:
                        act.wait_ge(weighted.sem, weighted[("gate", len(GATED) - 1)])
                    if h >= 4:
                        last = ("ex", x[1], (h - 4) // HG, 0, h % HG)
                        act.wait_ge(scored.sem, scored[last])
                    for t in range(T):
                        ins = act.activation(PQ[:, b, h % 4, t * LC:(t + 1) * LC], src[:, t * LC:(t + 1) * LC],
                                             ACT.Exp, bias=nbias[:, b, h % 2, t:t + 1], scale=SCALE)
                    ins.then_inc(empty, 1)
                if x[0] == "onT":
                    s, b = x[1]
                    if s == WINDOW:
                        act.copy(OT[:, b, SHIFT:S], src[:, 0:S - SHIFT])
                        act.copy(OT[:, b, 0:SHIFT], src[:, S - SHIFT:S]).then_inc(empty, 1)
                    else:
                        act.copy(OT[:, b, :], src[:, :]).then_inc(empty, 1)
                if x[0] == "ha":
                    (s, b), i = x[1:]
                    if LAYER[s] == 1:
                        if i >= 2:
                            act.wait_ge(emptied_by_vector.sem, emptied_by_vector[("hb", x[1], i - 2)])
                        act.activation(gated[i % 2][:, b, :], src[:, :], ACT.Silu, bias=col("up1a", i))\
                           .then_inc(empty, 1)
                    else:
                        act.activation(U[:, b, i, :], src[:, :], ACT.Gelu_apprx_tanh,
                                       bias=col(f"up{LAYER[s]}", i)).then_inc(empty, 1)

            for x in CHAIN:
                do(x)

        @block.vector
        def _(dve):
            chain = [0]

            def link(ins):
                chain[0] += 1
                ins.then_inc(s_vchain, 1)
                dve.wait_ge(s_vchain, chain[0])

            dve.memset(KS[:, 0, :, :], 0.0).then_inc(s_zero, 1)
            dve.wait_ge(s_silu, 1)
            link(dve.tensor_copy(acts[:, 0, :], col("cond", 0, B)))
            dve.tensor_copy(acts_wide.rearrange("p k b n -> p (k b) n"),
                            acts[:, :, :].rearrange("p k b -> p (k b)").unsqueeze(2).broadcast_to([P, 2 * B, P]))\
               .then_inc(s_wide, 1)
            link(dve.memset(V1[:, :, :, :], 1.0))
            for b in range(B):
                dve.memset(outputs[b][:, :], 0.0).then_inc(s_vset, 1)
            dve.memset(KS[:, 1, :, :], 0.0).then_inc(s_zero, 1)

            def norm(src, tiles, n, eps, stat, mean, v, r, to, x):
                for t in range(tiles):
                    chain[0] += 1
                    dve.bn_stats(stat[0:n, t, :], src(t)).then_inc(s_vchain, 1)
                dve.wait_ge(s_vchain, chain[0])
                for t in range(tiles):
                    chain[0] += 1
                    dve.bn_aggr(mean[0:n, t, :], stat[0:n, t, :]).then_inc(s_vchain, 1)
                dve.wait_ge(s_vchain, chain[0])
                dve.tensor_scalar(v, mean[0:n, 0:tiles, 1], eps, None, ALU.add).then_inc(variance.sem, 1)
                dve.wait_ge(rstd_ready.sem, rstd_ready[x])
                for t in range(tiles):
                    ins = dve.tensor_scalar(to(t), src(t), mean[0:n, t, 0:1], r[:, t:t + 1], ALU.subtract, ALU.mult)
                ins.then_inc(normed.sem, 1)

            def split(f, p, done):
                link(dve.tensor_tensor(f, f, p[:, 0], ALU.subtract))
                link(dve.tensor_copy(p[:, 1], f))
                dve.tensor_tensor(p[:, 2], f, p[:, 1], ALU.subtract).then_inc(done.sem, 1)

            second = {}

            def second_match(u, h):
                best, rest = top[:, u[1], h % 2], left[:, u[1], h % 2]
                dve.wait_ge(s_vchain, second[("tk", u, h)])
                for t in range(T):
                    chain[0] += 1
                    dve.match_replace(rest[:, t, :], best[:, t, 8:16], rest[:, t, :], NEG).then_inc(s_vchain, 1)

            def keep_top(u, h):
                b = u[1]
                dve.wait_ge(emptied_by_scalar.sem, emptied_by_scalar[("tk", u, h)])
                dve.scalar_tensor_tensor(out=PQ[:, b, h % 4, :], in0=left[:, b, h % 2].rearrange("p t k -> p (t k)"),
                                         scalar=NEG, in1=PQ[:, b, h % 4, :], op0=ALU.is_le, op1=ALU.mult)\
                   .then_inc(top_kept.sem, 1)

            def do(x):
                name = x[0]
                empty = emptied_by_vector.sem
                if name == "ln":
                    (s, b), which = x[1:]
                    if which:
                        dve.wait_ge(emptied_by_vector.sem, emptied_by_vector[("proj", x[1])])
                    elif s > 0:
                        before = ("down" if s - 1 in MLP_AFTER else "proj", (s - 1, b))
                        dve.wait_ge(emptied_by_vector.sem, emptied_by_vector[before])
                    else:
                        dve.wait_ge(s_x, 16)
                    norm(lambda t: X[:, b * T + t, :], T, P, LN_EPS[LAYER[s]], stats[:, b], mv[:, b],
                         veps[:, b, :], rstd[:, b, :], lambda t: xhat[:, b, t, :], x)
                if name == "stack":
                    s, b = x[1]
                    if s == SELF2:
                        dve.wait_ge(rope_q.sem, rope_q[("qs", x[1])])
                        link(dve.tensor_copy(parts[:, b, 0, 0, :], qkf[:, b, 0, :]))
                    else:
                        dve.wait_ge(emptied_by_scalar.sem, emptied_by_scalar[("q", x[1])])
                    split(qkf[:, b, 0, :], parts[:, b, 0], split_q)
                if name == "m":
                    (s, b), half = x[1:]
                    heads_ = slice(half * H2, (half + 1) * H2)
                    last = ("mx", x[1], half * H2 + H2 - 1, T - 1 if s in FULL else 0)
                    dve.wait_ge(emptied_by_vector.sem, emptied_by_vector[last])
                    best, rest = mmax[:, b, :, heads_], mres[:, b, :, heads_]
                    part = [mparts[:, b, :, half, n, :] for n in range(3)]
                    link(dve.tensor_scalar(part[0], best, -1.0, None, ALU.mult))
                    link(dve.scalar_tensor_tensor(out=rest, in0=best, scalar=-1.0, in1=part[0], op0=ALU.mult,
                                                  op1=ALU.subtract))
                    link(dve.tensor_copy(part[1], rest))
                    dve.tensor_tensor(part[2], rest, part[1], ALU.subtract).then_inc(max_parts.sem, 1)
                if name == "tkend":
                    second_match(x[1], H - 1)
                    dve.wait_ge(s_vchain, chain[0])
                    keep_top(x[1], H - 1)
                if name == "cT":
                    dve.wait_ge(s_ctx, 16)
                    for n, eps in enumerate((LN_EPS[0], LN_EPS[3])):
                        norm(lambda t: ctx[:, t, :], B, LC, eps, ctx_stats, ctx_mv, ctx_veps[:, n, :],
                             ctx_rstd[:, n, :], lambda t: ctx_hat[:, n, t, :], ("ln", "ctx", n))
                if name == "ck":
                    dve.wait_ge(emptied_by_scalar.sem, emptied_by_scalar[x])
                    split(ctx_k, ctx_parts[:, x[1]], split_c)
                if name in NO_BANK or (reader(x) != "V" and name != "tk"):
                    return
                dve.wait_ge(filled.sem, filled[x])
                src = bank(x)
                if name == "mod":
                    i, n = mods_of(x)[0], len(mods_of(x))
                    bias = col("mod", 2 * i, 2 * n)
                    link(dve.tensor_tensor(M[:, i:i + n, :, :].rearrange("p m k b -> p (m k) b"),
                                           src[:, 2 * i * B:2 * (i + n) * B].rearrange("p (m b) -> p m b", b=B),
                                           bias.unsqueeze(2).broadcast_to([P, 2 * n, B]), ALU.add))
                    if x[1] == 0:
                        dve.tensor_scalar(M[:, i:i + n, 1, :], M[:, i:i + n, 1, :], 1.0, None, ALU.add)\
                           .then_inc(empty, 1)
                        return
                    link(dve.tensor_scalar(M[:, i:i + n, 1, :], M[:, i:i + n, 1, :], 1.0, None, ALU.add))
                    dve.tensor_tensor(M[:, 5:8, 1, :], M[:, 5:8, 1, :],
                                      col("norm", 0, 3).unsqueeze(2).broadcast_to([P, 3, B]),
                                      ALU.mult).then_inc(empty, 1)
                    link(dve.memset(ctx_V[:, :, :, :], 0.0))
                    link(dve.memset(ctx_V[0:LC, :, :, :], 1.0))
                if name == "v":
                    s, b = x[1]
                    to = heads(V1[:, b].rearrange("p t n -> p (t n)"))[:, :, 0:D]
                    frm = src[:, :].rearrange("p (n d) -> p n d", d=D)
                    if s == SELF2:
                        dve.tensor_copy(to, frm).then_inc(empty, 1)
                    else:
                        if x[1] == UNITS[0]:
                            dve.wait_ge(s_vrows, 16)
                        at = VROW_AT[f"v{LAYER[s]}"][0]
                        bias = vrows[:, at:at + C].rearrange("p (h d) -> p h d", d=D)
                        for t in range(T):
                            ins = dve.tensor_tensor(to[:, t * H:(t + 1) * H, :], frm[:, t * H:(t + 1) * H, :],
                                                    bias, ALU.add)
                        ins.then_inc(empty, 1)
                if name in ("q", "qs", "k", "ks"):
                    b = x[1][1]
                    i = "qk".index(name[0])
                    if x == ("k", (SELF2, 0)):
                        dve.wait_ge(s_late, 64)
                    if name == "qs":
                        dve.wait_ge(rope_q.sem, rope_q[("ks", x[1])])
                    table = rope[:, len(name) - 1, :].unsqueeze(1).broadcast_to([P, 2, S // 2])
                    to = qkf[:, b, i, :] if len(name) == 1 else res[:, b, :]
                    dve.tensor_tensor(to.rearrange("p (n s) -> p n s", n=2),
                                      src[:, :].rearrange("p (n s) -> p n s", n=2), table, ALU.mult)\
                       .then_inc(empty, 1)
                    if len(name) == 2:
                        dve.wait_ge(emptied_by_vector.sem, emptied_by_vector[x])
                        dve.tensor_tensor(qkf[:, b, i, :], qkf[:, b, i, :], res[:, b, :], ALU.add)\
                           .then_inc(rope_q.sem, 1)
                if name == "mx":
                    (s, b), h, t = x[1:]
                    if s == SELF0:
                        dve.tensor_reduce(mmax[:, b, t, h:h + 1], src[:, :], AX, ALU.max).then_inc(empty, 1)
                    elif s == SELF2:
                        n = MASKED_MAXIMA.index(x)
                        if n >= 2:
                            dve.wait_ge(emptied_by_vector.sem, emptied_by_vector[MASKED_MAXIMA[n - 2]])
                        dve.tensor_tensor_reduce(junk[:, n % 2, :], src[:, :], mask_q[:, t, :], 1.0, NEG, ALU.add,
                                                 ALU.max, mmax[:, b, t, h:h + 1]).then_inc(empty, 1)
                    else:
                        n = P if s == WINDOW else LC
                        dve.tensor_reduce(mmax[:, b, :, h:h + 1], src[:, 0:T * n].rearrange("p (t k) -> p t k", t=T),
                                          AX, ALU.max).then_inc(empty, 1)
                if name == "tk":
                    u, h = x[1:]
                    b, a = u[1], h % 2
                    if h >= 2:
                        dve.wait_ge(top_kept.sem, top_kept[("tk", u, h - 2)])
                    tile = [src[:, t * LC:(t + 1) * LC] for t in range(T)]
                    best, rest = top[:, b, a], left[:, b, a]
                    for t in range(T):
                        chain[0] += 1
                        dve.max(best[:, t, 0:8], tile[t]).then_inc(s_vchain, 1)
                    first = chain[0]
                    if h:
                        second_match(u, h - 1)
                    matched = chain[0]
                    dve.wait_ge(s_vchain, first)
                    for t in range(T):
                        chain[0] += 1
                        dve.match_replace(rest[:, t, :], best[:, t, 0:8], tile[t], NEG).then_inc(s_vchain, 1)
                    replaced = chain[0]
                    if h:
                        dve.wait_ge(s_vchain, matched)
                        keep_top(u, h - 1)
                    dve.wait_ge(s_vchain, replaced)
                    dve.tensor_scalar(nbias[:, b, a, :], best[:, :, 0], -SCALE, None, ALU.mult)\
                       .then_inc(top_found.sem, 1)
                    for t in range(T):
                        chain[0] += 1
                        dve.max(best[:, t, 8:16], rest[:, t, :]).then_inc(s_vchain, 1)
                    second[x] = chain[0]
                if name == "oT":
                    b, t = x[1][1], x[2]
                    v = src[:, :].rearrange("p (h r) -> p h r", r=P // HG)
                    link(dve.reciprocal(rsum[:, b, t, :], v[:, :, D]))
                    dve.tensor_tensor(On[:, b, t, :].rearrange("p (h d) -> p h d", d=D), v[:, :, 0:D],
                                      rsum[:, b, t, :].unsqueeze(2).broadcast_to([P, H, D]), ALU.mult)\
                       .then_inc(empty, 1)
                if name in ("proj", "down"):
                    b, which = x[1][1], int(name == "down")
                    if bias_row(x[1], which) is not None:
                        dve.wait_ge(biased.sem, biased[(x[1], which)])
                    xs = X[:, b * T:(b + 1) * T, :].rearrange("p t c -> p (t c)")
                    dve.tensor_tensor(xs, src[:, :], xs, ALU.add).then_inc(empty, 1)
                if name == "hb":
                    (s, b), i = x[1:]
                    dve.wait_ge(emptied_by_scalar.sem, emptied_by_scalar[("ha", x[1], i)])
                    dve.scalar_tensor_tensor(out=U[:, b, i, :], in0=src[:, :], scalar=col("up1b", i),
                                             in1=gated[i % 2][:, b, :], op0=ALU.add, op1=ALU.mult).then_inc(empty, 1)
                if name == "cT":
                    cs = src[:, 0:2 * B * LC].rearrange("p (n b k) -> p n b k", n=2, b=B)
                    link(dve.tensor_copy(ctxT[:, 0:2], cs))
                    for b in range(B):
                        ins = dve.tensor_scalar(ctxT[:, 2, b, :], src[:, (2 * B + b) * LC:(2 * B + b + 1) * LC],
                                                M[:, MOD_KV3, 1, b:b + 1], M[:, MOD_KV3, 0, b:b + 1],
                                                ALU.mult, ALU.add)
                    ins.then_inc(empty, 1)
                if name == "cv":
                    c = x[1]
                    to = heads(ctx_V[0:LC, c].rearrange("p b n -> p (b n)"))[:, :, 0:D]
                    frm = src[0:LC, 0:B * C].rearrange("p (n d) -> p n d", d=D)
                    if c == 2:
                        dve.tensor_copy(to, frm).then_inc(empty, 1)
                    else:
                        at = VROW_AT[f"vc{c}"][0]
                        bias = vrows[0:LC, at:at + C].rearrange("p (h d) -> p h d", d=D)
                        for b in range(B):
                            ins = dve.tensor_tensor(to[:, b * H:(b + 1) * H, :], frm[:, b * H:(b + 1) * H, :], bias,
                                                    ALU.add)
                        ins.then_inc(empty, 1)
                if name == "gate":
                    i = x[1]
                    o = ROW_AT["gate"][0] + i * C
                    if i == 0:
                        dve.wait_ge(s_raw, 32)
                    if i >= GATE_ROWS:
                        dve.wait_ge(weighted.sem, weighted[("gate", i - GATE_ROWS)])
                    g = gate_row[:, i % GATE_ROWS]
                    dve.tensor_tensor(g, src[:, 0:B * C].rearrange("p (b c) -> p b c", b=B),
                                      rows[:, o:o + C].unsqueeze(1).broadcast_to([P, B, C]), ALU.add)\
                       .then_inc(empty, 1)

            for x in CHAIN:
                do(x)

        @block.tensor
        def _(pe):
            def turn(to, frm, eye, n):
                return pe.matmul(to, frm, eye[0:n, 0:n], start=True, stop=True, is_transpose=True)

            def queries(b, h, rows_, at=0, n=S):
                return QS[0:rows_, b, h % H2, at:at + n]

            def stacks_placed(u):
                pe.wait_ge(s_qs[u[1]], query_moves(u))
                if u[0] in OWN_KEYS:
                    pe.wait_ge(s_ks[u[1]], key_moves(u))
                else:
                    pe.wait_ge(s_kc[u[1]], key_moves(u))

            def piece(x):
                name = x[0]
                to = free_bank(pe, x)
                if name == "mod":
                    pe.wait_ge(s_wide, 1)
                    if x[1]:
                        pe.wait_ge(s_ada, 16)
                    else:
                        pe.wait_ge(s_ada0, 16)
                    for i in mods_of(x):
                        layer, *chunks = MODS[i]
                        for j, chunk in enumerate(chunks):
                            at = ADA_AT[layer][0] + chunk * C
                            n = 2 * i + j
                            ins = pe.matmul(to[:, n * B:(n + 1) * B], ada[:, at:at + C],
                                            acts[:, 0 if layer == 2 else 1, :], start=True, stop=True)
                if name == "hT":
                    b = x[1][1]
                    pe.wait_ge(normed.sem, normed[("ln",) + x[1:]])
                    if x[1] == UNITS[0]:
                        pe.wait_ge(s_small, 32)
                    for t in range(T):
                        ins = turn(to[:, t * P:(t + 1) * P], xhat[:, b, t, :], ident, P)
                if name in ("q", "k", "qs", "ks"):
                    s, b = x[1]
                    pe.wait_ge(emptied_by_scalar.sem, emptied_by_scalar[("hT", x[1], 0)])
                    if x[1] == UNITS[0]:
                        pe.wait_ge(s_w0, 16)
                    if x[1] == (CROSS0, 0):
                        pe.wait_ge(s_w, 16)
                    wname = f"{name[0]}{LAYER[s]}{name[1:]}" if s in OWN_KEYS else f"qc{LAYER[s]}"
                    ins = pe.matmul(to[:, :], w(wname), hT[:, b, :], start=True, stop=True)
                if name == "v":
                    s, b = x[1]
                    for t in range(T):
                        ins = pe.matmul(to[:, t * C:(t + 1) * C], hT[:, b, t * P:(t + 1) * P], w(f"v{LAYER[s]}"),
                                        start=True, stop=True)
                if name == "mx":
                    (s, b), h, t = x[1:]
                    if h + t == 0:
                        stacks_placed(x[1])
                        pe.wait_ge(s_const, 3)
                    if s in FULL:
                        ins = pe.matmul(to[:, :], queries(b, h, QK_ROWS, t * P, P), KS[0:QK_ROWS, b, h, :],
                                        start=True, stop=True)
                    else:
                        n = P if s == WINDOW else LC
                        masked = s in (WINDOW, CROSS2)
                        tiles = to[:, 0:T * n].rearrange("p (t k) -> p t k", t=T)
                        if s == WINDOW:
                            pe.matmul(tiles, identb[:, :], wmask[:, :].unsqueeze(1).broadcast_to([P, T, P]),
                                      start=True, stop=False, skip_group_check=True)
                        if s == CROSS2:
                            pe.matmul(tiles, first_row[:, 0:P], cmask[:, b, 0:LC].unsqueeze(1).broadcast_to([P, T, LC]),
                                      start=True, stop=False, skip_group_check=True)
                        for i in range(T):
                            keys = KS[0:QK_ROWS, b, h, i * P:(i + 1) * P] if s == WINDOW else KC[0:QK_ROWS, b, h, 0:LC]
                            ins = pe.matmul(to[:, i * n:(i + 1) * n], queries(b, h, QK_ROWS, i * P, P), keys,
                                            start=not masked, stop=True, skip_group_check=masked)
                if name == "tk":
                    u, h = x[1:]
                    if h == 0:
                        stacks_placed(u)
                    for i in range(T):
                        ins = pe.matmul(to[:, i * LC:(i + 1) * LC], queries(u[1], h, QK_ROWS, i * P, P),
                                        KC[0:QK_ROWS, u[1], h, 0:LC], start=True, stop=True)
                if name == "mT":
                    b, half = x[1][1], x[2]
                    pe.wait_ge(max_parts.sem, max_parts[("m", x[1], half)])
                    tb = to[:, :].bitcast(BF16)
                    for t in range(T):
                        ins = turn(tb[0:3 * H2, t * P:(t + 1) * P],
                                   mparts[:, b, t, half].rearrange("p n h -> p (n h)"), identb, P)
                if name == "oT":
                    u, t = x[1:]
                    pe.wait_ge(saved.sem, saved[("save", u, G - 1)])
                    for g in range(G):
                        ins = turn(to[:, g * P:(g + 1) * P], OG[:, u[1], g, t * P:(t + 1) * P], ident, P)
                if name == "onT":
                    pe.wait_ge(emptied_by_vector.sem, emptied_by_vector[("oT", x[1], T - 1)])
                    for t in range(T):
                        ins = turn(to[:, t * P:(t + 1) * P], On[:, x[1][1], t, :], ident, P)
                if name == "proj":
                    s, b = x[1]
                    pe.wait_ge(emptied_by_scalar.sem, emptied_by_scalar[("onT", x[1])])
                    i = GATE_OF.get((s, 0))
                    if i is None:
                        matrix = w("cp0" if s == CROSS0 else "p3")
                    else:
                        pe.wait_ge(weighted.sem, weighted[("gate", i)])
                        matrix = Wg[:, b, RAW_AT[i][0]:RAW_AT[i][0] + C]
                    for t in range(T):
                        ins = pe.matmul(to[:, t * C:(t + 1) * C], OT[:, b, t * P:(t + 1) * P], matrix,
                                        start=True, stop=True)
                if name in ("ha", "hb"):
                    (s, b), i = x[1:]
                    pe.wait_ge(emptied_by_scalar.sem, emptied_by_scalar[("hT", x[1], 1)])
                    wname = f"up{LAYER[s]}" + (name[1] if LAYER[s] == 1 else "")
                    ins = pe.matmul(to[:, :], w(wname, i), hT[:, b, :], start=True, stop=True)
                if name == "down":
                    s, b = x[1]
                    if LAYER[s] == 1:
                        pe.wait_ge(emptied_by_vector.sem, emptied_by_vector[("hb", x[1], NI - 1)])
                    else:
                        pe.wait_ge(emptied_by_scalar.sem, emptied_by_scalar[("ha", x[1], NI - 1)])
                    at = RAW_AT[GATE_OF[(s, 1)]][0]
                    pe.wait_ge(weighted.sem, weighted[("gate", GATE_OF[(s, 1)])])
                    for t in range(T):
                        for n in range(NI):
                            ins = pe.matmul(to[:, t * C:(t + 1) * C], U[:, b, n, t * P:(t + 1) * P],
                                            Wg[:, b, at + n * C:at + (n + 1) * C], start=n == 0, stop=n == NI - 1)
                if name == "cT":
                    pe.wait_ge(normed.sem, normed[("ln", "ctx", 1)])
                    for n in range(3):
                        for b in range(B):
                            frm = ctx[:, b, :] if n == 0 else ctx_hat[:, n - 1, b, :]
                            ins = turn(to[:, (n * B + b) * LC:(n * B + b + 1) * LC], frm, ident, LC)
                if name == "ck":
                    pe.wait_ge(emptied_by_vector.sem, emptied_by_vector[("cT",)])
                    pe.wait_ge(s_wc, 16)
                    src = ctxT[:, (1, 0, 0, 2)[x[1]]].rearrange("p b k -> p (b k)")
                    ins = pe.matmul(to[:, 0:B * LC], wc(f"kc{x[1]}"), src, start=True, stop=True)
                if name == "cv":
                    c = x[1]
                    for b in range(B):
                        ins = pe.matmul(to[0:LC, b * C:(b + 1) * C], ctxT[:, (1, 0, 0, 2)[c], b, :], wc(f"vc{c}"),
                                        start=True, stop=True)
                if name == "gate":
                    layer, chunk = GATED[x[1]][:2]
                    at = ADA_AT[layer][0] + chunk * C
                    for b in range(B):
                        ins = pe.matmul(to[:, b * C:(b + 1) * C], acts_wide[:, 0 if layer == 2 else 1, b, :],
                                        ada[:, at:at + C], start=True, stop=True)
                if name == "mask":
                    kt = x[1]
                    pe.wait_ge(s_cmask, 3)
                    tb = to[:, :].bitcast(BF16)
                    for t in range(T):
                        ins = turn(tb[:, t * P:(t + 1) * P], mask_q[:, t, kt * P:(kt + 1) * P], identb, P)
                ins.then_inc(filled.sem, 1)

            def score(x):
                u, g, kt, j = x[1:]
                (s, b), h, n = u, g * HG + j, ITEM_NO[x]
                if n >= SCORES:
                    pe.wait_ge(exped.sem, exped[ITEMS[n - SCORES]])
                to = scores[n % SCORES]
                half = h // H2
                if s != TOPK16 and h % H2 + kt == 0:
                    pe.wait_ge(s_ms[b], max_moves(u, half))
                    if s == SELF0:
                        pe.wait_ge(s_ones[b], 16 * 4)
                rows_ = QK_ROWS + 3 * (half + 1)
                q = queries(b, h, rows_)
                if s in FULL:
                    if s == SELF2:
                        pe.matmul(to[:, :], identb[:, :], mask_k[:, kt, :], start=True, stop=False)
                    ins = pe.matmul(to[:, :], KS[0:rows_, b, h, kt * P:(kt + 1) * P], q, start=s == SELF0, stop=True)
                if s == WINDOW:
                    pe.matmul(to[:, :].rearrange("p (t k) -> p t k", t=T), identb[:, :],
                              wmask[:, :].unsqueeze(1).broadcast_to([P, T, P]), start=True, stop=False,
                              skip_group_check=True)
                    for t in range(T):
                        c = slice(t * P, (t + 1) * P)
                        ins = pe.matmul(to[:, c], KS[0:rows_, b, h, c], q[:, c], start=False, stop=True,
                                        skip_group_check=True)
                if s in (CROSS0, CROSS2, CROSS3):
                    if s == CROSS2:
                        pe.matmul(to[0:LCP, :], cmask[:, b, :], first_row[:, :], start=True, stop=False)
                    ins = pe.matmul(to[0:LCP, :], KC[0:rows_, b, h, :], q, start=s != CROSS2, stop=True)
                if s == TOPK16:
                    pe.wait_ge(top_kept.sem, top_kept[("tk", u, h)])
                    for t in range(T):
                        ins = turn(to[0:LC, t * P:(t + 1) * P], PQ[:, b, h % 4, t * LC:(t + 1) * LC], ident, P)
                ins.then_inc(scored.sem, 1)

            def sum_values(x):
                u, g, kt = x[1:]
                s, b = u
                to = outputs[b]
                pe.wait_ge(exped.sem, exped[("ex", u, g, kt, HG - 1)])
                if kt == 0:
                    at = SAVES[b].index(("save", u, g))
                    if at:
                        pe.wait_ge(saved.sem, saved[SAVES[b][at - 1]])
                    else:
                        pe.wait_ge(s_vset, B)
                    if s in OWN_KEYS:
                        pe.wait_ge(emptied_by_vector.sem, emptied_by_vector[("v", u)])
                if s == WINDOW:
                    for t in range(T):
                        c = slice(t * P, (t + 1) * P)
                        for j in range(HG):
                            h, slot = g * HG + j, OWN_NO[("ex", u, g, kt, j)] % RING
                            ins = pe.matmul(to[32 * j:32 * j + VW, c], V1[:, b, t, h * VW:(h + 1) * VW],
                                            PT[:, b, slot, c], start=True, stop=True)
                else:
                    for j in range(HG):
                        h, slot = g * HG + j, OWN_NO[("ex", u, g, kt, j)] % RING
                        v = slice(h * VW, (h + 1) * VW)
                        if s in FULL:
                            ins = pe.matmul(to[32 * j:32 * j + VW, :], V1[:, b, kt, v], PT[:, b, slot, :],
                                            start=kt == 0, stop=kt == T - 1)
                        else:
                            ins = pe.matmul(to[32 * j:32 * j + VW, :], ctx_V[:, CTX_OF[s], b, v],
                                            PT[0:LCP, b, slot, :], start=True, stop=True)
                ins.then_inc(summed.sem, 1)

            for x in CHAIN:
                if x[0] == "ex":
                    score(x)
                elif x[0] == "pv":
                    sum_values(x)
                elif x[0] not in NO_BANK:
                    piece(x)


def _layout(i):
    f = lambda a: np.asarray(a)
    L0, L1, L2, L3 = ({k[9:]: f(v) for k, v in i.items() if k.startswith(f"L{n}_xcond_")} for n in range(4))

    def dh(a):
        return a.reshape(a.shape[:-1] + (2, H2, D)).swapaxes(-1, -2).reshape(a.shape)

    def swap(a):
        a = a.reshape(a.shape[:-1] + (H, 2, D // 2))
        return a[..., ::-1, :].reshape(a.shape[:-3] + (C,))

    def cut(a, *n):
        return [a[..., j * C:(j + 1) * C] for j in n]

    def tall(a):
        return a.reshape(NI, P, C).transpose(1, 0, 2).reshape(P, NI * C)

    q0, k0, v0 = cut(L0["W_qkv"], 0, 1, 2)
    kc0, vc0 = cut(L0["W_kvc"], 0, 1)
    q1, k1, v1 = cut(L1["w_qkv"], 0, 1, 2)
    kc1, vc1 = cut(L1["w_kv"], 0, 1)
    q2, k2, v2 = cut(L2["qkv_W"], 0, 1, 2)
    kc3, vc3 = cut(L3["Wkv"], 0, 1)
    weights = {"q0": dh(q0), "k0": dh(k0), "v0": v0, "qc0": dh(L0["W_qc"]), "kc0": dh(kc0), "vc0": vc0,
               "cp0": L0["W_cproj"], "up0": L0["W_mlp1"], "q1": dh(q1), "k1": dh(k1), "v1": v1,
               "qc1": dh(L1["w_q"]), "kc1": dh(kc1), "vc1": vc1, "up1a": L1["w_m1"][:, :HID],
               "up1b": L1["w_m1"][:, HID:], "q2": dh(q2), "k2": dh(k2), "v2": v2, "q2s": dh(swap(q2)),
               "k2s": dh(swap(k2)), "qc2": dh(L2["cq_W"]), "kc2": dh(L2["ck_W"]), "vc2": L2["cv_W"],
               "up2": L2["mlp_W1"], "qc3": dh(L3["Wq"]), "kc3": dh(kc3), "vc3": vc3, "p3": L3["Wp"]}
    w_pack = np.concatenate([weights[n] for n, _ in W_MAIN], 1)
    wc_pack = np.concatenate([weights[n] for n, _ in W_CTX], 1)
    ada = np.concatenate([L0["W_mod"], L1["w_ada"], L2["adaLN_W"], L3["Wss_q"], L3["Wss_kv"]], 1)
    raw = np.concatenate([L0["W_proj"], tall(L0["W_mlp2"]), L1["w_so"], L1["w_co"], tall(L1["w_m2"]),
                          L2["attn_out_W"], L2["co_W"], tall(L2["mlp_W2"])], 1)
    b_ada = [L0["b_mod"], L1["b_ada"], L2["adaLN_b"], np.concatenate([L3["bss_q"], L3["bss_kv"]])]
    mod_cols = [b_ada[layer][c * C:(c + 1) * C] for layer, *cs in MODS for c in cs]
    bq0, bk0, bv0 = cut(L0["b_qkv"], 0, 1, 2)
    bq1, bk1, bv1 = cut(L1["b_qkv"], 0, 1, 2)
    bkc0, bvc0 = cut(L0["b_kvc"], 0, 1)
    bkc1, bvc1 = cut(L1["b_kv"], 0, 1)
    bkc3, bvc3 = cut(L3["bkv"], 0, 1)
    blocks = lambda a: [a[j * P:(j + 1) * P] for j in range(NI)]
    columns = mod_cols + [L2["norm1_w"], L2["normc_w"], L2["norm2_w"], dh(bq0), dh(bk0), dh(bq1), dh(bk1),
                          dh(L0["b_qc"]), dh(L1["b_q"]), dh(L3["bq"]), dh(bkc0), dh(bkc1), dh(bkc3)] \
        + blocks(L0["b_mlp1"]) + blocks(L1["b_m1"][:HID]) + blocks(L1["b_m1"][HID:]) + blocks(L2["mlp_b1"]) \
        + [f(i["cond_1024"])[j] for j in range(B)]
    vrow = np.concatenate([bv0, bv1, L0["b_cproj"], L3["bp"], bvc0, bvc1, bvc3])
    row = np.concatenate([b_ada[layer][c * C:(c + 1) * C] for layer, c, _, _ in GATED]
                         + [L0["b_proj"], L0["b_mlp2"], L1["b_so"], L1["b_co"], L1["b_m2"], L2["mlp_b2"]])

    eye = np.eye(P, dtype=np.float32)
    a = np.arange(P)
    window = np.where(a[:, None] // WIN == a[None, :] // WIN, 0.0, NEG).astype(np.float32)
    freq = 1.0 / 10000.0 ** (np.arange(0, D, 2, dtype=np.float32) / D)
    angle = np.outer(np.arange(S // 2, dtype=np.float32), freq)
    emb = np.concatenate([angle, angle], -1)
    table = np.stack([np.cos(emb), np.sin(emb) * np.where(np.arange(D) < D // 2, -1.0, 1.0)]).astype(np.float32)
    table = np.broadcast_to(table.transpose(2, 0, 1)[:, None], (2, D, H2, 2, S // 2)).reshape(P, 2, S // 2)
    return {
        "x": f(i["x"]), "ctx": f(i["ctx_1024"]),
        "cmask": f(i["mask_BxS2_bf1"]).reshape(1, B * LC),
        "smask": f(i["mask_SxS_bk0"]),
        "w": w_pack, "wc": wc_pack, "ada": ada, "raw": raw, "col": np.stack(columns, 1), "vrow": vrow, "row": row,
        "ident": eye, "wmask": window,
        "rope": table,
    }


def kernel(**inputs):
    import concourse.bacc as bacc
    from concourse.bass_utils import run_bass_kernel_spmd

    nc = bacc.Bacc("TRN2", target_bir_lowering=False, num_devices=1)
    arrays, args = {}, []
    for name, a in _layout(inputs).items():
        a = np.ascontiguousarray(a)
        arrays[f"in_{name}"] = a
        args.append(nc.dram_tensor(f"in_{name}", a.shape, mybir.dt.from_np(a.dtype), kind="ExternalInput").ap())
    args.append(nc.dram_tensor("out_0", (B, S, C), F32, kind="ExternalOutput").ap())
    pixart_four_layers(nc, *args)
    r = run_bass_kernel_spmd(nc, [arrays], core_ids=[0])
    return r.results[0]["out_0"]
```
